# Optimizing a Trainium2 kernel written in Bass

```python
import numpy as np
import jax
import jax.numpy as jnp

def _softmax(x, axis=-1):
    return jax.nn.softmax(x, axis=axis)

def _gelu(x):
    return jax.nn.gelu(x, approximate=True)

def _silu(x):
    return jax.nn.silu(x)

def _sigmoid(x):
    return jax.nn.sigmoid(x)

def _layernorm(x, axis=-1, eps=1e-05):
    m = jnp.mean(x, axis=axis, keepdims=True)
    v = jnp.var(x, axis=axis, keepdims=True)
    return (x - m) / jnp.sqrt(v + eps)

def _scatter_add(tgt, idx, src, axis=0):
    return tgt.at[idx].add(src)

def _segment_sum(src, seg, n):
    return jax.ops.segment_sum(src, seg, n)
kernel_name = 'mk_perceiver_d2_seqx_r4_b472a0'

def setup_inputs(seed: int=0):
    np.random.seed(seed)
    _w = jnp.asarray

    def _rec_inputs():
        import jax
        import jax.numpy as jnp
        _rk = jax.random.key(seed)
        x = -0.0003929 + 0.9999 * jax.random.normal(jax.random.fold_in(_rk, 1), (1, 128, 256), jnp.float32)
        _lenS = 128 - jax.random.randint(jax.random.fold_in(_rk, 7), (1,), 0, max(1, 128 // 4) + 1, jnp.int32)
        _lenS2 = 12544 - jax.random.randint(jax.random.fold_in(_rk, 8), (1,), 0, max(1, 12544 // 4) + 1, jnp.int32)
        _ctx_512P = jax.random.normal(jax.random.fold_in(_rk, 11), (1, 16, 128), jnp.float32)
        _ctx_512c = jax.random.dirichlet(jax.random.fold_in(_rk, 511), 0.3 * jnp.ones((16,), jnp.float32), (1, 12544))
        _ctx_512t = jnp.einsum('bsk,bkd->bsd', _ctx_512c, _ctx_512P)
        _ctx_512t = _ctx_512t * jax.lax.rsqrt(jnp.mean(jnp.square(_ctx_512t)) + 1e-12) * 0.953939
        ctx_512 = -1.39393e-06 + 0.999914 * (_ctx_512t + 0.3 * jax.random.normal(jax.random.fold_in(_rk, 611), (1, 12544, 128), jnp.float32))
        return (x, ctx_512)
    x, ctx_512 = _rec_inputs()

    def _L0_xattn_setup():
        import jax, jax.numpy as jnp
        import numpy as np
        HEADS = 16
        D_MODEL = 256
        IMG_MODEL = 128
        D_K = D_MODEL // HEADS
        key = jax.random.key(seed)
        ks = jax.random.split(key, 12)
        B, LQ, LKV = (8, 512, 256)
        s_dm = 1.0 / np.sqrt(D_MODEL)
        s_im = 1.0 / np.sqrt(IMG_MODEL)
        return {'q': jax.random.normal(ks[0], (B, LQ, D_MODEL), jnp.float32), 'k': jax.random.normal(ks[1], (B, LKV, IMG_MODEL), jnp.float32), 'v': jax.random.normal(ks[2], (B, LKV, IMG_MODEL), jnp.float32), 'Wq': jax.random.normal(ks[3], (D_MODEL, D_MODEL), jnp.float32) * s_dm, 'bq': jnp.zeros((D_MODEL,), jnp.float32), 'Wk': jax.random.normal(ks[4], (IMG_MODEL, D_MODEL), jnp.float32) * s_im, 'bk': jnp.zeros((D_MODEL,), jnp.float32), 'Wv': jax.random.normal(ks[5], (IMG_MODEL, D_MODEL), jnp.float32) * s_im, 'bv': jnp.zeros((D_MODEL,), jnp.float32), 'Wo': jax.random.normal(ks[6], (D_MODEL, D_MODEL), jnp.float32) * s_dm, 'bo': jnp.zeros((D_MODEL,), jnp.float32)}
    _L0_xattn_all = _L0_xattn_setup()
    _L0_xattn_in = {k: v for k, v in _L0_xattn_all.items() if k in ('Wq', 'bq', 'Wk', 'bk', 'Wv', 'bv', 'Wo', 'bo')}
    del _L0_xattn_all

    def _L0_attn_setup():
        import jax, jax.numpy as jnp
        import numpy as np
        B, N, DIM, H, DH = (1, 512, 256, 16, 64)
        EPS = 0.001

        def _split_heads(t):
            b, n, _ = t.shape
            return t.reshape(b, n, H, DH).transpose(0, 2, 1, 3)
        key = jax.random.key(seed)
        ks = jax.random.split(key, 6)
        x = jax.random.normal(ks[0], (B, N, DIM), dtype=jnp.float32)
        scale = 1.0 / np.sqrt(DIM)
        Wq = jax.random.normal(ks[1], (DIM, H * DH), dtype=jnp.float32) * scale
        Wk = jax.random.normal(ks[2], (DIM, H * DH), dtype=jnp.float32) * scale
        Wv = jax.random.normal(ks[3], (DIM, H * DH), dtype=jnp.float32) * scale
        Wo = jax.random.normal(ks[4], (H * DH, DIM), dtype=jnp.float32) * (1.0 / np.sqrt(H * DH))
        bo = jax.random.normal(ks[5], (DIM,), dtype=jnp.float32) * 0.01
        return {'x': x, 'Wq': Wq, 'Wk': Wk, 'Wv': Wv, 'Wo': Wo, 'bo': bo}
    _L0_attn_all = _L0_attn_setup()
    _L0_attn_in = {k: v for k, v in _L0_attn_all.items() if k in ('Wq', 'Wk', 'Wv', 'Wo', 'bo')}
    del _L0_attn_all

    def _L0_ffn_setup():
        import jax, jax.numpy as jnp
        import numpy as np
        E = 8
        K = 2
        C = 256
        F = 512
        EPS = 1e-05
        key = jax.random.key(seed)
        ks = jax.random.split(key, 6)
        x = jax.random.normal(ks[0], (2, 256, C), dtype=jnp.float32)
        ln_gamma = 1.0 + 0.02 * jax.random.normal(ks[1], (C,), dtype=jnp.float32)
        ln_beta = 0.02 * jax.random.normal(ks[2], (C,), dtype=jnp.float32)
        gate_w = jax.random.normal(ks[3], (E, C), dtype=jnp.float32) / np.sqrt(C)
        w1 = jax.random.normal(ks[4], (E, F, C), dtype=jnp.float32) / np.sqrt(C)
        w2 = jax.random.normal(ks[5], (E, C, F), dtype=jnp.float32) / np.sqrt(F)
        return {'x': x, 'ln_gamma': ln_gamma, 'ln_beta': ln_beta, 'gate_w': gate_w, 'w1': w1, 'w2': w2}
    _L0_ffn_all = _L0_ffn_setup()
    _L0_ffn_in = {k: v for k, v in _L0_ffn_all.items() if k in ('ln_gamma', 'ln_beta', 'gate_w', 'w1', 'w2')}
    del _L0_ffn_all

    def _L1_xattn_setup():
        import jax, jax.numpy as jnp
        import numpy as np
        DIM = 256
        LATENT_DIM = 128
        NUM_HEADS = 16
        HEAD_DIM = DIM // NUM_HEADS
        SCALE = HEAD_DIM ** (-0.5)
        key = jax.random.key(seed)
        k1, k2, k3, k4, k5 = jax.random.split(key, 5)
        B, xN, zN = (2, 512, 512)
        x = jax.random.normal(k1, (B, xN, DIM), dtype=jnp.float32)
        z = jax.random.normal(k2, (B, zN, LATENT_DIM), dtype=jnp.float32)
        Wq = jax.random.normal(k3, (DIM, DIM), dtype=jnp.float32) * DIM ** (-0.5)
        Wkv = jax.random.normal(k4, (2 * DIM, LATENT_DIM), dtype=jnp.float32) * LATENT_DIM ** (-0.5)
        Wo = jax.random.normal(k5, (DIM, DIM), dtype=jnp.float32) * DIM ** (-0.5)
        return {'x': x, 'z': z, 'Wq': Wq, 'Wkv': Wkv, 'Wo': Wo}
    _L1_xattn_all = _L1_xattn_setup()
    _L1_xattn_in = {k: v for k, v in _L1_xattn_all.items() if k in ('Wq', 'Wkv', 'Wo')}
    del _L1_xattn_all

    def _L1_attn_setup():
        import math
        import jax, jax.numpy as jnp
        import numpy as np
        EMB = 256
        HEADS = 16
        HEAD_DIM = EMB // HEADS

        def _srms_norm(x, eps=1e-12):
            dtype = x.dtype
            xf = x.astype(jnp.float32)
            scale = 1.0 / math.sqrt(x.shape[-1])
            n = jnp.linalg.norm(xf * scale, axis=-1, keepdims=True)
            return (xf / jnp.maximum(n, eps)).astype(dtype)
        key = jax.random.key(seed)
        ks = jax.random.split(key, 6)
        b, l = (4, 1024)
        x = jax.random.normal(ks[0], (b, l, EMB), dtype=jnp.float32)
        std = math.sqrt(2.0 / (EMB + EMB))
        Wq = jax.random.normal(ks[1], (EMB, EMB), dtype=jnp.float32) * std
        Wk = jax.random.normal(ks[2], (EMB, EMB), dtype=jnp.float32) * std
        Wv = jax.random.normal(ks[3], (EMB, EMB), dtype=jnp.float32) * std
        Wu = jax.random.normal(ks[4], (EMB, EMB), dtype=jnp.float32) * std
        Wo = jax.random.normal(ks[5], (EMB, EMB), dtype=jnp.float32) * std
        return {'x': x, 'Wq': Wq, 'Wk': Wk, 'Wv': Wv, 'Wu': Wu, 'Wo': Wo}
    _L1_attn_all = _L1_attn_setup()
    _L1_attn_in = {k: v for k, v in _L1_attn_all.items() if k in ('Wq', 'Wk', 'Wv', 'Wu', 'Wo')}
    del _L1_attn_all

    def _L1_ffn_setup():
        import jax, jax.numpy as jnp
        import numpy as np
        DIM = 256
        MOE_HID = 128
        SHARED_HID = 512
        N_EXPERTS = 16
        TOP_K = 2
        NORM_TOPK_PROB = True
        key = jax.random.key(seed)
        ks = jax.random.split(key, 9)
        s = 0.02
        x = jax.random.normal(ks[0], (2, 256, DIM), dtype=jnp.float32)
        Wg = jax.random.normal(ks[1], (N_EXPERTS, DIM), dtype=jnp.float32) * s
        We_gate = jax.random.normal(ks[2], (N_EXPERTS, MOE_HID, DIM), dtype=jnp.float32) * s
        We_up = jax.random.normal(ks[3], (N_EXPERTS, MOE_HID, DIM), dtype=jnp.float32) * s
        We_down = jax.random.normal(ks[4], (N_EXPERTS, DIM, MOE_HID), dtype=jnp.float32) * s
        Ws_gate = jax.random.normal(ks[5], (SHARED_HID, DIM), dtype=jnp.float32) * s
        Ws_up = jax.random.normal(ks[6], (SHARED_HID, DIM), dtype=jnp.float32) * s
        Ws_down = jax.random.normal(ks[7], (DIM, SHARED_HID), dtype=jnp.float32) * s
        Wsg = jax.random.normal(ks[8], (1, DIM), dtype=jnp.float32) * s
        return {'x': x, 'Wg': Wg, 'We_gate': We_gate, 'We_up': We_up, 'We_down': We_down, 'Ws_gate': Ws_gate, 'Ws_up': Ws_up, 'Ws_down': Ws_down, 'Wsg': Wsg}
    _L1_ffn_all = _L1_ffn_setup()
    _L1_ffn_in = {k: v for k, v in _L1_ffn_all.items() if k in ('Wg', 'We_gate', 'We_up', 'We_down', 'Ws_gate', 'Ws_up', 'Ws_down', 'Wsg')}
    del _L1_ffn_all
    return {'x': x, 'ctx_512': ctx_512, 'L0_xattn_Wq': _L0_xattn_in['Wq'], 'L0_xattn_bq': _L0_xattn_in['bq'], 'L0_xattn_Wk': _L0_xattn_in['Wk'], 'L0_xattn_bk': _L0_xattn_in['bk'], 'L0_xattn_Wv': _L0_xattn_in['Wv'], 'L0_xattn_bv': _L0_xattn_in['bv'], 'L0_xattn_Wo': _L0_xattn_in['Wo'], 'L0_xattn_bo': _L0_xattn_in['bo'], 'L0_attn_Wq': _L0_attn_in['Wq'], 'L0_attn_Wk': _L0_attn_in['Wk'], 'L0_attn_Wv': _L0_attn_in['Wv'], 'L0_attn_Wo': _L0_attn_in['Wo'], 'L0_attn_bo': _L0_attn_in['bo'], 'L0_ffn_ln_gamma': _L0_ffn_in['ln_gamma'], 'L0_ffn_ln_beta': _L0_ffn_in['ln_beta'], 'L0_ffn_gate_w': _L0_ffn_in['gate_w'], 'L0_ffn_w1': _L0_ffn_in['w1'], 'L0_ffn_w2': _L0_ffn_in['w2'], 'L1_xattn_Wq': _L1_xattn_in['Wq'], 'L1_xattn_Wkv': _L1_xattn_in['Wkv'], 'L1_xattn_Wo': _L1_xattn_in['Wo'], 'L1_attn_Wq': _L1_attn_in['Wq'], 'L1_attn_Wk': _L1_attn_in['Wk'], 'L1_attn_Wv': _L1_attn_in['Wv'], 'L1_attn_Wu': _L1_attn_in['Wu'], 'L1_attn_Wo': _L1_attn_in['Wo'], 'L1_ffn_Wg': _L1_ffn_in['Wg'], 'L1_ffn_We_gate': _L1_ffn_in['We_gate'], 'L1_ffn_We_up': _L1_ffn_in['We_up'], 'L1_ffn_We_down': _L1_ffn_in['We_down'], 'L1_ffn_Ws_gate': _L1_ffn_in['Ws_gate'], 'L1_ffn_Ws_up': _L1_ffn_in['Ws_up'], 'L1_ffn_Ws_down': _L1_ffn_in['Ws_down'], 'L1_ffn_Wsg': _L1_ffn_in['Wsg']}

def reference(x, ctx_512, L0_xattn_Wq, L0_xattn_bq, L0_xattn_Wk, L0_xattn_bk, L0_xattn_Wv, L0_xattn_bv, L0_xattn_Wo, L0_xattn_bo, L0_attn_Wq, L0_attn_Wk, L0_attn_Wv, L0_attn_Wo, L0_attn_bo, L0_ffn_ln_gamma, L0_ffn_ln_beta, L0_ffn_gate_w, L0_ffn_w1, L0_ffn_w2, L1_xattn_Wq, L1_xattn_Wkv, L1_xattn_Wo, L1_attn_Wq, L1_attn_Wk, L1_attn_Wv, L1_attn_Wu, L1_attn_Wo, L1_ffn_Wg, L1_ffn_We_gate, L1_ffn_We_up, L1_ffn_We_down, L1_ffn_Ws_gate, L1_ffn_Ws_up, L1_ffn_Ws_down, L1_ffn_Wsg):
    import jax
    import jax.numpy as jnp

    def _L0_xattn_ref(q, k, v, Wq, bq, Wk, bk, Wv, bv, Wo, bo):
        import jax, jax.numpy as jnp
        import numpy as np
        HEADS = 16
        D_MODEL = 256
        IMG_MODEL = 128
        D_K = D_MODEL // HEADS
        B, LQ, _ = q.shape
        LKV = k.shape[1]
        qh = (q @ Wq + bq).reshape(B, LQ, HEADS, D_K).transpose(0, 2, 1, 3)
        kh = (k @ Wk + bk).reshape(B, LKV, HEADS, D_K).transpose(0, 2, 1, 3)
        vh = (v @ Wv + bv).reshape(B, LKV, HEADS, D_K).transpose(0, 2, 1, 3)
        scale = 1.0 / np.sqrt(D_K)
        scores = jnp.einsum('bhqd,bhkd->bhqk', qh, kh) * scale
        attn = jax.nn.softmax(scores, axis=-1)
        out = jnp.einsum('bhqk,bhkd->bhqd', attn, vh)
        concat = out.transpose(0, 2, 1, 3).reshape(B, LQ, D_MODEL)
        return concat @ Wo + bo

    def _L0_attn_ref(x, Wq, Wk, Wv, Wo, bo):
        import jax, jax.numpy as jnp
        import numpy as np
        B, N, DIM, H, DH = (1, 512, 256, 16, 64)
        EPS = 0.001

        def _split_heads(t):
            b, n, _ = t.shape
            return t.reshape(b, n, H, DH).transpose(0, 2, 1, 3)
        b, n, _ = x.shape
        q = _split_heads(x @ Wq)
        k = _split_heads(x @ Wk)
        v = _split_heads(x @ Wv)
        q = jax.nn.relu(q) + EPS
        k = jax.nn.relu(k) + EPS
        k_cumsum = jnp.cumsum(k, axis=2)
        context = jnp.cumsum(jnp.einsum('bhnd,bhne->bhnde', k, v), axis=2)
        D_inv = 1.0 / jnp.einsum('bhnd,bhnd->bhn', k_cumsum, q)
        attn = jnp.einsum('bhnd,bhnde,bhn->bhne', q, context, D_inv)
        attn = attn.transpose(0, 2, 1, 3).reshape(b, n, H * DH)
        return attn @ Wo + bo

    def _L0_ffn_ref(x, ln_gamma, ln_beta, gate_w, w1, w2):
        import jax, jax.numpy as jnp
        import numpy as np
        E = 8
        K = 2
        C = 256
        F = 512
        EPS = 1e-05
        B, T, Cc = x.shape
        xf = x.reshape(-1, Cc)
        mu = jnp.mean(xf, axis=-1, keepdims=True)
        var = jnp.var(xf, axis=-1, keepdims=True)
        rn = (xf - mu) * jax.lax.rsqrt(var + EPS) * ln_gamma + ln_beta
        logits = rn @ gate_w.T
        probs = jax.nn.softmax(logits, axis=-1)
        rw, sel = jax.lax.top_k(probs, K)
        comb = jnp.sum(jax.nn.one_hot(sel, E, dtype=xf.dtype) * rw[..., None], axis=1)
        h = jax.nn.gelu(jnp.einsum('nc,efc->enf', xf, w1), approximate=False)
        y = jnp.einsum('enf,ecf->enc', h, w2)
        out = jnp.einsum('enc,ne->nc', y, comb)
        return out.reshape(B, T, Cc)

    def _L1_xattn_ref(x, z, Wq, Wkv, Wo):
        import jax, jax.numpy as jnp
        import numpy as np
        DIM = 256
        LATENT_DIM = 128
        NUM_HEADS = 16
        HEAD_DIM = DIM // NUM_HEADS
        SCALE = HEAD_DIM ** (-0.5)
        B, xN, _ = x.shape
        _, zN, _ = z.shape
        Q = (x @ Wq.T).reshape(B, xN, NUM_HEADS, HEAD_DIM)
        KV = (z @ Wkv.T).reshape(B, zN, 2, NUM_HEADS, HEAD_DIM)
        K = KV[:, :, 0]
        V = KV[:, :, 1]
        attn = jnp.einsum('bqhd,bkhd->bhqk', Q, K) * SCALE
        attn = jax.nn.softmax(attn, axis=-1)
        O = jnp.einsum('bhqk,bkhd->bqhd', attn, V).reshape(B, xN, DIM)
        return O @ Wo.T

    def _L1_attn_ref(x, Wq, Wk, Wv, Wu, Wo):
        import math
        import jax, jax.numpy as jnp
        import numpy as np
        EMB = 256
        HEADS = 16
        HEAD_DIM = EMB // HEADS

        def _srms_norm(x, eps=1e-12):
            dtype = x.dtype
            xf = x.astype(jnp.float32)
            scale = 1.0 / math.sqrt(x.shape[-1])
            n = jnp.linalg.norm(xf * scale, axis=-1, keepdims=True)
            return (xf / jnp.maximum(n, eps)).astype(dtype)
        b, l, d = x.shape
        h, hd = (HEADS, HEAD_DIM)
        scale = math.sqrt(hd)

        def proj(W):
            return jnp.einsum('bld,ed->ble', x, W).reshape(b, l, h, hd).transpose(0, 2, 1, 3)
        q = jax.nn.relu(proj(Wq)) / scale
        k = jax.nn.relu(proj(Wk)) / scale
        v = proj(Wv)
        u = jax.nn.silu(proj(Wu))
        kv = jnp.einsum('bhlk,bhlv->bhkv', k, v)
        out = jnp.einsum('bhlk,bhkv->bhlv', q, kv)
        out = _srms_norm(out) * u
        out = out.transpose(0, 2, 1, 3).reshape(b, l, d)
        return jnp.einsum('bld,ed->ble', out, Wo)

    def _L1_ffn_ref(x, Wg, We_gate, We_up, We_down, Ws_gate, Ws_up, Ws_down, Wsg):
        import jax, jax.numpy as jnp
        import numpy as np
        DIM = 256
        MOE_HID = 128
        SHARED_HID = 512
        N_EXPERTS = 16
        TOP_K = 2
        NORM_TOPK_PROB = True
        B, S, D = x.shape
        xt = x.reshape(-1, D)
        gates = jax.nn.softmax(xt @ Wg.T, axis=-1)
        scores, inds = jax.lax.top_k(gates, TOP_K)
        if NORM_TOPK_PROB:
            scores = scores / jnp.sum(scores, axis=-1, keepdims=True)
        g = jnp.einsum('td,ehd->teh', xt, We_gate)
        u = jnp.einsum('td,ehd->teh', xt, We_up)
        h = jax.nn.silu(g) * u
        y_all = jnp.einsum('teh,edh->ted', h, We_down)
        y_sel = jnp.take_along_axis(y_all, inds[:, :, None], axis=1)
        y = jnp.sum(y_sel * scores[:, :, None], axis=1)
        shared = jax.nn.silu(xt @ Ws_gate.T) * (xt @ Ws_up.T) @ Ws_down.T
        y = y + jax.nn.sigmoid(xt @ Wsg.T) * shared
        return y.reshape(B, S, D)
    x = x + _L0_xattn_ref(_layernorm(x, axis=-1), ctx_512, ctx_512, L0_xattn_Wq, L0_xattn_bq, L0_xattn_Wk, L0_xattn_bk, L0_xattn_Wv, L0_xattn_bv, L0_xattn_Wo, L0_xattn_bo)
    x = x + _L0_attn_ref(_layernorm(x, axis=-1), L0_attn_Wq, L0_attn_Wk, L0_attn_Wv, L0_attn_Wo, L0_attn_bo)
    x = x + _L0_ffn_ref(_layernorm(x, axis=-1), L0_ffn_ln_gamma, L0_ffn_ln_beta, L0_ffn_gate_w, L0_ffn_w1, L0_ffn_w2)
    x = x + _L1_xattn_ref(_layernorm(x, axis=-1), ctx_512, L1_xattn_Wq, L1_xattn_Wkv, L1_xattn_Wo)
    x = x + _L1_attn_ref(_layernorm(x, axis=-1), L1_attn_Wq, L1_attn_Wk, L1_attn_Wv, L1_attn_Wu, L1_attn_Wo)
    x = x + _L1_ffn_ref(_layernorm(x, axis=-1), L1_ffn_Wg, L1_ffn_We_gate, L1_ffn_We_up, L1_ffn_We_down, L1_ffn_Ws_gate, L1_ffn_Ws_up, L1_ffn_Ws_down, L1_ffn_Wsg)
    return x

_drawn_inputs = setup_inputs


def setup_inputs(seed=0):
    import zlib

    import numpy as np

    out = dict(_drawn_inputs(seed))
    spreads = {'L0_xattn_bq': (0.0, 0.1),
     'L0_xattn_bk': (0.0, 0.8),
     'L0_xattn_bv': (0.0, 0.1),
     'L0_xattn_bo': (0.0, 0.1)}
    factors = {'L0_attn_bo': 4.277,
     'L0_ffn_ln_gamma': 3.47,
     'L0_ffn_ln_beta': 3.852,
     'L1_ffn_Wg': 8.0,
     'L1_ffn_We_gate': 8.0,
     'L1_ffn_We_up': 8.0,
     'L1_ffn_We_down': 8.0,
     'L1_ffn_Ws_gate': 6.875,
     'L1_ffn_Ws_up': 6.962,
     'L1_ffn_Ws_down': 6.86,
     'L1_ffn_Wsg': 8.0}
    for name, (base, spread) in spreads.items():
        noise = np.random.default_rng([zlib.crc32(name.encode()), seed]).standard_normal(out[name].shape)
        drawn = base * np.exp(spread * noise) if base else spread * noise
        out[name] = jnp.asarray(drawn.astype(out[name].dtype))
    for name, factor in factors.items():
        out[name] = (out[name] * factor).astype(out[name].dtype)
    return out
```

```python
from contextlib import ExitStack

import concourse.bass as bass
import numpy as np
from concourse import mybir

F32 = mybir.dt.float32
BF16 = mybir.dt.bfloat16
ALU = mybir.AluOpType
ACT = mybir.ActivationFunctionType
AX = mybir.AxisListType

P = 128
D = 256
DC = D // P
CD = 128
KEYS = 12544
HEADS = 16
HD = D // HEADS
VW = HD + 1
TILES = KEYS // P
CHUNK = 1792
CHUNKS = KEYS // CHUNK
CT = CHUNK // P
UNIT = 448
UNITS = KEYS // UNIT
UPC = CHUNK // UNIT
GT = 7
GROUPS = TILES // GT
GPC = CT // GT
GH = 8
VB = 4
BATCHES = -(-CT // VB)
REST_SLOTS = 2
K_AT = {0: 0, 2: 1, 4: 2, 6: 3}
V_AT = {8: 0, 9: 1, 10: 2, 11: 3}
MAX_AHEAD = 6
STACK = 6 * HD
QPART = (0, 0, 0, 1, 1, 2)
KROWS = ((0, 48), (48, 32), (80, 16))
SROWS = STACK + 3

LH, LD = 16, 64
LEPS = 1e-3
E0, F0 = 8, 512
E1, F1 = 16, 128
FS = 512
LN_EPS = 1e-5

_CONSTS = {"ident": P, "causal": P, "numsel": 2 * P - HD, "densel": 2 * P - HD, "blockdiag": P,
           "rev0": E0, "rev1": E1, "onecol": 31, "spread": LH * LD}


def _const_at(name):
    at = 0
    for n, w in _CONSTS.items():
        if n == name:
            return at, at + w
        at += w


def _constants():
    p = np.arange(P)[:, None]
    out = np.zeros((P, sum(_CONSTS.values())), np.float32)

    def put(name, a):
        lo, hi = _const_at(name)
        out[:, lo:hi] = a
    col = np.arange(P)[None, :]
    put("ident", p == col)
    put("causal", p <= col)
    j = np.arange(2 * P - HD)[None, :] - (P - HD)
    put("numsel", (p % 32 == j) & (j >= 0) & (j < HD))
    put("densel", (p % 32 == HD) & (j >= 0) & (j < HD))
    put("blockdiag", p // HD == col // HD)
    put("rev0", E0 - np.arange(E0)[None, :] + 0 * p)
    put("rev1", E1 - np.arange(E1)[None, :] + 0 * p)
    put("onecol", (np.arange(31)[None, :] == 15) & (p >= 0))
    put("spread", p == np.arange(LH * LD)[None, :] // LD)
    return out


def program(nc, a, out):
    ctx = ExitStack()
    with ctx:
        def sb(name, shape, dt=F32):
            return ctx.enter_context(nc.sbuf_tensor(name, shape, dt))

        sems = {}

        def sem(name):
            if name not in sems:
                sems[name] = ctx.enter_context(nc.semaphore(name))
            return sems[name]

        k_scratch = nc.dram_tensor("k_scratch", [2, HEADS, 3, HD, KEYS], BF16, kind="Internal").ap()
        v_scratch = nc.dram_tensor("v_scratch", [2 * HEADS, P, TILES * VW], F32, kind="Internal").ap()
        q_scratch = nc.dram_tensor("q_scratch", [2, 3, D, P], BF16, kind="Internal").ap()

        consts = sb("consts", [P, sum(_CONSTS.values())])

        def const(name):
            lo, hi = _const_at(name)
            return consts[:, lo:hi]
        ident, causal, blockdiag = const("ident"), const("causal"), const("blockdiag")
        numsel, densel, onecol, spread = const("numsel"), const("densel"), const("onecol"), const("spread")
        wk = sb("wk", [CD, 2 * D])
        wv = sb("wv", [CD, 2 * D])
        bk = sb("bk", [P, 2 * DC])
        bv = sb("bv", [P, 2 * D])
        bq = sb("bq", [P, DC])
        wq = sb("wq", [P, 2, DC, D])
        wo = sb("wo", [P, 2, DC, D])
        bias_rows = sb("bias_rows", [P, 4, D])
        gate0 = sb("gate0", [P, DC, E0])
        gate1 = sb("gate1", [P, DC, E1 + 1])
        xs = sb("xs", [P, 7, D])
        xb = sb("xb", [P, 2, D])
        xhat = sb("xhat", [P, D])
        xhatT = sb("xhatT", [P, 2, DC, P])
        rn = sb("rn", [P, D])
        small = sb("small", [P, 96])
        attnT = sb("attnT", [P, DC, P])
        rden = sb("rden", [P, DC, P])
        qf = sb("qf", [P, DC, P])
        qr = sb("qr", [P, DC, P])
        qp = sb("qp", [P, DC, 3, P], BF16)
        qstack = sb("qstack", [P, HEADS, P], BF16)
        maxima = sb("maxima", [P, 2, UNITS])
        negmax = sb("negmax", [P, 2, 1])
        negrest = sb("negrest", [P, 2, 1])
        gates = sb("gates", [P, 7, E1])
        negparts = sb("negparts", [P, 2, 3], BF16)
        unity = sb("unity", [P, 1])
        identb = sb("identb", [P, P], BF16)

        region_k = sb("region_k", [P, 2 * KEYS], BF16)
        kstack = region_k[:, :].rearrange("p (b k) -> p b k", b=2)
        as_f = region_k[:, :].bitcast(F32)
        w2 = as_f[:, 0:32 * D].rearrange("p (f c) -> p f c", f=32)
        h0T = as_f[:, 32 * D:32 * D + 32 * P].rearrange("p (f n) -> p f n", f=32)
        region_w = sb("region_w", [P, 16384])
        lin_w = region_w[:, 0:DC * 3072].rearrange("p (k n) -> p k n", k=DC)
        lin_wo = region_w[:, 6144:8192].rearrange("p (f c) -> p f c", f=8)
        w1 = region_w[:, 8192:16384].rearrange("p (k n) -> p k n", k=DC)
        we_in = region_w[:, 0:DC * 2 * 20 * P].rearrange("p (k s f) -> p k s f", k=DC, s=2)
        we_out = region_w[:, 10240:10240 + 20 * D].rearrange("p (e c) -> p e c", e=20)
        o_heads = sb("o_heads", [P, HEADS, P])
        PARTS = CHUNK * 3 // 2
        VRING = GH * CT * VW
        w_at, k_at = 8192, KEYS // 2
        ctx_buf = [region_w[:, w_at:w_at + CHUNK], as_f[:, k_at:k_at + CHUNK]]
        k_parts = [r.bitcast(BF16).rearrange("p (s k) -> p s k", s=3) for r in (
            region_w[:, w_at + CHUNK:w_at + CHUNK + PARTS], as_f[:, k_at + CHUNK:k_at + CHUNK + PARTS])]
        v_ring = [r.rearrange("p (h t c) -> p h t c", h=GH, t=CT) for r in (
            region_w[:, w_at + CHUNK + PARTS:w_at + CHUNK + PARTS + VRING],
            o_heads[:, :, :].rearrange("p a b -> p (a b)")[:, 0:VRING])]
        rest_at = w_at + CHUNK + PARTS + VRING
        k_rest = region_w[:, rest_at:rest_at + REST_SLOTS * UNIT].rearrange("p (b k) -> p b k", b=REST_SLOTS)

        vbuf = sb("vbuf", [P, 2, TILES * VW + 32 - VW])
        probs = sb("probs", [P, 2, GT * P])
        linq = sb("linq", [P, 8, P])
        link = sb("link", [P, 8, P])
        linv = o_heads[:, 0:8, :].rearrange("p a b -> p (a b)")
        lin_oT = o_heads[:, 8:16, :]
        lin_aT = vbuf[:, :, :].rearrange("p a b -> p (a b)")[:, 0:LH * P].rearrange("p (h n) -> p h n", h=LH)
        lin_rd = probs[0:LH, 0, 0:P]
        w_kvu = sb("w_kvu", [P, DC, 3 * D])
        w_q2 = region_w[:, 15360:15872].rearrange("p (k n) -> p k n", k=DC)
        w_o2 = region_w[:, 15872:16384].rearrange("p (k n) -> p k n", k=DC)
        q2T = linq[:, 0:2, :]
        kvu = o_heads[:, 0:6, :].rearrange("p a b -> p (a b)")
        kvm = linq[:, 2:4, :]
        o2 = linq[:, 4:6, :].rearrange("p a b -> p (a b)")
        o2sq = linq[:, 6:8, :].rearrange("p a b -> p (a b)")
        o2T = link[:, 0:2, :]
        h1T = vbuf[:, :, :].rearrange("p a b -> p (a b)")[:, 0:20 * P].rearrange("p (e n) -> p e n", e=20)
        acc = link[:, 0:8, :].rearrange("p a b -> p (a b)").rearrange("p (s c) -> p s c", s=4)
        silu_g = probs[:, :, 0:4 * P]

        psum = ctx.enter_context(nc.psum_tensor("psum", [P, 8, 512], F32))
        bank = [psum[:, b, :] for b in range(8)]
        s_slots = [psum[:, 0:2, :].rearrange("p a b -> p (a b)"), psum[:, 2:4, :].rearrange("p a b -> p (a b)")]
        o_bank = bank[4]
        x_bank = bank[5]
        a_banks = [bank[6], bank[7]]

        block = ctx.enter_context(nc.Block())

        KREST_AHEAD, VBATCH_AHEAD = UPC, BATCHES
        SPLIT_AHEAD = REST_SLOTS
        STORED_K, STORED_V = 16 * GH, 16

        def prep_use(p, c):
            return (CHUNKS + 1) // 2 + (p - 1) * CHUNKS + c

        def halves(eng, layer, pair):
            for half in range(2):
                p = (2 * layer + half + 1) % 4
                some = lambda c: c if p else None
                first = half * (GH // 2)
                with eng.Fori(first, first + GH // 2 - 1) as i:
                    pair(i, False, p, (some(2 * (i - first)), some(2 * (i - first) + 1)))
                pair(first + GH // 2 - 1, half == 1, p, (some(CHUNKS - 1), None))

        def batch_tiles(m):
            return range(VB * m, min(VB * m + VB, CT))

        def once(eng, name, *pairs):
            for dst, src in pairs:
                eng.dma_start(dst, src).then_inc(sem(name), 16)
            return 16 * len(pairs)
        on_all = lambda v: v.rearrange("(a n) -> a n", a=1).broadcast_to([P, v.shape[0]])

        def vcols(buf, t):
            return vbuf[:, buf, t * VW:t * VW + 32]

        @block.sync
        def _(sp):
            once(sp, "x_loaded", (xs[:, 0, :], a["x"]))
            once(sp, "consts_loaded", (consts[:, :], a["consts"]))
            once(sp, "q_weights_loaded", (wq[:, 0], a["wq0"].rearrange("(k p) n -> p k n", p=P)),
                 (bq[:, :], a["bq"]))
            once(sp, "kv_weights_loaded", (wk[:, :], a["wk"]), (wv[:, :], a["wv"]),
                 (bk[:, 0:DC], a["bk"]), (bv[:, 0:D], on_all(a["bv"])))

            def load_ctx(c, buf, half):
                at = half * (CHUNK // 2)
                sp.dma_start(ctx_buf[buf][:, at:at + CHUNK // 2],
                             a["ctxT"][:, bass.ds(c * CHUNK + at, CHUNK // 2)])\
                    .then_inc(sem(f"ctx_loaded{buf}_{half}"), 16)

            def store_k(p, c, g, buf):
                sp.wait_ge(sem("k_unit_split"), SPLIT_AHEAD + UPC * (g + 1))
                for h in range(GH):
                    sp.dma_start(k_scratch[p // 2, GH * (p % 2) + h, :, :, bass.ds(c * CHUNK, CHUNK)]
                                 .rearrange("s d k -> d s k"), k_parts[buf][h * HD:(h + 1) * HD])\
                        .then_inc(sem(f"k_stored{buf}"), 16)

            def store_v(p, c, g, buf):
                sp.wait_ge(sem("v_batch_done"), VBATCH_AHEAD + BATCHES * (g + 1))
                sp.dma_start(v_scratch[GH * p:GH * (p + 1), :, bass.ds(c * CT * VW, CT * VW)]
                             .rearrange("h p n -> p h n"),
                             v_ring[buf].rearrange("p h t c -> p h (t c)")).then_inc(sem(f"v_stored{buf}"), 16)

            for buf in range(2):
                for half in range(2):
                    load_ctx(buf, buf, half)
            def stack_q(layer):
                sp.wait_ge(sem("q_split"), layer + 1)
                for g in range(DC):
                    sp.dma_start(q_scratch[layer, :, g * P:(g + 1) * P, :].rearrange("s r n -> r s n"), qp[:, g])\
                        .then_inc(sem("q_stored"), 16)
                sp.wait_ge(sem("q_stored"), 16 * DC * (layer + 1))
                for b, s in enumerate(QPART):
                    sp.dma_start(qstack[b * HD:(b + 1) * HD, :, :],
                                 q_scratch[layer, s].rearrange("(h d) n -> d h n", d=HD))\
                        .then_inc(sem("q_stacked"), 16)
            stack_q(0)
            once(sp, "mid_weights_loaded",
                 (wq[:, 1], a["wq1"].rearrange("(k p) n -> p k n", p=P)),
                 (wo[:, 0], a["wo0"].rearrange("(k p) n -> p k n", p=P)),
                 (wo[:, 1], a["wo1"].rearrange("(k p) n -> p k n", p=P)),
                 (bias_rows[:, 0, :], on_all(a["bo0"])), (bias_rows[:, 1, :], on_all(a["lin_bo"])),
                 (bias_rows[:, 2, :], on_all(a["gamma"])), (bias_rows[:, 3, :], on_all(a["beta"])),
                 (gate0[:, :, :], a["gate0"].rearrange("(k p) n -> p k n", p=P)),
                 (gate1[:, :, :], a["gate1"].rearrange("(k p) n -> p k n", p=P)),
                 (w_kvu[:, :, :], a["w_kvu"].rearrange("(k p) n -> p k n", p=P)))

            def after_chunk(c, buf, more):
                store_k(0, c, c, buf)
                store_v(0, c, c, buf)
                if more:
                    sp.wait_ge(sem("v_in_psum"), BATCHES * (c + 1))
                    for half in range(2):
                        load_ctx(c + 2, buf, half)

            with sp.Fori(0, CHUNKS // 2 - 1) as i:
                after_chunk(2 * i, 0, True)
                after_chunk(2 * i + 1, 1, True)
            after_chunk(CHUNKS - 3, 0, True)
            after_chunk(CHUNKS - 2, 1, False)
            after_chunk(CHUNKS - 1, 0, False)

            for buf, uses in ((0, (CHUNKS + 1) // 2), (1, CHUNKS // 2)):
                sp.wait_ge(sem(f"k_stored{buf}"), STORED_K * (uses + 1))
                sp.wait_ge(sem(f"v_stored{buf}"), STORED_V * (uses + 1))

            def load_k(layer, h, buf, c):
                cols = slice(c * CHUNK, (c + 1) * CHUNK)
                for row, rows in KROWS:
                    sp.dma_start(kstack[row:row + rows, buf, cols],
                                 k_scratch[layer, bass.ds(h, 1)].rearrange("a s d k -> (a s d) k")[0:rows, cols])\
                        .then_inc(sem(f"k_loaded{buf}_{c}"), 16)

            def load_v(layer, h, buf):
                sp.dma_start(vbuf[:, buf, 0:TILES * VW],
                             v_scratch[bass.ds(layer * HEADS + h, 1)].rearrange("a p n -> p (a n)"))\
                    .then_inc(sem(f"v_loaded{buf}"), 16)

            def attention_loads(layer):
                base = layer * HEADS
                for h in range(2):
                    sp.dma_start(kstack[STACK:SROWS, h, :], a["ones"]).then_inc(sem("ones_loaded"), 16)
                for h in range(2):
                    for c in range(CHUNKS):
                        load_k(layer, h, h, c)
                    if h == 0 and layer == 1:
                        stack_q(1)
                    load_v(layer, h, h)

                def head(h, par, more, p, c, new_piece):
                    g = CHUNKS * (p or 0) + c if p else None
                    for cc in range(CHUNKS):
                        if more:
                            sp.wait_ge(sem("scores_done"), (base + h) * GROUPS + GPC * (cc + 1))
                            if new_piece:
                                sp.wait_ge(sem("k_stored0"), STORED_K * (prep_use(new_piece, cc) + 2))
                            load_k(layer, h + 2, par, cc)
                        if p and cc == 3:
                            store_k(p, c, g, 0)
                            if not (isinstance(c, int) and c == CHUNKS - 1):
                                sp.wait_ge(sem("v_in_psum"), BATCHES * g + 2)
                                load_ctx(c + 1, 0, 0)
                        if p and cc == 5:
                            if not (isinstance(c, int) and c == CHUNKS - 1):
                                sp.wait_ge(sem("v_in_psum"), BATCHES * (g + 1))
                                load_ctx(c + 1, 0, 1)
                            store_v(p, c, g, 0)
                    if more:
                        sp.wait_ge(sem("head_done"), base + h + 1)
                        if new_piece:
                            sp.wait_ge(sem("v_stored0"), STORED_V * (prep_use(new_piece, CHUNKS) + 1))
                        load_v(layer, h + 2, par)

                for half in range(2):
                    p = (2 * layer + half + 1) % 4
                    if p:
                        sp.wait_ge(sem("v_in_psum"), BATCHES * CHUNKS * p)
                        load_ctx(0, 0, 0)
                        load_ctx(0, 0, 1)
                    first = half * (GH // 2)
                    with sp.Fori(first, first + GH // 2 - 1) as i:
                        head(2 * i, 0, True, p, 2 * (i - first), None)
                        head(2 * i + 1, 1, True, p, 2 * (i - first) + 1, None)
                    i = first + GH // 2 - 1
                    new_piece = p if half == 0 else None
                    head(2 * i, 0, half == 0, p, CHUNKS - 1, new_piece)
                    if half == 1:
                        if layer == 0:
                            sp.wait_ge(sem("k_stored0"), STORED_K * (prep_use(2, CHUNKS) + 1))
                            sp.wait_ge(sem("v_stored0"), STORED_V * (prep_use(2, CHUNKS) + 1))
                            once(sp, "w1_loaded", (w1[:, :, :], a["w1"].rearrange("(k p) n -> p k n", p=P)))
                    head(2 * i + 1, 1, half == 0, None, 0, new_piece)
                    if layer == 1 and half == 0:
                        once(sp, "lin2_weights_loaded",
                             (w_q2, a["w_q2"].rearrange("(k p) n -> p k n", p=P)),
                             (w_o2, a["w_o2"].rearrange("(k p) n -> p k n", p=P)))
                        for s in range(2):
                            once(sp, "experts_loaded",
                                 (we_in[:, :, s, :], a["we_in"][:, s].rearrange("(k p) f -> p k f", p=P)))
                        once(sp, "experts_loaded",
                             (we_out[:, :, :], a["we_out"].rearrange("(e p) c -> p e c", p=P)))

            once(sp, "lin_weights_loaded",
                 (lin_w[:, :, :], a["lin_w"].rearrange("(k p) n -> p k n", p=P)),
                 (lin_wo[:, :, :], a["lin_wo"].rearrange("(f p) c -> p f c", p=P)))
            attention_loads(0)
            sp.wait_ge(sem("head_done"), HEADS)
            once(sp, "w2_loaded", (w2[:, :, :], a["w2"].rearrange("(f p) c -> p f c", p=P)))
            sp.wait_ge(sem("expert_in_psum"), E0)
            attention_loads(1)
            sp.wait_ge(sem("out_ready"), 1)
            sp.dma_start(out, xs[:, 6, :]).then_inc(sem("out_stored"), 16)
            sp.wait_ge(sem("out_stored"), 16)

        @block.tensor
        def _(pe):
            mm, tr = pe.matmul, pe.transpose

            def transpose_xhat(k, src, slot, b):
                for c in range(DC):
                    ins = tr(bank[b][:, c * P:(c + 1) * P], src[:, c * P:(c + 1) * P], ident)
                ins.then_inc(sem("xhatT_in_psum"), 1)

            def project_q(layer, par, b):
                for g in range(DC):
                    for c in range(DC):
                        ins = mm(bank[b][:, g * P:(g + 1) * P], wq[:, layer, c, g * P:(g + 1) * P],
                                 xhatT[:, par, c, :], start=(c == 0), stop=(c == DC - 1))
                ins.then_inc(sem("q_in_psum"), 1)

            pe.wait_ge(sem("consts_loaded"), 16)
            pe.wait_ge(sem("xhat_ready"), 1)
            transpose_xhat(0, xhat, 0, 0)
            pe.wait_ge(sem("q_weights_loaded"), 32)
            pe.wait_ge(sem("xhatT_ready"), 1)
            project_q(0, 0, 1)

            pe.wait_ge(sem("kv_weights_loaded"), 64)

            def k_unit(p, c_g, buf, n, b):
                mm(b[:, 0:UNIT], wk[:, p * P:(p + 1) * P], ctx_buf[buf][:, n * UNIT:(n + 1) * UNIT],
                   start=True, stop=True).then_inc(sem("k_in_psum"), 1)

            def v_batch(p, buf, m, b):
                for k, t in enumerate(batch_tiles(m)):
                    ins = mm(b[:, k * P:(k + 1) * P], ctx_buf[buf][:, t * P:(t + 1) * P], wv[:, p * P:(p + 1) * P],
                             start=True, stop=True)
                ins.then_inc(sem("v_in_psum"), 1)

            def first_prep(c, use, buf):
                for n in range(UPC):
                    if n % 2 == 0:
                        pe.wait_ge(sem(f"ctx_loaded{buf}_{n // 2}"), 16 * (use + 1))
                    pe.wait_ge(sem("k_rest_done"), UPC * c + n + 1)
                    k_unit(0, c, buf, n, bank[n])
                for m in range(BATCHES):
                    pe.wait_ge(sem("v_batch_done"), BATCHES * c + m + 1)
                    v_batch(0, buf, m, bank[4 + m])

            with pe.Fori(0, CHUNKS // 2) as i:
                first_prep(2 * i, i, 0)
                first_prep(2 * i + 1, i, 1)
            first_prep(CHUNKS - 1, CHUNKS // 2, 0)

            def attention(layer):
                base = layer * HEADS

                def max_unit(h, par, a_, loads=None):
                    n = (base + h) * UNITS + a_
                    if a_ % UPC == 0:
                        pe.wait_ge(sem(f"k_loaded{par}_{a_ // UPC}"), 48 * (layer * (HEADS // 2) + loads + 1))
                    if not (isinstance(n, int) and n < 2):
                        pe.wait_ge(sem("unit_reduced"), n - 1)
                    mm(a_banks[a_ % 2][:, 0:UNIT], qstack[0:STACK, bass.ds(h, 1), :],
                       kstack[0:STACK, par, a_ * UNIT:(a_ + 1) * UNIT], start=True, stop=True)\
                        .then_inc(sem("unit_in_psum"), 1)

                def max_row(h, par):
                    pe.wait_ge(sem("negmax_split"), base + h + 1)
                    tr(x_bank[96:99, 0:P // 2].bitcast(BF16), negparts[:, par, :], identb[:, :])\
                        .then_inc(sem("negmax_in_psum"), 1)

                def prep_beside(p, c, j):
                    g = CHUNKS * p + c
                    if j in K_AT:
                        n = K_AT[j]
                        if n % 2 == 0:
                            pe.wait_ge(sem(f"ctx_loaded0_{n // 2}"), 16 * (prep_use(p, c) + 1))
                        if n == 0:
                            pe.wait_ge(sem("v_batch_done"), VBATCH_AHEAD + BATCHES * g)
                        else:
                            pe.wait_ge(sem("k_rest_done"), KREST_AHEAD + UPC * g + n)
                        k_unit(p, c, 0, n, x_bank)
                    if j in V_AT:
                        m = V_AT[j]
                        if m == 0:
                            pe.wait_ge(sem("k_rest_done"), KREST_AHEAD + UPC * (g + 1))
                        else:
                            pe.wait_ge(sem("v_batch_done"), VBATCH_AHEAD + BATCHES * g + m)
                        v_batch(p, 0, m, x_bank)

                def scores(h, par, j):
                    if j == 0:
                        pe.wait_ge(sem("qstack_max_ready"), base + h + 1)
                    for t in range(GT):
                        key = (j * GT + t) * P
                        ins = mm(s_slots[j % 2][:, t * P:(t + 1) * P], kstack[0:SROWS, par, key:key + P],
                                 qstack[0:SROWS, bass.ds(h, 1), :], start=True, stop=True)
                    ins.then_inc(sem("scores_done"), 1)

                def values(h, par, j, loads):
                    pe.wait_ge(sem("exp_done"), (base + h) * GROUPS + j + 1)
                    if j == 0:
                        pe.wait_ge(sem("o_copied"), base + h + 1)
                        pe.wait_ge(sem(f"v_loaded{par}"), 16 * (layer * (HEADS // 2) + loads + 1))
                        pe.wait_ge(sem("vbuf_padded"), layer + 1)
                    for t in range(GT):
                        tile, g = j * GT + t, (j * GT + t) % 4
                        ins = mm(o_bank[32 * g:32 * g + 32, 0:P], vcols(par, tile),
                                 probs[:, j % 2, t * P:(t + 1) * P], start=(tile < 4), stop=(tile >= TILES - 4))
                    if j == GROUPS - 1:
                        ins.then_inc(sem("head_done"), 1)

                pe.wait_ge(sem("q_stacked"), 96 * (layer + 1))
                if layer == 0:
                    pe.wait_ge(sem("k_rest_done"), KREST_AHEAD + UPC * CHUNKS)
                    pe.wait_ge(sem("v_batch_done"), VBATCH_AHEAD + BATCHES * CHUNKS)
                else:
                    pe.wait_ge(sem("expert_mixed"), E0)
                for a_ in range(UNITS):
                    max_unit(0, 0, a_, 0)
                for a_ in range(MAX_AHEAD):
                    max_unit(1, 1, a_, 0)
                max_row(0, 0)
                pe.wait_ge(sem("ones_loaded"), 32 * (layer + 1))
                scores(0, 0, 0)

                def pair(i, last, p, chunks):
                    for par in range(2):
                        h = 2 * i + par
                        end = last and par == 1
                        for j in range(GROUPS):
                            if j == GROUPS - 2 and not end:
                                if chunks[par] is not None:
                                    pe.wait_ge(sem("v_batch_done"),
                                               VBATCH_AHEAD + BATCHES * (CHUNKS * p + chunks[par] + 1))
                                max_row(h + 1, 1 - par)
                            if j < GROUPS - 1:
                                scores(h, par, j + 1)
                            elif not end:
                                scores(h + 1, 1 - par, 0)
                            for q in (2 * j, 2 * j + 1):
                                a_ = q + MAX_AHEAD
                                if q % 2:
                                    if chunks[par] is not None:
                                        prep_beside(p, chunks[par], j)
                                    values(h, par, j, i)
                                if a_ < UNITS and not end:
                                    max_unit(h + 1, 1 - par, a_, i + par)
                                elif a_ >= UNITS and not last:
                                    max_unit(h + 2, par, a_ - UNITS, i + 1)

                halves(pe, layer, pair)

                for g in range(DC):
                    for hh in range(8):
                        h = 8 * g + hh
                        pe.wait_ge(sem("o_copied"), 1 + base + h + 1)
                        lo = P - HD - HD * hh
                        mm(bank[g][:, 0:P], numsel[:, lo:lo + P], o_heads[:, h, :], start=(hh == 0), stop=(hh == 7))
                    for hh in range(8):
                        lo = P - HD - HD * hh
                        ins = mm(bank[2 + g][:, 0:P], densel[:, lo:lo + P], o_heads[:, 8 * g + hh, :],
                                 start=(hh == 0), stop=(hh == 7))
                    ins.then_inc(sem("o_gathered"), 1)
                pe.wait_ge(sem("attnT_ready"), layer + 1)
                pe.wait_ge(sem("mid_weights_loaded"), 16 * 10)
                for g in range(DC):
                    ins = mm(bank[6][:, 0:D], attnT[:, g, :], wo[:, layer, g, :], start=(g == 0), stop=(g == DC - 1))
                ins.then_inc(sem("block_out"), 1)

            def normed(k, b):
                pe.wait_ge(sem("xhat_ready"), k + 1 if k < 3 else k)
                transpose_xhat(k, xhat, 0, b)

            pe.wait_ge(sem("identb_ready"), 1)
            attention(0)

            normed(1, 0)
            pe.wait_ge(sem("lin_weights_loaded"), 32)
            pe.wait_ge(sem("xhatT_ready"), 2)
            for m in range(2):
                for f in range(8):
                    for c in range(DC):
                        ins = mm(bank[1 + 2 * m + f // 4][:, (f % 4) * P:(f % 4 + 1) * P],
                                 lin_w[:, c, 1024 * m + f * P:1024 * m + (f + 1) * P], xhatT[:, 1, c, :],
                                 start=(c == 0), stop=(c == DC - 1))
                    if f % 4 == 3:
                        ins.then_inc(sem("lin_qk_in_psum"), 1)
            for f in range(2):
                for c in range(DC):
                    ins = mm(bank[5 + f], xhatT[:, 1, c, :], lin_w[:, c, 2048 + 512 * f:2048 + 512 * (f + 1)],
                             start=(c == 0), stop=(c == DC - 1))
                ins.then_inc(sem("lin_v_in_psum"), 1)
            pe.wait_ge(sem("lin_qk_ready"), 4)
            for h in range(LH):
                r, f = 64 * (h % 2), h // 2
                b = 1 + 2 * (h % 2) + f // 4
                ins = mm(bank[b][:, (f % 4) * P:(f % 4 + 1) * P], link[r:r + 64, f, :], linq[r:r + 64, f, :],
                         start=True, stop=True)
                if h in (LH // 2 - 1, LH - 1):
                    ins.then_inc(sem("lin_scores_in_psum"), 1)
            pe.wait_ge(sem("lin_aT_ready"), 4)
            for h in range(LH):
                ins = mm(bank[0][0:LH, 0:P], onecol[:, 15 - h:31 - h], lin_aT[:, h, :],
                         start=(h == 0), stop=(h == LH - 1))
            ins.then_inc(sem("lin_sums_in_psum"), 1)
            pe.wait_ge(sem("lin_v_ready"), 2)
            for h in range(LH):
                r, f = 64 * (h % 2), h // 2
                ins = mm(bank[5 + f // 4][r:r + 64, (f % 4) * P:(f % 4 + 1) * P],
                         linv[:, h * LD:(h + 1) * LD], lin_aT[:, h, :], start=True, stop=True)
            ins.then_inc(sem("lin_av_in_psum"), 1)
            pe.wait_ge(sem("lin_rsum_ready"), 1)
            for f in range(8):
                ins = mm(bank[1 + f // 4][:, (f % 4) * P:(f % 4 + 1) * P], spread[0:LH, f * P:(f + 1) * P],
                         lin_rd, start=True, stop=True)
            ins.then_inc(sem("lin_rsum_spread"), 1)
            pe.wait_ge(sem("lin_oT_ready"), 2)
            for f in range(8):
                ins = mm(bank[7][:, 0:D], lin_oT[:, f, :], lin_wo[:, f, :], start=(f == 0), stop=(f == 7))
            ins.then_inc(sem("block_out"), 1)

            normed(2, 0)
            pe.wait_ge(sem("xhatT_ready"), 3)
            pe.wait_ge(sem("w1_loaded"), 16)

            def expert_in0(e):
                b = 1 + e % 2
                if e >= 2:
                    pe.wait_ge(sem("h0_ready"), e - 1)
                for f in range(4):
                    for c in range(DC):
                        at = e * F0 + f * P
                        ins = mm(bank[b][:, f * P:(f + 1) * P], w1[:, c, at:at + P], xhatT[:, 0, c, :],
                                 start=(c == 0), stop=(c == DC - 1))
                ins.then_inc(sem("h0_in_psum"), 1)

            def gate_logits(w, n, b, par):
                for c in range(DC):
                    ins = mm(bank[b][:, 0:n], xhatT[:, par, c, :], w[:, c, :], start=(c == 0), stop=(c == DC - 1))
                ins.then_inc(sem("logits_in_psum"), 1)

            expert_in0(0)
            expert_in0(1)
            pe.wait_ge(sem("rn_ready"), 1)
            transpose_xhat(3, rn, 0, 3)
            pe.wait_ge(sem("xhatT_ready"), 4)
            gate_logits(gate0, E0, 0, 1)
            pe.wait_ge(sem("w2_loaded"), 16)
            for e in range(E0):
                if e >= 1 and e + 1 < E0:
                    expert_in0(e + 1)
                b = 4 + e % 4
                if e >= 4:
                    pe.wait_ge(sem("expert_mixed"), e - 3)
                pe.wait_ge(sem("h0_ready"), e + 1)
                for f in range(4):
                    ins = mm(bank[b][:, 0:D], h0T[:, 4 * e + f, :], w2[:, 4 * e + f, :], start=(f == 0), stop=(f == 3))
                ins.then_inc(sem("expert_in_psum"), 1)

            normed(4, 0)
            pe.wait_ge(sem("xhatT_ready"), 5)
            project_q(1, 0, 1)
            attention(1)

            normed(5, 0)
            pe.wait_ge(sem("lin2_weights_loaded"), 32)
            pe.wait_ge(sem("xhatT_ready"), 6)
            for g in range(DC):
                for c in range(DC):
                    ins = mm(bank[1][:, g * P:(g + 1) * P], w_q2[:, c, g * P:(g + 1) * P], xhatT[:, 1, c, :],
                             start=(c == 0), stop=(c == DC - 1))
            ins.then_inc(sem("q2_in_psum"), 1)
            for s, (b, lo, n) in enumerate(((2, 0, 512), (3, 512, 256))):
                for c in range(DC):
                    ins = mm(bank[b][:, 0:n], xhatT[:, 1, c, :], w_kvu[:, c, lo:lo + n],
                             start=(c == 0), stop=(c == DC - 1))
                ins.then_inc(sem("kvu_in_psum"), 1)
            pe.wait_ge(sem("kv2_ready"), 2)
            for g in range(DC):
                ins = mm(bank[4 + g][:, 0:P], kvu[:, g * P:(g + 1) * P], kvu[:, D + g * P:D + (g + 1) * P],
                         start=True, stop=True)
            ins.then_inc(sem("kv_outer_in_psum"), 1)
            pe.wait_ge(sem("q2_ready"), 1)
            pe.wait_ge(sem("kvm_ready"), 2)
            for g in range(DC):
                ins = mm(bank[7][:, g * P:(g + 1) * P], q2T[:, g, :], kvm[:, g, :], start=True, stop=True)
            ins.then_inc(sem("o2_in_psum"), 1)
            pe.wait_ge(sem("o2_ready"), 1)
            for c in range(DC):
                ins = tr(bank[0][:, c * P:(c + 1) * P], o2[:, c * P:(c + 1) * P], ident)
            ins.then_inc(sem("o2T_in_psum"), 1)
            pe.wait_ge(sem("o2T_ready"), 1)
            for c in range(DC):
                ins = mm(bank[6][:, 0:D], o2T[:, c, :], w_o2[:, c, :], start=(c == 0), stop=(c == DC - 1))
            ins.then_inc(sem("block_out"), 1)

            normed(6, 0)
            pe.wait_ge(sem("xhatT_ready"), 7)
            gate_logits(gate1, E1 + 1, 7, 0)
            pe.wait_ge(sem("experts_loaded"), 48)

            def experts_in(r):
                if r >= 2:
                    pe.wait_ge(sem("h1_ready"), r - 1)
                for s in range(2):
                    for f in range(4):
                        for c in range(DC):
                            at = (4 * r + f) * P
                            ins = mm(bank[1 + 2 * (r % 2) + s][:, f * P:(f + 1) * P], we_in[:, c, s, at:at + P],
                                     xhatT[:, 0, c, :], start=(c == 0), stop=(c == DC - 1))
                    ins.then_inc(sem("gate_in_psum" if s == 0 else "up_in_psum"), 1)

            def experts_out(r):
                pe.wait_ge(sem("h1_ready"), r + 1)
                for e in range(4 * r, 4 * r + 4):
                    b = (0, 5, 6)[e % 3]
                    if e < 16:
                        if e >= 3:
                            pe.wait_ge(sem("expert_mixed"), E0 + e - 2)
                        mm(bank[b][:, 0:D], h1T[:, e, :], we_out[:, e, :], start=True, stop=True)\
                            .then_inc(sem("expert_in_psum"), 1)
                    else:
                        if e == 16:
                            pe.wait_ge(sem("sigmoid_ready"), 1)
                        ins = mm(bank[7][:, 0:D], h1T[:, e, :], we_out[:, e, :], start=(e == 16), stop=(e == 19))
                if r == 4:
                    ins.then_inc(sem("shared_in_psum"), 1)
            experts_in(0)
            experts_in(1)
            for r in range(5):
                experts_out(r)
                if r + 2 < 5:
                    experts_in(r + 2)

        @block.scalar
        def _(act):
            def std(k):
                act.wait_ge(sem("var_ready"), k + 1)
                act.activation(small[:, 10:11], small[:, 8:9], ACT.Sqrt).then_inc(sem("std_ready"), 1)

            std(0)
            act.wait_ge(sem("bk_zeroed"), 1)
            act.wait_ge(sem("kv_weights_loaded"), 64)

            for buf in range(2):
                act.sem_inc(sem(f"k_stored{buf}"), STORED_K)

            def first_part(p, g, use, buf, n, b):
                if n == 0:
                    act.wait_ge(sem(f"k_stored{buf}"), STORED_K * (use + 1))
                act.wait_ge(sem("k_in_psum"), UPC * g + n + 1)
                act.activation(k_parts[buf][:, 0, n * UNIT:(n + 1) * UNIT], b[:, 0:UNIT],
                               ACT.Identity, bias=bk[:, p:p + 1]).then_inc(sem("k1_done"), 1)

            def first_prep(c, use, buf):
                for n in range(UPC):
                    first_part(0, c, use, buf, n, bank[n])

            with act.Fori(0, CHUNKS // 2) as i:
                first_prep(2 * i, i, 0)
                first_prep(2 * i + 1, i, 1)
            first_prep(CHUNKS - 1, CHUNKS // 2, 0)

            def attention(layer):
                base = layer * HEADS

                def exp_group(h, j):
                    act.wait_ge(sem("scores_done"), (base + h) * GROUPS + j + 1)
                    act.activation(probs[:, j % 2, :], s_slots[j % 2][:, 0:GT * P], ACT.Exp)\
                        .then_inc(sem("exp_done"), 1)

                def put_max(h, par):
                    act.wait_ge(sem("negmax_in_psum"), base + h + 1)
                    act.activation(qstack[96:99, bass.ds(h, 1), :],
                                   x_bank[96:99, 0:P // 2].bitcast(BF16), ACT.Copy)\
                        .then_inc(sem("qstack_max_ready"), 1)

                def copy_out(h, par):
                    act.wait_ge(sem("head_done"), base + h + 1)
                    ins = act.activation(o_heads[:, bass.ds(h, 1), :], o_bank[:, 0:P], ACT.Copy)
                    ins.then_inc(sem("o_copied"), 1)

                if layer == 0:
                    act.sem_inc(sem("o_copied"), 1)
                act.wait_ge(sem("q_stacked"), 96 * (layer + 1))
                put_max(0, 0)

                def pair(i, last, p, chunks):
                    for par in range(2):
                        h = 2 * i + par
                        for j in range(1, GROUPS):
                            exp_group(h, j)
                            if j - 1 in K_AT and chunks[par] is not None:
                                c = chunks[par]
                                first_part(p, CHUNKS * p + c, prep_use(p, c), 0, K_AT[j - 1], x_bank)
                            if j == GROUPS - 2 and not (last and par == 1):
                                put_max(h + 1, 1 - par)
                        if not (last and par == 1):
                            exp_group(h + 1, 0)
                        copy_out(h, par)

                exp_group(0, 0)
                halves(act, layer, pair)

            attention(0)

            std(1)
            for f in range(2):
                act.wait_ge(sem("lin_v_in_psum"), f + 1)
                act.activation(linv[:, 512 * f:512 * (f + 1)], bank[5 + f], ACT.Copy).then_inc(sem("lin_v_ready"), 1)
            for f in range(2):
                act.wait_ge(sem("lin_rsum_spread"), 1)
                act.activation(linq[:, 4 * f:4 * f + 4, :].rearrange("p f n -> p (f n)"), bank[1 + f], ACT.Copy)\
                    .then_inc(sem("lin_spread_ready"), 1)
            std(2)
            std(3)
            act.wait_ge(sem("gate_neg_ready"), 1)
            act.activation(small[:, 40:40 + E0], bank[0][:, 0:E0], ACT.Exp, bias=small[:, 12:13],
                           accum_out=small[:, 13:14]).then_inc(sem("gate_exp_ready"), 1)
            for e in range(E0):
                act.wait_ge(sem("h0_in_psum"), e + 1)
                act.activation(h0T[:, 4 * e:4 * e + 4, :], bank[1 + e % 2].rearrange("p (f n) -> p f n", f=4),
                               ACT.Gelu).then_inc(sem("h0_ready"), 1)
            std(4)
            attention(1)
            std(5)
            act.wait_ge(sem("kvu_in_psum"), 2)
            act.activation(kvu[:, 2 * D:3 * D], bank[3][:, 0:D], ACT.Silu).then_inc(sem("u2_ready"), 1)
            act.wait_ge(sem("o2_sumsq_ready"), 1)
            act.activation(small[:, 64:80], small[:, 40:56], ACT.Sqrt).then_inc(sem("o2_norm_ready"), 1)
            std(6)
            act.wait_ge(sem("gate_neg_ready"), 2)
            act.activation(small[:, 40:40 + E1], bank[7][:, 0:E1], ACT.Exp, bias=small[:, 12:13],
                           accum_out=small[:, 13:14]).then_inc(sem("gate_exp_ready"), 1)
            act.activation(small[:, 14:15], bank[7][:, E1:E1 + 1], ACT.Sigmoid).then_inc(sem("sigmoid_ready"), 1)
            for r in range(5):
                act.wait_ge(sem("gate_in_psum"), r + 1)
                if r >= 2:
                    act.wait_ge(sem("h1_ready"), r - 1)
                act.activation(silu_g[:, r % 2, :], bank[1 + 2 * (r % 2)], ACT.Silu).then_inc(sem("silu_done"), 1)

        @block.gpsimd
        def _(pool):
            def cast(dst, src):
                return pool.tensor_tensor(dst, src, unity[:, :].broadcast_to(list(src.shape)), ALU.mult)

            pool.memset(unity[:, :], 1.0).then_inc(sem("unity_ready"), 1)
            pool.wait_ge(sem("unity_ready"), 1)

            def split_unit(g, buf, n):
                cols = slice(n * UNIT, (n + 1) * UNIT)
                rest = k_rest[:, n % REST_SLOTS, :]
                pool.wait_ge(sem("k_rest_done"), KREST_AHEAD + UPC * g + n + 1)
                cast(k_parts[buf][:, 1, cols], rest).then_inc(sem("k2_done"), 1)
                pool.wait_ge(sem("k2_done"), UPC * g + n + 1)
                pool.tensor_tensor(k_parts[buf][:, 2, cols], rest, k_parts[buf][:, 1, cols], ALU.subtract)\
                    .then_inc(sem("k_unit_split"), 1)

            pool.sem_inc(sem("k_unit_split"), SPLIT_AHEAD)
            with pool.Fori(0, CHUNKS // 2) as i:
                for buf in range(2):
                    for n in range(UPC):
                        split_unit(2 * i + buf, buf, n)
            for n in range(UPC):
                split_unit(CHUNKS - 1, 0, n)

            def split_max(h, par, layer):
                n = layer * HEADS + h
                pool.wait_ge(sem("negmax_ready"), n + 1)
                cast(negparts[:, par, 0:1], negmax[:, par]).then_inc(sem("split_step"), 1)
                pool.wait_ge(sem("split_step"), 3 * n + 1)
                pool.tensor_tensor(negrest[:, par], negmax[:, par], negparts[:, par, 0:1], ALU.subtract)\
                    .then_inc(sem("split_step"), 1)
                pool.wait_ge(sem("split_step"), 3 * n + 2)
                cast(negparts[:, par, 1:2], negrest[:, par]).then_inc(sem("split_step"), 1)
                pool.wait_ge(sem("split_step"), 3 * n + 3)
                pool.tensor_tensor(negparts[:, par, 2:3], negrest[:, par], negparts[:, par, 1:2], ALU.subtract)\
                    .then_inc(sem("negmax_split"), 1)

            for layer in range(2):
                split_max(0, 0, layer)

                def pair(i, last, p, chunks):
                    for par in range(2):
                        if chunks[par] is not None:
                            for n in range(UPC):
                                split_unit(CHUNKS * p + chunks[par], 0, n)
                        if not (last and par == 1):
                            split_max(2 * i + par + 1, 1 - par, layer)

                halves(pool, layer, pair)

        @block.vector
        def _(dve):
            steps = [0]

            def after(ins):
                ins.then_inc(sem("dve_step"), 1)
                steps[0] += 1
                dve.wait_ge(sem("dve_step"), steps[0])

            def stats(k, src):
                after(dve.bn_stats(small[:, 0:6], src))
                after(dve.bn_aggr(small[:, 6:8], small[:, 0:6]))
                dve.tensor_scalar(small[:, 8:9], small[:, 7:8], LN_EPS, None, ALU.add)\
                    .then_inc(sem("var_ready"), 1)
                dve.wait_ge(sem("std_ready"), k + 1)
                after(dve.reciprocal(small[:, 11:12], small[:, 10:11]))

            def layernorm(k, src):
                stats(k, src)
                dve.tensor_scalar(xhat[:, :], src, small[:, 6:7], small[:, 11:12], ALU.subtract, ALU.mult)\
                    .then_inc(sem("xhat_ready"), 1)

            def copy_xhatT(k, par, b):
                dve.wait_ge(sem("xhatT_in_psum"), k + 1)
                dve.tensor_copy(xhatT[:, par].rearrange("p c n -> p (c n)"), bank[b][:, 0:D])\
                    .then_inc(sem("xhatT_ready"), 1)

            def split_q(layer, b):
                dve.wait_ge(sem("q_in_psum"), layer + 1)
                for g in range(DC):
                    src = bank[b][:, g * P:(g + 1) * P]
                    if layer == 0:
                        ins = dve.tensor_scalar(qf[:, g, :], src, bq[:, g:g + 1], HD ** -0.5, ALU.add, ALU.mult)
                    else:
                        ins = dve.tensor_scalar(qf[:, g, :], src, HD ** -0.5, None, ALU.mult)
                after(ins)
                if layer == 1:
                    dve.wait_ge(sem("q_stored"), 16 * DC)
                after(dve.tensor_copy(qp[:, :, 0, :], qf[:, :, :]))
                after(dve.tensor_tensor(qr[:, :, :], qf[:, :, :], qp[:, :, 0, :], ALU.subtract))
                after(dve.tensor_copy(qp[:, :, 1, :], qr[:, :, :]))
                dve.tensor_tensor(qp[:, :, 2, :], qr[:, :, :], qp[:, :, 1, :], ALU.subtract)\
                    .then_inc(sem("q_split"), 1)

            dve.memset(bk[:, DC:2 * DC], 0.0).then_inc(sem("bk_zeroed"), 1)
            after(dve.memset(bv[:, D:2 * D], 0.0))
            for buf in range(2):
                after(dve.memset(v_ring[buf][:, :, :, HD:VW].rearrange("p h t c -> p (h t c)"), 1.0))
            dve.memset(vbuf[:, :, TILES * VW:], 0.0).then_inc(sem("vbuf_padded"), 1)
            dve.wait_ge(sem("x_loaded"), 16)
            layernorm(0, xs[:, 0, :])
            dve.wait_ge(sem("consts_loaded"), 16)
            dve.tensor_copy(identb[:, :], ident).then_inc(sem("identb_ready"), 1)
            copy_xhatT(0, 0, 0)
            dve.wait_ge(sem("q_weights_loaded"), 32)
            split_q(0, 1)

            dve.sem_inc(sem("k_rest_done"), KREST_AHEAD)
            dve.sem_inc(sem("v_batch_done"), VBATCH_AHEAD)
            for buf in range(2):
                dve.sem_inc(sem(f"v_stored{buf}"), STORED_V)
            dve.wait_ge(sem("kv_weights_loaded"), 64)

            def k_remainder(p, g, buf, n, b):
                dve.wait_ge(sem("k_unit_split"), UPC * g + n + 1)
                dve.wait_ge(sem("k1_done"), UPC * g + n + 1)
                dve.scalar_tensor_tensor(k_rest[:, n % REST_SLOTS, :], b[:, 0:UNIT], bk[:, p:p + 1],
                                         k_parts[buf][:, 0, n * UNIT:(n + 1) * UNIT],
                                         ALU.add, ALU.subtract).then_inc(sem("k_rest_done"), 1)

            def v_to_ring(p, g, use, buf, m, b):
                if m == 0:
                    dve.wait_ge(sem(f"v_stored{buf}"), STORED_V * (use + 1))
                tiles = batch_tiles(m)
                nt = len(tiles)
                dve.wait_ge(sem("v_in_psum"), BATCHES * g + m + 1)
                dve.tensor_tensor(
                    v_ring[buf][:, :, tiles[0]:tiles[0] + nt, 0:HD].rearrange("p h t d -> p t h d"),
                    b[:, 0:nt * P].rearrange("p (t h d) -> p t h d", h=GH, d=HD),
                    bv[:, p * P:(p + 1) * P].rearrange("p (a h d) -> p a h d", a=1, d=HD)
                    .broadcast_to([P, nt, GH, HD]), ALU.add).then_inc(sem("v_batch_done"), 1)

            def first_prep(c, use, buf):
                for n in range(UPC):
                    k_remainder(0, c, buf, n, bank[n])
                for m in range(BATCHES):
                    v_to_ring(0, c, use, buf, m, bank[4 + m])

            with dve.Fori(0, CHUNKS // 2) as i:
                first_prep(2 * i, i, 0)
                first_prep(2 * i + 1, i, 1)
            first_prep(CHUNKS - 1, CHUNKS // 2, 0)

            def attention(layer):
                base = layer * HEADS

                def reduce_unit(h, par, u):
                    n = (base + h) * UNITS + u
                    dve.wait_ge(sem("unit_in_psum"), n + 1)
                    dve.tensor_reduce(maxima[:, par, u:u + 1], a_banks[u % 2][:, 0:UNIT], AX.X, ALU.max)\
                        .then_inc(sem("unit_reduced"), 1)
                    if u == UNITS - 1:
                        dve.wait_ge(sem("unit_reduced"), n + 1)
                        dve.tensor_reduce(negmax[:, par], maxima[:, par], AX.X, ALU.max, negate=True)\
                            .then_inc(sem("negmax_ready"), 1)

                for u in range(UNITS):
                    reduce_unit(0, 0, u)
                for u in range(MAX_AHEAD):
                    reduce_unit(1, 1, u)

                def pair(i, last, p, chunks):
                    for par in range(2):
                        h = 2 * i + par
                        for j in range(GROUPS):
                            for q in (2 * j, 2 * j + 1):
                                u = q + MAX_AHEAD
                                if u < UNITS and not (last and par == 1):
                                    reduce_unit(h + 1, 1 - par, u)
                                elif u >= UNITS and not last:
                                    reduce_unit(h + 2, par, u - UNITS)
                                if chunks[par] is None:
                                    continue
                                c = chunks[par]
                                if q % 2 and j in K_AT:
                                    k_remainder(p, CHUNKS * p + c, 0, K_AT[j], x_bank)
                                if q % 2 == 0 and j in V_AT:
                                    v_to_ring(p, CHUNKS * p + c, prep_use(p, c), 0, V_AT[j], x_bank)

                halves(dve, layer, pair)

                dve.wait_ge(sem("o_gathered"), 2 * layer + 2)
                after(dve.reciprocal(rden[:, :, :], psum[:, 2:4, 0:P]))
                dve.tensor_tensor(attnT[:, :, :], psum[:, 0:2, 0:P], rden[:, :, :], ALU.mult)\
                    .then_inc(sem("attnT_ready"), 1)

            def add_block(k, b, res, dst):
                dve.wait_ge(sem("block_out"), k)
                after(dve.tensor_tensor(dst, bank[b][:, 0:D], res, ALU.add))

            attention(0)
            dve.wait_ge(sem("mid_weights_loaded"), 16 * 10)
            after(dve.tensor_tensor(xb[:, 0, :], xs[:, 0, :], bias_rows[:, 0, :], ALU.add))
            add_block(1, 6, xb[:, 0, :], xs[:, 1, :])

            layernorm(1, xs[:, 1, :])
            dve.tensor_tensor(xb[:, 1, :], xs[:, 1, :], bias_rows[:, 1, :], ALU.add).then_inc(sem("xb_ready"), 1)
            copy_xhatT(1, 1, 0)
            for n in range(4):
                dve.wait_ge(sem("lin_qk_in_psum"), n + 1)
                dst = (linq, link)[n // 2][:, 4 * (n % 2):4 * (n % 2) + 4, :]
                dve.tensor_scalar(dst, bank[1 + n].rearrange("p (f n) -> p f n", f=4), 0.0, LEPS, ALU.max, ALU.add)\
                    .then_inc(sem("lin_qk_ready"), 1)
            by_parity = lin_aT.rearrange("p (f r) n -> p r f n", r=2)
            for f in range(2):
                dve.wait_ge(sem("lin_scores_in_psum"), f + 1)
                for r in range(2):
                    dve.tensor_tensor(by_parity[:, r, 4 * f:4 * f + 4, :],
                                      bank[1 + 2 * r + f].rearrange("p (f n) -> p f n", f=4),
                                      causal.rearrange("p (a n) -> p a n", a=1).broadcast_to([P, 4, P]), ALU.mult)\
                        .then_inc(sem("lin_aT_ready"), 1)
            dve.wait_ge(sem("lin_sums_in_psum"), 1)
            dve.reciprocal(lin_rd, bank[0][0:LH, 0:P]).then_inc(sem("lin_rsum_ready"), 1)
            dve.wait_ge(sem("lin_av_in_psum"), 1)
            for f in range(2):
                dve.wait_ge(sem("lin_spread_ready"), f + 1)
                dve.tensor_tensor(lin_oT[:, 4 * f:4 * f + 4, :], bank[5 + f].rearrange("p (f n) -> p f n", f=4),
                                  linq[:, 4 * f:4 * f + 4, :], ALU.mult).then_inc(sem("lin_oT_ready"), 1)
            dve.wait_ge(sem("xb_ready"), 1)
            add_block(2, 7, xb[:, 1, :], xs[:, 2, :])

            def mixture_weights(k, b, n, rev, normalise):
                g = lambda j: gates[:, j, 0:n]
                one = lambda j: small[:, j:j + 1]
                dve.wait_ge(sem("logits_in_psum"), k + 1)
                dve.tensor_reduce(one(12), bank[b][:, 0:n], AX.X, ALU.max, negate=True)\
                    .then_inc(sem("gate_neg_ready"), 1)
                dve.wait_ge(sem("gate_exp_ready"), k + 1)
                after(dve.reciprocal(one(15), one(13)))
                after(dve.tensor_scalar(g(0), small[:, 40:40 + n], one(15), None, ALU.mult))
                for r in range(2):
                    p_, pick, left = (0, 1, 2) if r == 0 else (2, 3, None)
                    after(dve.tensor_reduce(one(16 + 2 * r), g(p_), AX.X, ALU.max))
                    after(dve.scalar_tensor_tensor(g(4), g(p_), one(16 + 2 * r), rev, ALU.is_equal, ALU.mult))
                    after(dve.tensor_reduce(one(17 + 2 * r), g(4), AX.X, ALU.max))
                    after(dve.tensor_scalar(g(pick), g(4), one(17 + 2 * r), None, ALU.is_equal))
                    if r == 0:
                        after(dve.scalar_tensor_tensor(g(left), g(pick), -2.0, g(p_), ALU.mult, ALU.add))
                after(dve.tensor_tensor(g(5), g(1), g(3), ALU.add))
                after(dve.tensor_tensor(g(6), g(5), g(0), ALU.mult))
                if normalise:
                    after(dve.tensor_tensor(one(20), one(16), one(18), ALU.add))
                    after(dve.reciprocal(one(21), one(20)))
                    after(dve.tensor_scalar(g(6), g(6), one(21), None, ALU.mult))

            def mix(n, e, b, res, dst):
                dve.wait_ge(sem("expert_in_psum"), n + 1)
                dve.scalar_tensor_tensor(dst, bank[b][:, 0:D], gates[:, 6, e:e + 1], res, ALU.mult, ALU.add)\
                    .then_inc(sem("expert_mixed"), 1)
                dve.wait_ge(sem("expert_mixed"), n + 1)

            layernorm(2, xs[:, 2, :])
            copy_xhatT(2, 0, 0)
            dve.wait_ge(sem("xhat_ready"), 3)
            stats(3, xhat[:, :])
            after(dve.tensor_scalar(rn[:, :], xhat[:, :], small[:, 6:7], small[:, 11:12], ALU.subtract, ALU.mult))
            after(dve.tensor_tensor(rn[:, :], rn[:, :], bias_rows[:, 2, :], ALU.mult))
            dve.tensor_tensor(rn[:, :], rn[:, :], bias_rows[:, 3, :], ALU.add).then_inc(sem("rn_ready"), 1)
            copy_xhatT(3, 1, 3)
            mixture_weights(0, 0, E0, const("rev0"), False)
            for e in range(E0):
                mix(e, e, 4 + e % 4, xs[:, 2, :] if e == 0 else acc[:, (e - 1) % 2, :],
                    xs[:, 3, :] if e == E0 - 1 else acc[:, e % 2, :])

            dve.memset(vbuf[:, :, TILES * VW:], 0.0).then_inc(sem("vbuf_padded"), 1)
            after(dve.memset(v_ring[0][:, :, :, HD:VW].rearrange("p h t c -> p (h t c)"), 1.0))
            layernorm(4, xs[:, 3, :])
            copy_xhatT(4, 0, 0)
            split_q(1, 1)
            attention(1)
            add_block(3, 6, xs[:, 3, :], xs[:, 4, :])

            layernorm(5, xs[:, 4, :])
            copy_xhatT(5, 1, 0)
            dve.wait_ge(sem("kvu_in_psum"), 1)
            dve.tensor_scalar(kvu[:, 0:D], bank[2][:, 0:D], 0.0, HD ** -0.5, ALU.max, ALU.mult)\
                .then_inc(sem("kv2_ready"), 1)
            dve.tensor_copy(kvu[:, D:2 * D], bank[2][:, D:2 * D]).then_inc(sem("kv2_ready"), 1)
            dve.wait_ge(sem("q2_in_psum"), 1)
            dve.tensor_scalar(q2T, bank[1][:, 0:D].rearrange("p (g n) -> p g n", g=DC), 0.0, HD ** -0.5,
                              ALU.max, ALU.mult).then_inc(sem("q2_ready"), 1)
            dve.wait_ge(sem("kv_outer_in_psum"), 1)
            for g in range(DC):
                dve.tensor_tensor(kvm[:, g, :], bank[4 + g][:, 0:P], blockdiag, ALU.mult).then_inc(sem("kvm_ready"), 1)
            dve.wait_ge(sem("o2_in_psum"), 1)
            raw = acc[:, 2, :]
            after(dve.tensor_copy(raw, bank[7][:, 0:D]))
            after(dve.scalar_tensor_tensor(o2sq, raw, 1.0 / HD, raw, ALU.mult, ALU.mult))
            dve.tensor_reduce(small[:, 40:56], o2sq.rearrange("p (h d) -> p h d", d=HD), AX.X, ALU.add)\
                .then_inc(sem("o2_sumsq_ready"), 1)
            dve.wait_ge(sem("o2_norm_ready"), 1)
            after(dve.tensor_scalar(small[:, 64:80], small[:, 64:80], 1e-12, None, ALU.max))
            after(dve.reciprocal(small[:, 80:96], small[:, 64:80]))
            after(dve.tensor_tensor(o2.rearrange("p (h d) -> p h d", d=HD), raw.rearrange("p (h d) -> p h d", d=HD),
                                    small[:, 80:96].rearrange("p (h a) -> p h a", a=1).broadcast_to([P, HEADS, HD]),
                                    ALU.mult))
            dve.wait_ge(sem("u2_ready"), 1)
            dve.tensor_tensor(o2, o2, kvu[:, 2 * D:3 * D], ALU.mult).then_inc(sem("o2_ready"), 1)
            dve.wait_ge(sem("o2T_in_psum"), 1)
            dve.tensor_copy(o2T.rearrange("p c n -> p (c n)"), bank[0][:, 0:D]).then_inc(sem("o2T_ready"), 1)
            add_block(4, 6, xs[:, 4, :], xs[:, 5, :])

            layernorm(6, xs[:, 5, :])
            copy_xhatT(6, 0, 0)
            mixture_weights(1, 7, E1, const("rev1"), True)

            def gated(r):
                dve.wait_ge(sem("silu_done"), r + 1)
                dve.wait_ge(sem("up_in_psum"), r + 1)
                dve.tensor_tensor(h1T[:, 4 * r:4 * r + 4, :], silu_g[:, r % 2, :].rearrange("p (f n) -> p f n", f=4),
                                  bank[2 + 2 * (r % 2)].rearrange("p (f n) -> p f n", f=4), ALU.mult)\
                    .then_inc(sem("h1_ready"), 1)
            gated(0)
            for r in range(4):
                gated(r + 1)
                for e in range(4 * r, 4 * r + 4):
                    mix(E0 + e, e, (0, 5, 6)[e % 3], xs[:, 5, :] if e == 0 else acc[:, (e - 1) % 2, :],
                        acc[:, e % 2, :])
            dve.wait_ge(sem("shared_in_psum"), 1)
            dve.scalar_tensor_tensor(xs[:, 6, :], bank[7][:, 0:D], small[:, 14:15], acc[:, (E1 - 1) % 2, :],
                                     ALU.mult, ALU.add).then_inc(sem("out_ready"), 1)


def kernel(**inputs):
    import concourse.bacc as bacc
    from concourse.bass_utils import run_bass_kernel_spmd

    v = {k: np.asarray(x) for k, x in inputs.items()}
    hid = lambda w: w.transpose(2, 0, 1).reshape(w.shape[2], -1)
    arrays = {
        "x": v["x"][0], "ctxT": v["ctx_512"][0].T, "consts": _constants(),
        "ones": np.full((3, KEYS), 0x3F80, np.uint16),
        "wk": np.concatenate([v["L0_xattn_Wk"], v["L1_xattn_Wkv"][:D].T], 1),
        "wv": np.concatenate([v["L0_xattn_Wv"], v["L1_xattn_Wkv"][D:].T], 1),
        "bq": v["L0_xattn_bq"].reshape(DC, P).T, "bk": v["L0_xattn_bk"].reshape(DC, P).T, "bv": v["L0_xattn_bv"], "bo0": v["L0_xattn_bo"],
        "wq0": v["L0_xattn_Wq"], "wq1": v["L1_xattn_Wq"].T, "wo0": v["L0_xattn_Wo"], "wo1": v["L1_xattn_Wo"].T,
        "lin_w": np.concatenate([v["L0_attn_Wq"], v["L0_attn_Wk"], v["L0_attn_Wv"]], 1),
        "lin_wo": v["L0_attn_Wo"], "lin_bo": v["L0_attn_bo"],
        "gamma": v["L0_ffn_ln_gamma"], "beta": v["L0_ffn_ln_beta"], "gate0": v["L0_ffn_gate_w"].T,
        "w1": hid(v["L0_ffn_w1"]), "w2": v["L0_ffn_w2"].transpose(0, 2, 1).reshape(E0 * F0, D),
        "w_q2": v["L1_attn_Wq"].T, "w_o2": v["L1_attn_Wo"].T,
        "w_kvu": np.concatenate([v["L1_attn_Wk"].T, v["L1_attn_Wv"].T, v["L1_attn_Wu"].T], 1),
        "gate1": np.concatenate([v["L1_ffn_Wg"].T, v["L1_ffn_Wsg"].T], 1),
        "we_in": np.stack([np.concatenate([hid(v["L1_ffn_We_gate"]), v["L1_ffn_Ws_gate"].T], 1),
                           np.concatenate([hid(v["L1_ffn_We_up"]), v["L1_ffn_Ws_up"].T], 1)], 1),
        "we_out": np.concatenate([v["L1_ffn_We_down"].transpose(0, 2, 1).reshape(E1 * F1, D),
                                  v["L1_ffn_Ws_down"].T], 0),
    }
    nc = bacc.Bacc("TRN2", target_bir_lowering=False, num_devices=1)
    feed, aps = {}, {}
    for name, x in arrays.items():
        x = np.ascontiguousarray(x)
        feed[f"in_{name}"] = x
        dt = BF16 if name == "ones" else mybir.dt.from_np(x.dtype)
        t = nc.dram_tensor(f"in_{name}", x.shape, mybir.dt.from_np(x.dtype), kind="ExternalInput").ap()
        aps[name] = t.bitcast(BF16) if name == "ones" else t
    out = nc.dram_tensor("out", (P, D), F32, kind="ExternalOutput").ap()
    program(nc, aps, out)
    r = run_bass_kernel_spmd(nc, [feed], core_ids=[0])
    return r.results[0]["out"].reshape(1, P, D)
```

```python
from contextlib import ExitStack

import concourse.bass as bass
import numpy as np
from concourse import mybir

F32 = mybir.dt.float32
BF16 = mybir.dt.bfloat16
ALU = mybir.AluOpType
ACT = mybir.ActivationFunctionType
AX = mybir.AxisListType

P = 128
D = 256
DC = D // P
CD = 128
KEYS = 12544
HEADS = 16
HD = D // HEADS
VW = HD + 1
TILES = KEYS // P
CHUNK = 1792
CHUNKS = KEYS // CHUNK
CT = CHUNK // P
UNIT = 448
UNITS = KEYS // UNIT
UPC = CHUNK // UNIT
GT = 7
GROUPS = TILES // GT
GPC = CT // GT
GH = 8
BATCHES = 4
REST_SLOTS = 2
PREP = (("K", 0, 1), ("K", 1, 3), ("K", 2, 5), ("K", 3, 7), ("V", 0, 9), ("V", 1, 10), ("V", 2, 11), ("V", 3, 13))
FIRST_PREP = (("K", 0), ("K", 1), ("V", 0), ("K", 2), ("V", 1), ("K", 3), ("V", 2), ("V", 3))
V_TILES = ((0, 3), (3, 6), (6, 10), (10, 14))
V_BEFORE_MAX = 3
HALF_READ = 3
K_AT = {j: n for kind, n, j in PREP if kind == "K"}
V_AT = {j: n for kind, n, j in PREP if kind == "V"}
MAX_AHEAD = 6
EARLY = -(-MAX_AHEAD // UPC)
STACK = 6 * HD
QPART = (0, 0, 0, 1, 1, 2)
KROWS = ((0, 3), (48, 2), (80, 1))
SROWS = STACK + 3

LH, LD = 16, 64
LEPS = 1e-3
E0, F0 = 8, 512
E1, F1 = 16, 128
FS = 512
SLOTS1 = E1 + FS // F1
EPP = SLOTS1 // (GH // 2)
LN_EPS = 1e-5

_CONSTS = {"ident": P, "causal": P, "numsel": 2 * P - HD, "densel": 2 * P - HD, "blockdiag": P,
           "rev0": E0, "rev1": E1, "onecol": 31, "spread": LH * LD}


def _const_at(name):
    at = 0
    for n, w in _CONSTS.items():
        if n == name:
            return at, at + w
        at += w


def _constants():
    p = np.arange(P)[:, None]
    out = np.zeros((P, sum(_CONSTS.values())), np.float32)

    def put(name, a):
        lo, hi = _const_at(name)
        out[:, lo:hi] = a
    col = np.arange(P)[None, :]
    put("ident", p == col)
    put("causal", p <= col)
    j = np.arange(2 * P - HD)[None, :] - (P - HD)
    put("numsel", (p % 32 == j) & (j >= 0) & (j < HD))
    put("densel", (p % 32 == HD) & (j >= 0) & (j < HD))
    put("blockdiag", p // HD == col // HD)
    put("rev0", E0 - np.arange(E0)[None, :] + 0 * p)
    put("rev1", E1 - np.arange(E1)[None, :] + 0 * p)
    put("onecol", (np.arange(31)[None, :] == 15) & (p >= 0))
    put("spread", p == np.arange(LH * LD)[None, :] // LD)
    return out


def program(nc, a, out):
    ctx = ExitStack()
    with ctx:
        def sb(name, shape, dt=F32):
            return ctx.enter_context(nc.sbuf_tensor(name, shape, dt))

        sems = {}

        def sem(name):
            if name not in sems:
                sems[name] = ctx.enter_context(nc.semaphore(name))
            return sems[name]

        k_scratch = nc.dram_tensor("k_scratch", [2, HEADS, 3, HD, KEYS], BF16, kind="Internal").ap()
        v_scratch = nc.dram_tensor("v_scratch", [2 * HEADS, P, TILES * VW], F32, kind="Internal").ap()
        q_scratch = nc.dram_tensor("q_scratch", [2, 3, D, P], BF16, kind="Internal").ap()

        consts = sb("consts", [P, sum(_CONSTS.values())])

        def const(name):
            lo, hi = _const_at(name)
            return consts[:, lo:hi]
        ident, causal, blockdiag = const("ident"), const("causal"), const("blockdiag")
        numsel, densel, onecol, spread = const("numsel"), const("densel"), const("onecol"), const("spread")
        wk = sb("wk", [CD, 2 * D])
        wv = sb("wv", [CD, 2 * D])
        bk = sb("bk", [P, 2 * DC])
        bv = sb("bv", [P, 2 * D])
        bq = sb("bq", [P, DC])
        wq = sb("wq", [P, 2, DC, D])
        wo = sb("wo", [P, 2, DC, D])
        bias_rows = sb("bias_rows", [P, 4, D])
        gate0 = sb("gate0", [P, DC, E0])
        gate1 = sb("gate1", [P, DC, E1 + 1])
        xs = sb("xs", [P, 7, D])
        xb = sb("xb", [P, 2, D])
        xhat = sb("xhat", [P, D])
        xhatT = sb("xhatT", [P, 2, DC, P])
        rn = sb("rn", [P, D])
        small = sb("small", [P, 96])
        attnT = sb("attnT", [P, DC, P])
        rden = sb("rden", [P, DC, P])
        qf = sb("qf", [P, DC, P])
        qr = sb("qr", [P, DC, P])
        qp = sb("qp", [P, DC, 3, P], BF16)
        qstack = sb("qstack", [P, HEADS, P], BF16)
        maxima = sb("maxima", [P, 2, UNITS])
        negmax = sb("negmax", [P, 2, 1])
        negrest = sb("negrest", [P, 2, 1])
        gates = sb("gates", [P, 7, E1])
        negparts = sb("negparts", [P, 2, 3], BF16)
        unity = sb("unity", [P, 1])
        identb = sb("identb", [P, P], BF16)

        region_k = sb("region_k", [P, 2 * KEYS], BF16)
        kstack = region_k[:, :].rearrange("p (b k) -> p b k", b=2)
        as_f = region_k[:, :].bitcast(F32)
        h0T = as_f[:, KEYS - 32 * P:KEYS].rearrange("p (f n) -> p f n", f=32)
        region_w = sb("region_w", [P, 16384])
        lin_w = region_w[:, 0:DC * 3072].rearrange("p (k n) -> p k n", k=DC)
        lin_wo = region_w[:, 6144:8192].rearrange("p (f c) -> p f c", f=8)
        w2 = region_w[:, 0:32 * D].rearrange("p (f c) -> p f c", f=32)
        w1 = region_w[:, 8192:16384].rearrange("p (k n) -> p k n", k=DC)
        we_in = region_w[:, 0:DC * 2 * 20 * P].rearrange("p (k s f) -> p k s f", k=DC, s=2)
        we_out = region_w[:, 10240:10240 + 20 * D].rearrange("p (e c) -> p e c", e=20)
        o_heads = sb("o_heads", [P, HEADS, P])
        PARTS = CHUNK * 3 // 2
        VRING = GH * CT * VW
        w_at, k_at = 8192, KEYS // 2
        ctx_buf = [region_w[:, w_at:w_at + CHUNK], as_f[:, k_at:k_at + CHUNK]]
        k_parts = [r.bitcast(BF16).rearrange("p (s k) -> p s k", s=3) for r in (
            region_w[:, w_at + CHUNK:w_at + CHUNK + PARTS], as_f[:, k_at + CHUNK:k_at + CHUNK + PARTS])]
        v_ring = [r.rearrange("p (h t c) -> p h t c", h=GH, t=CT) for r in (
            region_w[:, w_at + CHUNK + PARTS:w_at + CHUNK + PARTS + VRING],
            o_heads[:, :, :].rearrange("p a b -> p (a b)")[:, 0:VRING])]
        rest_at = w_at + CHUNK + PARTS + VRING
        k_rest = region_w[:, rest_at:rest_at + REST_SLOTS * UNIT].rearrange("p (b k) -> p b k", b=REST_SLOTS)

        vbuf = sb("vbuf", [P, 2, TILES * VW + 32 - VW])
        probs = sb("probs", [P, 2, GT * P])
        linq = sb("linq", [P, 8, P])
        link = sb("link", [P, 8, P])
        linv = o_heads[:, 0:8, :].rearrange("p a b -> p (a b)")
        lin_oT = o_heads[:, 8:16, :]
        lin_aT = vbuf[:, :, :].rearrange("p a b -> p (a b)")[:, 0:LH * P].rearrange("p (h n) -> p h n", h=LH)
        lin_rd = probs[0:LH, 0, 0:P]
        w_kvu = sb("w_kvu", [P, DC, 3 * D])
        w_q2 = region_w[:, 15360:15872].rearrange("p (k n) -> p k n", k=DC)
        w_o2 = region_w[:, 15872:16384].rearrange("p (k n) -> p k n", k=DC)
        q2T = linq[:, 0:2, :]
        kvu = o_heads[:, 0:6, :].rearrange("p a b -> p (a b)")
        kvm = linq[:, 2:4, :]
        o2 = linq[:, 4:6, :].rearrange("p a b -> p (a b)")
        o2sq = linq[:, 6:8, :].rearrange("p a b -> p (a b)")
        o2T = link[:, 0:2, :]
        h1T = vbuf[:, :, :].rearrange("p a b -> p (a b)")[:, 0:20 * P].rearrange("p (e n) -> p e n", e=20)
        acc = link[:, 0:8, :].rearrange("p a b -> p (a b)").rearrange("p (s c) -> p s c", s=4)
        silu_g = probs[:, :, 0:4 * P]

        psum = ctx.enter_context(nc.psum_tensor("psum", [P, 8, 512], F32))
        bank = [psum[:, b, :] for b in range(8)]
        s_slots = [psum[:, 0:2, :].rearrange("p a b -> p (a b)"), psum[:, 2:4, :].rearrange("p a b -> p (a b)")]
        o_bank = bank[4]
        x_bank = bank[5]
        a_banks = [bank[6], bank[7]]

        block = ctx.enter_context(nc.Block())

        KREST_AHEAD, VBATCH_AHEAD = 2, BATCHES
        REDUCED_AHEAD = 2
        SPLIT_AHEAD = REST_SLOTS
        STORED_K, STORED_V = 16 * GH, 16

        def prep_use(p, c):
            return (CHUNKS + 1) // 2 + (p - 1) * CHUNKS + c

        def halves(eng, layer, pair):
            for half in range(2):
                p = (2 * layer + half + 1) % 4
                some = lambda c: c if p else None
                first = half * (GH // 2)
                with eng.Fori(first, first + GH // 2 - 1) as i:
                    c = 2 * (i - first) + p % 2
                    pair(i, False, p, (some(c), some(c + 1)))
                pair(first + GH // 2 - 1, half == 1, p, (None if p % 2 else some(CHUNKS - 1), None))

        def batch_tiles(m):
            return range(*V_TILES[m])

        def once(eng, name, *pairs):
            for dst, src in pairs:
                eng.dma_start(dst, src).then_inc(sem(name), 16)
            return 16 * len(pairs)
        on_all = lambda v: v.rearrange("(a n) -> a n", a=1).broadcast_to([P, v.shape[0]])

        def vcols(buf, t):
            return vbuf[:, buf, t * VW:t * VW + 32]

        PROLOGUE_BANKS = (((bank[0], bank[1]), bank[2:6]), ((bank[2], bank[3]), bank[4:8]))

        @block.sync
        def _(sp):
            once(sp, "x_loaded", (xs[:, 0, :], a["x"]))
            once(sp, "kv_weights_loaded", (wk[:, :], a["wk"]), (wv[:, :], a["wv"]),
                 (bk[:, 0:DC], a["bk"]), (bv[:, 0:D], on_all(a["bv"])))

            def load_ctx(c, buf, half):
                at = half * (CHUNK // 2)
                sp.dma_start(ctx_buf[buf][:, at:at + CHUNK // 2],
                             a["ctxT"][:, bass.ds(c * CHUNK + at, CHUNK // 2)])\
                    .then_inc(sem(f"ctx_loaded{buf}_{half}"), 16)

            def store_k(p, c, g, buf):
                sp.wait_ge(sem("k_unit_split"), SPLIT_AHEAD + UPC * (g + 1))
                for h in range(GH):
                    sp.dma_start(k_scratch[p // 2, GH * (p % 2) + h, :, :, bass.ds(c * CHUNK, CHUNK)]
                                 .rearrange("s d k -> d s k"), k_parts[buf][h * HD:(h + 1) * HD])\
                        .then_inc(sem(f"k_stored{buf}"), 16)

            def store_v(p, c, g, buf):
                sp.wait_ge(sem("v_batch_done"), VBATCH_AHEAD + BATCHES * (g + 1))
                sp.dma_start(v_scratch[GH * p:GH * (p + 1), :, bass.ds(c * CT * VW, CT * VW)]
                             .rearrange("h p n -> p h n"),
                             v_ring[buf].rearrange("p h t c -> p h (t c)")).then_inc(sem(f"v_stored{buf}"), 16)

            for half in range(2):
                load_ctx(0, 0, half)
            once(sp, "ident_loaded", (ident, a["consts"][:, 0:P]))
            once(sp, "q_weights_loaded", (wq[:, 0], a["wq0"].rearrange("(k p) n -> p k n", p=P)),
                 (bq[:, :], a["bq"]))
            for half in range(2):
                load_ctx(1, 1, half)
            sp.dma_start(kstack[STACK:SROWS, 0, :], a["ones"]).then_inc(sem("ones_loaded"), 16)

            def stack_q(layer):
                sp.wait_ge(sem("q_split"), layer + 1)
                for g in range(DC):
                    sp.dma_start(q_scratch[layer, :, g * P:(g + 1) * P, :].rearrange("s r n -> r s n"), qp[:, g])\
                        .then_inc(sem("q_stored"), 16)
                sp.wait_ge(sem("q_stored"), 16 * DC * (layer + 1))
                for b, s in enumerate(QPART):
                    sp.dma_start(qstack[b * HD:(b + 1) * HD, :, :],
                                 q_scratch[layer, s].rearrange("(h d) n -> d h n", d=HD))\
                        .then_inc(sem("q_stacked"), 16)

            def stack(layer, h, buf, cols, name):
                for row, parts in KROWS:
                    rows = parts * HD
                    sp.dma_start(kstack[row:row + rows, buf, cols],
                                 k_scratch[layer, bass.ds(h, 1)].rearrange("a s d k -> (a s d) k")[0:rows, cols])\
                        .then_inc(sem(name), 16)

            def load_first_stack(c, par, uses):
                sp.wait_ge(sem(f"k_stored{par}"), STORED_K * (uses + 1))
                stack(0, 0, 0, bass.ds(c * CHUNK, CHUNK), f"first_stack_loaded{par}")

            def after_chunk(c, use, buf, more=True, before=True):
                if before:
                    load_first_stack(c - 1, 1 - buf, use + buf)
                if more:
                    sp.wait_ge(sem("v_in_psum"), BATCHES * (c + 1))
                    for half in range(2):
                        load_ctx(c + 2, buf, half)
                store_v(0, c, c, buf)
                store_k(0, c, c, buf)

            after_chunk(0, 0, 0, before=False)
            stack_q(0)
            after_chunk(1, 0, 1)
            with sp.Fori(1, CHUNKS // 2 - 1) as i:
                after_chunk(2 * i, i, 0)
                after_chunk(2 * i + 1, i, 1)
            after_chunk(CHUNKS - 3, CHUNKS // 2 - 1, 0)
            after_chunk(CHUNKS - 2, CHUNKS // 2 - 1, 1, more=False)
            def load_k(layer, h, buf, c):
                stack(layer, h, buf, slice(c * CHUNK, (c + 1) * CHUNK), f"k_loaded{buf}_{c}")

            def load_v(layer, h, buf):
                sp.dma_start(vbuf[:, buf, 0:TILES * VW],
                             v_scratch[bass.ds(layer * HEADS + h, 1)].rearrange("a p n -> p (a n)"))\
                    .then_inc(sem(f"v_loaded{buf}"), 16)

            def prologue_context(layer):
                for half in range(2):
                    load_ctx(0, 0, half)

            def load_ones(buf):
                sp.dma_start(kstack[STACK:SROWS, buf, :], a["ones"]).then_inc(sem("ones_loaded"), 16)

            def second_stack_start(layer):
                for c in range(EARLY):
                    load_k(layer, 1, 1, c)

            load_first_stack(CHUNKS - 2, 1, CHUNKS // 2)
            sp.wait_ge(sem("v_in_psum"), BATCHES * CHUNKS)
            prologue_context(0)
            store_v(0, CHUNKS - 1, CHUNKS - 1, 0)
            store_k(0, CHUNKS - 1, CHUNKS - 1, 0)
            load_ones(1)
            second_stack_start(0)
            load_first_stack(CHUNKS - 1, 0, CHUNKS // 2 + 1)
            for buf, uses in ((0, (CHUNKS + 1) // 2), (1, CHUNKS // 2)):
                sp.wait_ge(sem(f"v_stored{buf}"), STORED_V * (uses + 1))

            def attention_loads(layer):
                base = layer * HEADS
                if layer == 0:
                    load_v(0, 0, 0)
                for c in range(EARLY, CHUNKS):
                    load_k(layer, 1, 1, c)
                if layer == 0:
                    load_v(0, 1, 1)
                p = 2 * layer + 1
                store_v(p, 0, CHUNKS * p, 0)
                store_k(p, 0, CHUNKS * p, 0)
                sp.wait_ge(sem("k_in_psum"), UPC * (CHUNKS * p + 1))
                sp.wait_ge(sem("v_in_psum"), BATCHES * (CHUNKS * p + 1))
                for half in range(2):
                    load_ctx(1, 0, half)

                if layer == 0:
                    once(sp, "mid_weights_loaded",
                         (wq[:, 1], a["wq1"].rearrange("(k p) n -> p k n", p=P)),
                         (wo[:, 0], a["wo0"].rearrange("(k p) n -> p k n", p=P)),
                         (wo[:, 1], a["wo1"].rearrange("(k p) n -> p k n", p=P)),
                         (bias_rows[:, 0, :], on_all(a["bo0"])), (bias_rows[:, 1, :], on_all(a["lin_bo"])),
                         (bias_rows[:, 2, :], on_all(a["gamma"])), (bias_rows[:, 3, :], on_all(a["beta"])),
                         (gate0[:, :, :], a["gate0"].rearrange("(k p) n -> p k n", p=P)),
                         (gate1[:, :, :], a["gate1"].rearrange("(k p) n -> p k n", p=P)),
                         (w_kvu[:, :, :], a["w_kvu"].rearrange("(k p) n -> p k n", p=P)),
                         (consts[:, P:], a["consts"][:, P:]))

                def head(h, par, more, p, c, new_piece, extra=None):
                    g = CHUNKS * (p or 0) + c if p else None
                    for cc in range(CHUNKS):
                        if more:
                            sp.wait_ge(sem("scores_done"), (base + h) * GROUPS + GPC * (cc + 1))
                            if new_piece:
                                sp.wait_ge(sem("k_stored0"), STORED_K * (prep_use(new_piece, cc) + 2))
                            load_k(layer, h + 2, par, cc)
                        if p and cc == 4:
                            store_k(p, c, g, 0)
                        if p and cc == 5 and not (isinstance(c, int) and c == CHUNKS - 1):
                            sp.wait_ge(sem("v_in_psum"), BATCHES * g + HALF_READ)
                            load_ctx(c + 1, 0, 0)
                        if extra and cc == 5:
                            extra()
                    if p:
                        if not (isinstance(c, int) and c == CHUNKS - 1):
                            sp.wait_ge(sem("v_in_psum"), BATCHES * (g + 1))
                            load_ctx(c + 1, 0, 1)
                        store_v(p, c, g, 0)
                    if more:
                        sp.wait_ge(sem("head_done"), base + h + 1)
                        if new_piece:
                            sp.wait_ge(sem("v_stored0"), STORED_V * (prep_use(new_piece, CHUNKS) + 1))
                        load_v(layer, h + 2, par)

                for half in range(2):
                    p = (2 * layer + half + 1) % 4
                    first = half * (GH // 2)

                    def weights(i):
                        n = i - first

                        def lin_in():
                            cols = bass.ds(n * (3072 // 4), 3072 // 4)
                            once(sp, "lin_weights_loaded",
                                 (lin_w[:, :, cols], a["lin_w"].rearrange("(k p) n -> p k n", p=P)[:, :, cols]))

                        def lin_out():
                            once(sp, "lin_weights_loaded",
                                 (lin_wo[:, bass.ds(2 * n, 2), :],
                                  a["lin_wo"].rearrange("(f p) c -> p f c", p=P)[:, bass.ds(2 * n, 2), :]))

                        def experts_in():
                            cols = bass.ds(n * EPP * P, EPP * P)
                            for s in range(2):
                                once(sp, "experts_loaded",
                                     (we_in[:, :, s, cols], a["we_in"][:, s, cols].rearrange("(k p) f -> p k f", p=P)))

                        def experts_out():
                            once(sp, "experts_loaded",
                                 (we_out[:, bass.ds(n * EPP, EPP), :],
                                  a["we_out"].rearrange("(e p) c -> p e c", p=P)[:, bass.ds(n * EPP, EPP), :]))
                        if layer == 0 and half == 0:
                            return lin_in, lin_out
                        if layer == 1 and half == 1:
                            return experts_in, experts_out
                        return None, None
                    with sp.Fori(first, first + GH // 2 - 1) as i:
                        beside = weights(i)
                        c = 2 * (i - first) + p % 2
                        head(2 * i, 0, True, p, c, None, beside[0])
                        head(2 * i + 1, 1, True, p, c + 1, None, beside[1])
                    i = first + GH // 2 - 1
                    beside = weights(i)
                    new_piece = p if half == 0 else None
                    head(2 * i, 0, half == 0, None if p % 2 else p, CHUNKS - 1, new_piece, beside[0])
                    if layer == 0 and half == 1:
                        sp.wait_ge(sem("k_stored0"), STORED_K * (prep_use(2, CHUNKS) + 1))
                        sp.wait_ge(sem("v_stored0"), STORED_V * (prep_use(2, CHUNKS) + 1))
                        once(sp, "w1_loaded", (w1[:, :, :], a["w1"].rearrange("(k p) n -> p k n", p=P)))
                    head(2 * i + 1, 1, half == 0, None, 0, new_piece, beside[1])
                    if layer == 1 and half == 0:
                        for part in range(2):
                            sp.wait_ge(sem(f"ctx_loaded0_{part}"), 16 * (prep_use(3, CHUNKS) + 1))
                        once(sp, "lin2_weights_loaded",
                             (w_q2, a["w_q2"].rearrange("(k p) n -> p k n", p=P)),
                             (w_o2, a["w_o2"].rearrange("(k p) n -> p k n", p=P)))

            attention_loads(0)
            sp.wait_ge(sem("head_done"), HEADS)
            load_ones(0)
            for c in range(CHUNKS):
                load_k(1, 0, 0, c)
            second_stack_start(1)
            w2_rows = a["w2"].rearrange("(f p) c -> p f c", p=P)
            sp.wait_ge(sem("lin_v_in_psum"), 2)
            once(sp, "w2_loaded", (w2[:, 0:24, :], w2_rows[:, 0:24, :]))
            sp.wait_ge(sem("block_out"), 2)
            once(sp, "w2_loaded", (w2[:, 24:32, :], w2_rows[:, 24:32, :]))
            for h in range(2):
                load_v(1, h, h)
            sp.wait_ge(sem("h0_in_psum"), E0)
            prologue_context(1)
            sp.wait_ge(sem("expert_in_psum"), E0)
            load_ones(1)
            stack_q(1)
            attention_loads(1)
            sp.wait_ge(sem("out_ready"), 1)
            sp.dma_start(out, xs[:, 6, :]).then_inc(sem("out_stored"), 16)
            sp.wait_ge(sem("out_stored"), 16)

        @block.tensor
        def _(pe):
            mm, tr = pe.matmul, pe.transpose

            def transpose_xhat(k, src, slot, b):
                for c in range(DC):
                    ins = tr(bank[b][:, c * P:(c + 1) * P], src[:, c * P:(c + 1) * P], ident)
                ins.then_inc(sem("xhatT_in_psum"), 1)

            def project_q(layer, par, b):
                for g in range(DC):
                    for c in range(DC):
                        ins = mm(bank[b][:, g * P:(g + 1) * P], wq[:, layer, c, g * P:(g + 1) * P],
                                 xhatT[:, par, c, :], start=(c == 0), stop=(c == DC - 1))
                ins.then_inc(sem("q_in_psum"), 1)

            pe.wait_ge(sem("kv_weights_loaded"), 64)

            def k_unit(p, c_g, buf, n, b):
                mm(b[:, 0:UNIT], wk[:, p * P:(p + 1) * P], ctx_buf[buf][:, n * UNIT:(n + 1) * UNIT],
                   start=True, stop=True).then_inc(sem("k_in_psum"), 1)

            def v_batch(p, buf, m, b):
                for k, t in enumerate(batch_tiles(m)):
                    ins = mm(b[:, k * P:(k + 1) * P], ctx_buf[buf][:, t * P:(t + 1) * P], wv[:, p * P:(p + 1) * P],
                             start=True, stop=True)
                ins.then_inc(sem("v_in_psum"), 1)

            def max_matmul(n, a_, qh, keys):
                pe.wait_ge(sem("unit_reduced"), REDUCED_AHEAD + n - 1)
                mm(a_banks[a_ % 2][:, 0:UNIT], qstack[0:STACK, bass.ds(qh, 1), :], keys, start=True, stop=True)\
                    .then_inc(sem("unit_in_psum"), 1)

            def first_stack_units(c, par, uses):
                pe.wait_ge(sem(f"first_stack_loaded{par}"), 48 * (uses + 1))
                for n in range(UPC):
                    max_matmul(UPC * c + n, n, 0, kstack[0:STACK, 0, bass.ds(c * CHUNK + n * UNIT, UNIT)])

            def first_prep(c, use, buf, stack=True):
                for kind, n in FIRST_PREP:
                    if kind == "K":
                        if n % 2 == 0:
                            pe.wait_ge(sem(f"ctx_loaded{buf}_{n // 2}"), 16 * (use + 1))
                        pe.wait_ge(sem("k_rest_done"), UPC * c + n + 1)
                        k_unit(0, c, buf, n, bank[n % 2])
                    else:
                        if stack and n == BATCHES - 1:
                            first_stack_units(c - 2, buf, use - 1)
                        pe.wait_ge(sem("v_batch_done"), BATCHES * c + n + 1)
                        v_batch(0, buf, n, bank[2 + n])

            first_prep(0, 0, 0, stack=False)
            pe.wait_ge(sem("ident_loaded"), 16)
            pe.wait_ge(sem("xhat_ready"), 1)
            transpose_xhat(0, xhat, 0, 6)
            pe.wait_ge(sem("q_weights_loaded"), 32)
            pe.wait_ge(sem("xhatT_ready"), 1)
            project_q(0, 0, 7)
            first_prep(1, 0, 1, stack=False)
            pe.wait_ge(sem("q_stacked"), 96)
            with pe.Fori(1, CHUNKS // 2) as i:
                first_prep(2 * i, i, 0)
                first_prep(2 * i + 1, i, 1)
            first_prep(CHUNKS - 1, CHUNKS // 2, 0)
            first_stack_units(CHUNKS - 2, 1, CHUNKS // 2 - 1)

            def prologue_chunk(layer):
                p = 2 * layer + 1
                g = CHUNKS * p
                k_banks, v_banks = PROLOGUE_BANKS[layer]
                for half in range(2):
                    pe.wait_ge(sem(f"ctx_loaded0_{half}"), 16 * (prep_use(p, 0) + 1))
                for m in range(BATCHES):
                    pe.wait_ge(sem("v_batch_done"), BATCHES * g + m + 1)
                    v_batch(p, 0, m, v_banks[m])
                for n in range(UPC):
                    pe.wait_ge(sem("k_rest_done"), UPC * g + n + 1)
                    k_unit(p, 0, 0, n, k_banks[n % 2])

            prologue_chunk(0)
            first_stack_units(CHUNKS - 1, 0, CHUNKS // 2)

            def attention(layer):
                base = layer * HEADS

                def max_unit(h, par, a_, loads=None):
                    n = (base + h) * UNITS + a_
                    if a_ % UPC == 0:
                        pe.wait_ge(sem(f"k_loaded{par}_{a_ // UPC}"),
                                   48 * (layer * (HEADS // 2) + loads + (1 if par else 0)))
                    max_matmul(n, a_, h, kstack[0:STACK, par, a_ * UNIT:(a_ + 1) * UNIT])

                def max_row(h, par):
                    pe.wait_ge(sem("negmax_split"), base + h + 1)
                    tr(x_bank[96:99, 0:P // 2].bitcast(BF16), negparts[:, par, :], identb[:, :])\
                        .then_inc(sem("negmax_in_psum"), 1)

                def prep_beside(p, c, j):
                    g = CHUNKS * p + c
                    for at, (kind, n, beside) in enumerate(PREP):
                        if beside != j:
                            continue
                        if kind == "K" and n % 2 == 0:
                            pe.wait_ge(sem(f"ctx_loaded0_{n // 2}"), 16 * (prep_use(p, c) + 1))
                        if at == 0:
                            pe.wait_ge(sem("v_batch_done"), VBATCH_AHEAD + BATCHES * g)
                        elif PREP[at - 1][0] == "K":
                            pe.wait_ge(sem("k_rest_done"), KREST_AHEAD + UPC * g + PREP[at - 1][1] + 1)
                        else:
                            pe.wait_ge(sem("v_batch_done"), VBATCH_AHEAD + BATCHES * g + PREP[at - 1][1] + 1)
                        if kind == "K":
                            k_unit(p, c, 0, n, x_bank)
                        else:
                            v_batch(p, 0, n, x_bank)

                def scores(h, par, j):
                    if j == 0:
                        pe.wait_ge(sem("qstack_max_ready"), base + h + 1)
                    for t in range(GT):
                        key = (j * GT + t) * P
                        ins = mm(s_slots[j % 2][:, t * P:(t + 1) * P], kstack[0:SROWS, par, key:key + P],
                                 qstack[0:SROWS, bass.ds(h, 1), :], start=True, stop=True)
                    ins.then_inc(sem("scores_done"), 1)

                def values(h, par, j, loads):
                    pe.wait_ge(sem("exp_done"), (base + h) * GROUPS + j + 1)
                    if j == 0:
                        pe.wait_ge(sem("o_copied"), base + h + 1)
                        pe.wait_ge(sem(f"v_loaded{par}"), 16 * (layer * (HEADS // 2) + loads + 1))
                        pe.wait_ge(sem("vbuf_padded"), layer + 1)
                    for t in range(GT):
                        tile, g = j * GT + t, (j * GT + t) % 4
                        ins = mm(o_bank[32 * g:32 * g + 32, 0:P], vcols(par, tile),
                                 probs[:, j % 2, t * P:(t + 1) * P], start=(tile < 4), stop=(tile >= TILES - 4))
                    if j == GROUPS - 1:
                        ins.then_inc(sem("head_done"), 1)

                pe.wait_ge(sem("k_rest_done"), KREST_AHEAD + UPC * (CHUNKS * (2 * layer + 1) + 1))
                pe.wait_ge(sem("v_batch_done"), VBATCH_AHEAD + BATCHES * (CHUNKS * (2 * layer + 1) + 1))
                pe.wait_ge(sem("q_stacked"), 96 * (layer + 1))
                if layer == 1:
                    for a_ in range(UNITS):
                        max_unit(0, 0, a_, 0)
                for a_ in range(MAX_AHEAD):
                    max_unit(1, 1, a_, 0)
                max_row(0, 0)
                pe.wait_ge(sem("ones_loaded"), 32 * (layer + 1))
                scores(0, 0, 0)

                def pair(i, last, p, chunks):
                    for par in range(2):
                        h = 2 * i + par
                        end = last and par == 1
                        for j in range(GROUPS):
                            if j == GROUPS - 2 and not end:
                                if chunks[par] is not None:
                                    pe.wait_ge(sem("v_batch_done"),
                                               VBATCH_AHEAD + BATCHES * (CHUNKS * p + chunks[par]) + V_BEFORE_MAX)
                                max_row(h + 1, 1 - par)
                            if j < GROUPS - 1:
                                scores(h, par, j + 1)
                            elif not end:
                                scores(h + 1, 1 - par, 0)
                            for q in (2 * j, 2 * j + 1):
                                a_ = q + MAX_AHEAD
                                if q % 2:
                                    if chunks[par] is not None:
                                        prep_beside(p, chunks[par], j)
                                    values(h, par, j, i)
                                if a_ < UNITS and not end:
                                    max_unit(h + 1, 1 - par, a_, i + par)
                                elif a_ >= UNITS and not last:
                                    max_unit(h + 2, par, a_ - UNITS, i + 1)

                halves(pe, layer, pair)

                for g in range(DC):
                    for hh in range(8):
                        h = 8 * g + hh
                        pe.wait_ge(sem("o_copied"), 1 + base + h + 1)
                        lo = P - HD - HD * hh
                        mm(bank[g][:, 0:P], numsel[:, lo:lo + P], o_heads[:, h, :], start=(hh == 0), stop=(hh == 7))
                    for hh in range(8):
                        lo = P - HD - HD * hh
                        ins = mm(bank[2 + g][:, 0:P], densel[:, lo:lo + P], o_heads[:, 8 * g + hh, :],
                                 start=(hh == 0), stop=(hh == 7))
                    ins.then_inc(sem("o_gathered"), 1)
                pe.wait_ge(sem("attnT_ready"), layer + 1)
                pe.wait_ge(sem("mid_weights_loaded"), 16 * 11)
                for g in range(DC):
                    ins = mm(bank[6][:, 0:D], attnT[:, g, :], wo[:, layer, g, :], start=(g == 0), stop=(g == DC - 1))
                ins.then_inc(sem("block_out"), 1)

            def normed(k, b):
                pe.wait_ge(sem("xhat_ready"), k + 1 if k < 3 else k)
                transpose_xhat(k, xhat, 0, b)

            pe.wait_ge(sem("identb_ready"), 1)
            attention(0)

            normed(1, 0)
            pe.wait_ge(sem("lin_weights_loaded"), 32 * (GH // 2))
            pe.wait_ge(sem("xhatT_ready"), 2)
            for m in range(2):
                for f in range(8):
                    for c in range(DC):
                        ins = mm(bank[1 + 2 * m + f // 4][:, (f % 4) * P:(f % 4 + 1) * P],
                                 lin_w[:, c, 1024 * m + f * P:1024 * m + (f + 1) * P], xhatT[:, 1, c, :],
                                 start=(c == 0), stop=(c == DC - 1))
                    if f % 4 == 3:
                        ins.then_inc(sem("lin_qk_in_psum"), 1)
            for f in range(2):
                for c in range(DC):
                    ins = mm(bank[5 + f], xhatT[:, 1, c, :], lin_w[:, c, 2048 + 512 * f:2048 + 512 * (f + 1)],
                             start=(c == 0), stop=(c == DC - 1))
                ins.then_inc(sem("lin_v_in_psum"), 1)
            pe.wait_ge(sem("lin_qk_ready"), 4)
            for h in range(LH):
                r, f = 64 * (h % 2), h // 2
                b = 1 + 2 * (h % 2) + f // 4
                ins = mm(bank[b][:, (f % 4) * P:(f % 4 + 1) * P], link[r:r + 64, f, :], linq[r:r + 64, f, :],
                         start=True, stop=True)
                if h in (LH // 2 - 1, LH - 1):
                    ins.then_inc(sem("lin_scores_in_psum"), 1)
            pe.wait_ge(sem("lin_aT_ready"), 4)
            for h in range(LH):
                ins = mm(bank[0][0:LH, 0:P], onecol[:, 15 - h:31 - h], lin_aT[:, h, :],
                         start=(h == 0), stop=(h == LH - 1))
            ins.then_inc(sem("lin_sums_in_psum"), 1)
            pe.wait_ge(sem("lin_v_ready"), 2)
            for h in range(LH):
                r, f = 64 * (h % 2), h // 2
                ins = mm(bank[5 + f // 4][r:r + 64, (f % 4) * P:(f % 4 + 1) * P],
                         linv[:, h * LD:(h + 1) * LD], lin_aT[:, h, :], start=True, stop=True)
            ins.then_inc(sem("lin_av_in_psum"), 1)
            pe.wait_ge(sem("lin_rsum_ready"), 1)
            for f in range(8):
                ins = mm(bank[1 + f // 4][:, (f % 4) * P:(f % 4 + 1) * P], spread[0:LH, f * P:(f + 1) * P],
                         lin_rd, start=True, stop=True)
            ins.then_inc(sem("lin_rsum_spread"), 1)
            pe.wait_ge(sem("lin_oT_ready"), 2)
            for f in range(8):
                ins = mm(bank[7][:, 0:D], lin_oT[:, f, :], lin_wo[:, f, :], start=(f == 0), stop=(f == 7))
            ins.then_inc(sem("block_out"), 1)

            normed(2, 0)
            pe.wait_ge(sem("xhatT_ready"), 3)
            pe.wait_ge(sem("w1_loaded"), 16)

            def expert_in0(e):
                b = 1 + e % 2
                if e >= 2:
                    pe.wait_ge(sem("h0_ready"), e - 1)
                for f in range(4):
                    for c in range(DC):
                        at = e * F0 + f * P
                        ins = mm(bank[b][:, f * P:(f + 1) * P], w1[:, c, at:at + P], xhatT[:, 0, c, :],
                                 start=(c == 0), stop=(c == DC - 1))
                ins.then_inc(sem("h0_in_psum"), 1)

            def gate_logits(w, n, b, par):
                for c in range(DC):
                    ins = mm(bank[b][:, 0:n], xhatT[:, par, c, :], w[:, c, :], start=(c == 0), stop=(c == DC - 1))
                ins.then_inc(sem("logits_in_psum"), 1)

            expert_in0(0)
            expert_in0(1)
            pe.wait_ge(sem("rn_ready"), 1)
            transpose_xhat(3, rn, 0, 3)
            pe.wait_ge(sem("xhatT_ready"), 4)
            gate_logits(gate0, E0, 0, 1)
            pe.wait_ge(sem("w2_loaded"), 32)
            for e in range(E0):
                if e >= 1 and e + 1 < E0:
                    expert_in0(e + 1)
                b = 4 + e % 4
                if e >= 4:
                    pe.wait_ge(sem("expert_mixed"), e - 3)
                pe.wait_ge(sem("h0_ready"), e + 1)
                for f in range(4):
                    ins = mm(bank[b][:, 0:D], h0T[:, 4 * e + f, :], w2[:, 4 * e + f, :], start=(f == 0), stop=(f == 3))
                ins.then_inc(sem("expert_in_psum"), 1)

            normed(4, 0)
            pe.wait_ge(sem("xhatT_ready"), 5)
            project_q(1, 0, 1)
            pe.wait_ge(sem("expert_mixed"), E0)
            prologue_chunk(1)
            attention(1)

            normed(5, 0)
            pe.wait_ge(sem("lin2_weights_loaded"), 32)
            pe.wait_ge(sem("xhatT_ready"), 6)
            for g in range(DC):
                for c in range(DC):
                    ins = mm(bank[1][:, g * P:(g + 1) * P], w_q2[:, c, g * P:(g + 1) * P], xhatT[:, 1, c, :],
                             start=(c == 0), stop=(c == DC - 1))
            ins.then_inc(sem("q2_in_psum"), 1)
            for s, (b, lo, n) in enumerate(((2, 0, 512), (3, 512, 256))):
                for c in range(DC):
                    ins = mm(bank[b][:, 0:n], xhatT[:, 1, c, :], w_kvu[:, c, lo:lo + n],
                             start=(c == 0), stop=(c == DC - 1))
                ins.then_inc(sem("kvu_in_psum"), 1)
            pe.wait_ge(sem("kv2_ready"), 2)
            for g in range(DC):
                ins = mm(bank[4 + g][:, 0:P], kvu[:, g * P:(g + 1) * P], kvu[:, D + g * P:D + (g + 1) * P],
                         start=True, stop=True)
            ins.then_inc(sem("kv_outer_in_psum"), 1)
            pe.wait_ge(sem("q2_ready"), 1)
            pe.wait_ge(sem("kvm_ready"), 2)
            for g in range(DC):
                ins = mm(bank[7][:, g * P:(g + 1) * P], q2T[:, g, :], kvm[:, g, :], start=True, stop=True)
            ins.then_inc(sem("o2_in_psum"), 1)
            pe.wait_ge(sem("o2_ready"), 1)
            for c in range(DC):
                ins = tr(bank[0][:, c * P:(c + 1) * P], o2[:, c * P:(c + 1) * P], ident)
            ins.then_inc(sem("o2T_in_psum"), 1)
            pe.wait_ge(sem("o2T_ready"), 1)
            for c in range(DC):
                ins = mm(bank[6][:, 0:D], o2T[:, c, :], w_o2[:, c, :], start=(c == 0), stop=(c == DC - 1))
            ins.then_inc(sem("block_out"), 1)

            normed(6, 0)
            pe.wait_ge(sem("xhatT_ready"), 7)
            gate_logits(gate1, E1 + 1, 7, 0)
            pe.wait_ge(sem("experts_loaded"), 48 * (GH // 2))

            def experts_in(r):
                if r >= 2:
                    pe.wait_ge(sem("h1_ready"), r - 1)
                for s in range(2):
                    for f in range(4):
                        for c in range(DC):
                            at = (4 * r + f) * P
                            ins = mm(bank[1 + 2 * (r % 2) + s][:, f * P:(f + 1) * P], we_in[:, c, s, at:at + P],
                                     xhatT[:, 0, c, :], start=(c == 0), stop=(c == DC - 1))
                    ins.then_inc(sem("gate_in_psum" if s == 0 else "up_in_psum"), 1)

            def experts_out(r):
                pe.wait_ge(sem("h1_ready"), r + 1)
                for e in range(4 * r, 4 * r + 4):
                    b = (0, 5, 6)[e % 3]
                    if e < 16:
                        if e >= 3:
                            pe.wait_ge(sem("expert_mixed"), E0 + e - 2)
                        mm(bank[b][:, 0:D], h1T[:, e, :], we_out[:, e, :], start=True, stop=True)\
                            .then_inc(sem("expert_in_psum"), 1)
                    else:
                        if e == 16:
                            pe.wait_ge(sem("sigmoid_ready"), 1)
                        ins = mm(bank[7][:, 0:D], h1T[:, e, :], we_out[:, e, :], start=(e == 16), stop=(e == 19))
                if r == 4:
                    ins.then_inc(sem("shared_in_psum"), 1)
            experts_in(0)
            experts_in(1)
            for r in range(5):
                experts_out(r)
                if r + 2 < 5:
                    experts_in(r + 2)

        @block.scalar
        def _(act):
            def std(k):
                act.wait_ge(sem("var_ready"), k + 1)
                act.activation(small[:, 10:11], small[:, 8:9], ACT.Sqrt).then_inc(sem("std_ready"), 1)

            std(0)
            act.wait_ge(sem("bk_zeroed"), 1)
            act.wait_ge(sem("kv_weights_loaded"), 64)

            for buf in range(2):
                act.sem_inc(sem(f"k_stored{buf}"), STORED_K)

            def first_part(p, g, use, buf, n, b):
                if n == 0:
                    act.wait_ge(sem(f"k_stored{buf}"), STORED_K * (use + 1))
                act.wait_ge(sem("k_in_psum"), UPC * g + n + 1)
                act.activation(k_parts[buf][:, 0, n * UNIT:(n + 1) * UNIT], b[:, 0:UNIT],
                               ACT.Identity, bias=bk[:, p:p + 1]).then_inc(sem("k1_done"), 1)

            def first_prep(c, use, buf):
                for n in range(UPC):
                    first_part(0, c, use, buf, n, bank[n % 2])

            with act.Fori(0, CHUNKS // 2) as i:
                first_prep(2 * i, i, 0)
                first_prep(2 * i + 1, i, 1)
            first_prep(CHUNKS - 1, CHUNKS // 2, 0)

            def prologue_chunk(layer):
                p = 2 * layer + 1
                for n in range(UPC):
                    first_part(p, CHUNKS * p, prep_use(p, 0), 0, n, PROLOGUE_BANKS[layer][0][n % 2])

            def attention(layer):
                base = layer * HEADS

                def exp_group(h, j):
                    act.wait_ge(sem("scores_done"), (base + h) * GROUPS + j + 1)
                    act.activation(probs[:, j % 2, :], s_slots[j % 2][:, 0:GT * P], ACT.Exp)\
                        .then_inc(sem("exp_done"), 1)

                def put_max(h, par):
                    act.wait_ge(sem("negmax_in_psum"), base + h + 1)
                    act.activation(qstack[96:99, bass.ds(h, 1), :],
                                   x_bank[96:99, 0:P // 2].bitcast(BF16), ACT.Copy)\
                        .then_inc(sem("qstack_max_ready"), 1)

                def copy_out(h, par):
                    act.wait_ge(sem("head_done"), base + h + 1)
                    ins = act.activation(o_heads[:, bass.ds(h, 1), :], o_bank[:, 0:P], ACT.Copy)
                    ins.then_inc(sem("o_copied"), 1)

                if layer == 0:
                    act.sem_inc(sem("o_copied"), 1)
                prologue_chunk(layer)
                act.wait_ge(sem("q_stacked"), 96 * (layer + 1))
                put_max(0, 0)

                def pair(i, last, p, chunks):
                    for par in range(2):
                        h = 2 * i + par
                        for j in range(1, GROUPS):
                            exp_group(h, j)
                            if j - 1 in K_AT and chunks[par] is not None:
                                c = chunks[par]
                                first_part(p, CHUNKS * p + c, prep_use(p, c), 0, K_AT[j - 1], x_bank)
                            if j == GROUPS - 2 and not (last and par == 1):
                                put_max(h + 1, 1 - par)
                        if not (last and par == 1):
                            exp_group(h + 1, 0)
                        copy_out(h, par)

                exp_group(0, 0)
                halves(act, layer, pair)

            attention(0)

            std(1)
            for f in range(2):
                act.wait_ge(sem("lin_v_in_psum"), f + 1)
                act.activation(linv[:, 512 * f:512 * (f + 1)], bank[5 + f], ACT.Copy).then_inc(sem("lin_v_ready"), 1)
            for f in range(2):
                act.wait_ge(sem("lin_rsum_spread"), 1)
                act.activation(linq[:, 4 * f:4 * f + 4, :].rearrange("p f n -> p (f n)"), bank[1 + f], ACT.Copy)\
                    .then_inc(sem("lin_spread_ready"), 1)
            std(2)
            std(3)
            act.wait_ge(sem("gate_neg_ready"), 1)
            act.activation(small[:, 40:40 + E0], bank[0][:, 0:E0], ACT.Exp, bias=small[:, 12:13],
                           accum_out=small[:, 13:14]).then_inc(sem("gate_exp_ready"), 1)
            for e in range(E0):
                act.wait_ge(sem("h0_in_psum"), e + 1)
                act.activation(h0T[:, 4 * e:4 * e + 4, :], bank[1 + e % 2].rearrange("p (f n) -> p f n", f=4),
                               ACT.Gelu).then_inc(sem("h0_ready"), 1)
            std(4)
            attention(1)
            std(5)
            act.wait_ge(sem("kvu_in_psum"), 2)
            act.activation(kvu[:, 2 * D:3 * D], bank[3][:, 0:D], ACT.Silu).then_inc(sem("u2_ready"), 1)
            act.wait_ge(sem("o2_sumsq_ready"), 1)
            act.activation(small[:, 64:80], small[:, 40:56], ACT.Sqrt).then_inc(sem("o2_norm_ready"), 1)
            std(6)
            act.wait_ge(sem("gate_neg_ready"), 2)
            act.activation(small[:, 40:40 + E1], bank[7][:, 0:E1], ACT.Exp, bias=small[:, 12:13],
                           accum_out=small[:, 13:14]).then_inc(sem("gate_exp_ready"), 1)
            act.activation(small[:, 14:15], bank[7][:, E1:E1 + 1], ACT.Sigmoid).then_inc(sem("sigmoid_ready"), 1)
            for r in range(5):
                act.wait_ge(sem("gate_in_psum"), r + 1)
                if r >= 2:
                    act.wait_ge(sem("h1_ready"), r - 1)
                act.activation(silu_g[:, r % 2, :], bank[1 + 2 * (r % 2)], ACT.Silu).then_inc(sem("silu_done"), 1)

        @block.gpsimd
        def _(pool):
            def cast(dst, src):
                return pool.tensor_tensor(dst, src, unity[:, :].broadcast_to(list(src.shape)), ALU.mult)

            pool.memset(unity[:, :], 1.0).then_inc(sem("unity_ready"), 1)
            pool.wait_ge(sem("unity_ready"), 1)

            def split_unit(g, buf, n):
                cols = slice(n * UNIT, (n + 1) * UNIT)
                rest = k_rest[:, n % REST_SLOTS, :]
                pool.wait_ge(sem("k_rest_done"), KREST_AHEAD + UPC * g + n + 1)
                cast(k_parts[buf][:, 1, cols], rest).then_inc(sem("k2_done"), 1)
                pool.wait_ge(sem("k2_done"), UPC * g + n + 1)
                pool.tensor_tensor(k_parts[buf][:, 2, cols], rest, k_parts[buf][:, 1, cols], ALU.subtract)\
                    .then_inc(sem("k_unit_split"), 1)

            pool.sem_inc(sem("k_unit_split"), SPLIT_AHEAD)
            with pool.Fori(0, CHUNKS // 2) as i:
                for buf in range(2):
                    for n in range(UPC):
                        split_unit(2 * i + buf, buf, n)
            for n in range(UPC):
                split_unit(CHUNKS - 1, 0, n)

            def split_max(h, par, layer):
                n = layer * HEADS + h
                pool.wait_ge(sem("negmax_ready"), n + 1)
                cast(negparts[:, par, 0:1], negmax[:, par]).then_inc(sem("split_step"), 1)
                pool.wait_ge(sem("split_step"), 3 * n + 1)
                pool.tensor_tensor(negrest[:, par], negmax[:, par], negparts[:, par, 0:1], ALU.subtract)\
                    .then_inc(sem("split_step"), 1)
                pool.wait_ge(sem("split_step"), 3 * n + 2)
                cast(negparts[:, par, 1:2], negrest[:, par]).then_inc(sem("split_step"), 1)
                pool.wait_ge(sem("split_step"), 3 * n + 3)
                pool.tensor_tensor(negparts[:, par, 2:3], negrest[:, par], negparts[:, par, 1:2], ALU.subtract)\
                    .then_inc(sem("negmax_split"), 1)

            for layer in range(2):
                for n in range(UPC):
                    split_unit(CHUNKS * (2 * layer + 1), 0, n)
                split_max(0, 0, layer)

                def pair(i, last, p, chunks):
                    for par in range(2):
                        if chunks[par] is not None:
                            for n in range(UPC):
                                split_unit(CHUNKS * p + chunks[par], 0, n)
                        if not (last and par == 1):
                            split_max(2 * i + par + 1, 1 - par, layer)

                halves(pool, layer, pair)

        @block.vector
        def _(dve):
            steps = [0]

            def after(ins):
                ins.then_inc(sem("dve_step"), 1)
                steps[0] += 1
                dve.wait_ge(sem("dve_step"), steps[0])

            def stats(k, src):
                after(dve.bn_stats(small[:, 0:6], src))
                after(dve.bn_aggr(small[:, 6:8], small[:, 0:6]))
                dve.tensor_scalar(small[:, 8:9], small[:, 7:8], LN_EPS, None, ALU.add)\
                    .then_inc(sem("var_ready"), 1)
                dve.wait_ge(sem("std_ready"), k + 1)
                after(dve.reciprocal(small[:, 11:12], small[:, 10:11]))

            def layernorm(k, src):
                stats(k, src)
                dve.tensor_scalar(xhat[:, :], src, small[:, 6:7], small[:, 11:12], ALU.subtract, ALU.mult)\
                    .then_inc(sem("xhat_ready"), 1)

            def copy_xhatT(k, par, b):
                dve.wait_ge(sem("xhatT_in_psum"), k + 1)
                dve.tensor_copy(xhatT[:, par].rearrange("p c n -> p (c n)"), bank[b][:, 0:D])\
                    .then_inc(sem("xhatT_ready"), 1)

            def split_q(layer, b):
                dve.wait_ge(sem("q_in_psum"), layer + 1)
                for g in range(DC):
                    src = bank[b][:, g * P:(g + 1) * P]
                    if layer == 0:
                        ins = dve.tensor_scalar(qf[:, g, :], src, bq[:, g:g + 1], HD ** -0.5, ALU.add, ALU.mult)
                    else:
                        ins = dve.tensor_scalar(qf[:, g, :], src, HD ** -0.5, None, ALU.mult)
                after(ins)
                if layer == 1:
                    dve.wait_ge(sem("q_stored"), 16 * DC)
                after(dve.tensor_copy(qp[:, :, 0, :], qf[:, :, :]))
                after(dve.tensor_tensor(qr[:, :, :], qf[:, :, :], qp[:, :, 0, :], ALU.subtract))
                after(dve.tensor_copy(qp[:, :, 1, :], qr[:, :, :]))
                dve.tensor_tensor(qp[:, :, 2, :], qr[:, :, :], qp[:, :, 1, :], ALU.subtract)\
                    .then_inc(sem("q_split"), 1)

            dve.memset(bk[:, DC:2 * DC], 0.0).then_inc(sem("bk_zeroed"), 1)
            after(dve.memset(bv[:, D:2 * D], 0.0))
            for buf in range(2):
                after(dve.memset(v_ring[buf][:, :, :, HD:VW].rearrange("p h t c -> p (h t c)"), 1.0))
            dve.memset(vbuf[:, :, TILES * VW:], 0.0).then_inc(sem("vbuf_padded"), 1)
            dve.wait_ge(sem("x_loaded"), 16)
            layernorm(0, xs[:, 0, :])

            dve.sem_inc(sem("unit_reduced"), REDUCED_AHEAD)
            dve.sem_inc(sem("k_rest_done"), KREST_AHEAD)
            dve.sem_inc(sem("v_batch_done"), VBATCH_AHEAD)
            for buf in range(2):
                dve.sem_inc(sem(f"v_stored{buf}"), STORED_V)
            dve.wait_ge(sem("kv_weights_loaded"), 64)

            def k_remainder(p, g, buf, n, b):
                dve.wait_ge(sem("k_unit_split"), UPC * g + n + 1)
                dve.wait_ge(sem("k1_done"), UPC * g + n + 1)
                dve.scalar_tensor_tensor(k_rest[:, n % REST_SLOTS, :], b[:, 0:UNIT], bk[:, p:p + 1],
                                         k_parts[buf][:, 0, n * UNIT:(n + 1) * UNIT],
                                         ALU.add, ALU.subtract).then_inc(sem("k_rest_done"), 1)

            def v_to_ring(p, g, use, buf, m, b):
                if m == 0:
                    dve.wait_ge(sem(f"v_stored{buf}"), STORED_V * (use + 1))
                tiles = batch_tiles(m)
                nt = len(tiles)
                dve.wait_ge(sem("v_in_psum"), BATCHES * g + m + 1)
                dve.tensor_tensor(
                    v_ring[buf][:, :, tiles[0]:tiles[0] + nt, 0:HD].rearrange("p h t d -> p t h d"),
                    b[:, 0:nt * P].rearrange("p (t h d) -> p t h d", h=GH, d=HD),
                    bv[:, p * P:(p + 1) * P].rearrange("p (a h d) -> p a h d", a=1, d=HD)
                    .broadcast_to([P, nt, GH, HD]), ALU.add).then_inc(sem("v_batch_done"), 1)

            def reduce_scores(n, par, u, b):
                dve.wait_ge(sem("unit_in_psum"), n + 1)
                dve.tensor_reduce(maxima[:, par, bass.ds(u, 1)], b[:, 0:UNIT], AX.X, ALU.max)\
                    .then_inc(sem("unit_reduced"), 1)

            def reduce_first_stack(c):
                for n in range(UPC):
                    reduce_scores(UPC * c + n, 0, UPC * c + n, a_banks[n % 2])

            def first_prep(c, use, buf, stack=True):
                for kind, n in FIRST_PREP:
                    if kind == "K":
                        k_remainder(0, c, buf, n, bank[n % 2])
                    else:
                        if stack and n == BATCHES - 1:
                            reduce_first_stack(c - 2)
                        v_to_ring(0, c, use, buf, n, bank[2 + n])

            first_prep(0, 0, 0, stack=False)
            dve.wait_ge(sem("ident_loaded"), 16)
            dve.tensor_copy(identb[:, :], ident).then_inc(sem("identb_ready"), 1)
            copy_xhatT(0, 0, 6)
            dve.wait_ge(sem("q_weights_loaded"), 32)
            split_q(0, 7)
            first_prep(1, 0, 1, stack=False)
            with dve.Fori(1, CHUNKS // 2) as i:
                first_prep(2 * i, i, 0)
                first_prep(2 * i + 1, i, 1)
            first_prep(CHUNKS - 1, CHUNKS // 2, 0)
            reduce_first_stack(CHUNKS - 2)

            def prologue_chunk(layer):
                p = 2 * layer + 1
                k_banks, v_banks = PROLOGUE_BANKS[layer]
                for m in range(BATCHES):
                    v_to_ring(p, CHUNKS * p, prep_use(p, 0), 0, m, v_banks[m])
                for n in range(UPC):
                    k_remainder(p, CHUNKS * p, 0, n, k_banks[n % 2])

            def attention(layer):
                base = layer * HEADS

                def reduce_unit(h, par, u):
                    n = (base + h) * UNITS + u
                    reduce_scores(n, par, u, a_banks[u % 2])
                    if u == UNITS - 1:
                        dve.wait_ge(sem("unit_reduced"), REDUCED_AHEAD + n + 1)
                        dve.tensor_reduce(negmax[:, par], maxima[:, par], AX.X, ALU.max, negate=True)\
                            .then_inc(sem("negmax_ready"), 1)

                prologue_chunk(layer)
                for u in range(UNITS - UPC if layer == 0 else 0, UNITS):
                    reduce_unit(0, 0, u)
                for u in range(MAX_AHEAD):
                    reduce_unit(1, 1, u)

                def pair(i, last, p, chunks):
                    for par in range(2):
                        h = 2 * i + par
                        for j in range(GROUPS):
                            for q in (2 * j, 2 * j + 1):
                                u = q + MAX_AHEAD
                                if u < UNITS and not (last and par == 1):
                                    reduce_unit(h + 1, 1 - par, u)
                                elif u >= UNITS and not last:
                                    reduce_unit(h + 2, par, u - UNITS)
                                if chunks[par] is None:
                                    continue
                                c = chunks[par]
                                if q % 2 and j in K_AT:
                                    k_remainder(p, CHUNKS * p + c, 0, K_AT[j], x_bank)
                                if q % 2 == 0 and j in V_AT:
                                    v_to_ring(p, CHUNKS * p + c, prep_use(p, c), 0, V_AT[j], x_bank)

                halves(dve, layer, pair)

                dve.wait_ge(sem("o_gathered"), 2 * layer + 2)
                after(dve.reciprocal(rden[:, :, :], psum[:, 2:4, 0:P]))
                dve.tensor_tensor(attnT[:, :, :], psum[:, 0:2, 0:P], rden[:, :, :], ALU.mult)\
                    .then_inc(sem("attnT_ready"), 1)

            def add_block(k, b, res, dst):
                dve.wait_ge(sem("block_out"), k)
                after(dve.tensor_tensor(dst, bank[b][:, 0:D], res, ALU.add))

            attention(0)
            dve.wait_ge(sem("mid_weights_loaded"), 16 * 11)
            after(dve.tensor_tensor(xb[:, 0, :], xs[:, 0, :], bias_rows[:, 0, :], ALU.add))
            add_block(1, 6, xb[:, 0, :], xs[:, 1, :])

            layernorm(1, xs[:, 1, :])
            dve.tensor_tensor(xb[:, 1, :], xs[:, 1, :], bias_rows[:, 1, :], ALU.add).then_inc(sem("xb_ready"), 1)
            copy_xhatT(1, 1, 0)
            for n in range(4):
                dve.wait_ge(sem("lin_qk_in_psum"), n + 1)
                dst = (linq, link)[n // 2][:, 4 * (n % 2):4 * (n % 2) + 4, :]
                dve.tensor_scalar(dst, bank[1 + n].rearrange("p (f n) -> p f n", f=4), 0.0, LEPS, ALU.max, ALU.add)\
                    .then_inc(sem("lin_qk_ready"), 1)
            by_parity = lin_aT.rearrange("p (f r) n -> p r f n", r=2)
            for f in range(2):
                dve.wait_ge(sem("lin_scores_in_psum"), f + 1)
                for r in range(2):
                    dve.tensor_tensor(by_parity[:, r, 4 * f:4 * f + 4, :],
                                      bank[1 + 2 * r + f].rearrange("p (f n) -> p f n", f=4),
                                      causal.rearrange("p (a n) -> p a n", a=1).broadcast_to([P, 4, P]), ALU.mult)\
                        .then_inc(sem("lin_aT_ready"), 1)
            dve.wait_ge(sem("lin_sums_in_psum"), 1)
            dve.reciprocal(lin_rd, bank[0][0:LH, 0:P]).then_inc(sem("lin_rsum_ready"), 1)
            dve.wait_ge(sem("lin_av_in_psum"), 1)
            for f in range(2):
                dve.wait_ge(sem("lin_spread_ready"), f + 1)
                dve.tensor_tensor(lin_oT[:, 4 * f:4 * f + 4, :], bank[5 + f].rearrange("p (f n) -> p f n", f=4),
                                  linq[:, 4 * f:4 * f + 4, :], ALU.mult).then_inc(sem("lin_oT_ready"), 1)
            dve.wait_ge(sem("xb_ready"), 1)
            add_block(2, 7, xb[:, 1, :], xs[:, 2, :])

            def mixture_weights(k, b, n, rev, normalise):
                g = lambda j: gates[:, j, 0:n]
                one = lambda j: small[:, j:j + 1]
                dve.wait_ge(sem("logits_in_psum"), k + 1)
                dve.tensor_reduce(one(12), bank[b][:, 0:n], AX.X, ALU.max, negate=True)\
                    .then_inc(sem("gate_neg_ready"), 1)
                dve.wait_ge(sem("gate_exp_ready"), k + 1)
                after(dve.reciprocal(one(15), one(13)))
                after(dve.tensor_scalar(g(0), small[:, 40:40 + n], one(15), None, ALU.mult))
                for r in range(2):
                    p_, pick, left = (0, 1, 2) if r == 0 else (2, 3, None)
                    after(dve.tensor_reduce(one(16 + 2 * r), g(p_), AX.X, ALU.max))
                    after(dve.scalar_tensor_tensor(g(4), g(p_), one(16 + 2 * r), rev, ALU.is_equal, ALU.mult))
                    after(dve.tensor_reduce(one(17 + 2 * r), g(4), AX.X, ALU.max))
                    after(dve.tensor_scalar(g(pick), g(4), one(17 + 2 * r), None, ALU.is_equal))
                    if r == 0:
                        after(dve.scalar_tensor_tensor(g(left), g(pick), -2.0, g(p_), ALU.mult, ALU.add))
                after(dve.tensor_tensor(g(5), g(1), g(3), ALU.add))
                after(dve.tensor_tensor(g(6), g(5), g(0), ALU.mult))
                if normalise:
                    after(dve.tensor_tensor(one(20), one(16), one(18), ALU.add))
                    after(dve.reciprocal(one(21), one(20)))
                    after(dve.tensor_scalar(g(6), g(6), one(21), None, ALU.mult))

            def mix(n, e, b, res, dst):
                dve.wait_ge(sem("expert_in_psum"), n + 1)
                dve.scalar_tensor_tensor(dst, bank[b][:, 0:D], gates[:, 6, e:e + 1], res, ALU.mult, ALU.add)\
                    .then_inc(sem("expert_mixed"), 1)
                dve.wait_ge(sem("expert_mixed"), n + 1)

            layernorm(2, xs[:, 2, :])
            copy_xhatT(2, 0, 0)
            dve.wait_ge(sem("xhat_ready"), 3)
            stats(3, xhat[:, :])
            after(dve.tensor_scalar(rn[:, :], xhat[:, :], small[:, 6:7], small[:, 11:12], ALU.subtract, ALU.mult))
            after(dve.tensor_tensor(rn[:, :], rn[:, :], bias_rows[:, 2, :], ALU.mult))
            dve.tensor_tensor(rn[:, :], rn[:, :], bias_rows[:, 3, :], ALU.add).then_inc(sem("rn_ready"), 1)
            copy_xhatT(3, 1, 3)
            mixture_weights(0, 0, E0, const("rev0"), False)
            for e in range(E0):
                mix(e, e, 4 + e % 4, xs[:, 2, :] if e == 0 else acc[:, (e - 1) % 2, :],
                    xs[:, 3, :] if e == E0 - 1 else acc[:, e % 2, :])

            dve.memset(vbuf[:, :, TILES * VW:], 0.0).then_inc(sem("vbuf_padded"), 1)
            after(dve.memset(v_ring[0][:, :, :, HD:VW].rearrange("p h t c -> p (h t c)"), 1.0))
            layernorm(4, xs[:, 3, :])
            copy_xhatT(4, 0, 0)
            split_q(1, 1)
            attention(1)
            add_block(3, 6, xs[:, 3, :], xs[:, 4, :])

            layernorm(5, xs[:, 4, :])
            copy_xhatT(5, 1, 0)
            dve.wait_ge(sem("kvu_in_psum"), 1)
            dve.tensor_scalar(kvu[:, 0:D], bank[2][:, 0:D], 0.0, HD ** -0.5, ALU.max, ALU.mult)\
                .then_inc(sem("kv2_ready"), 1)
            dve.tensor_copy(kvu[:, D:2 * D], bank[2][:, D:2 * D]).then_inc(sem("kv2_ready"), 1)
            dve.wait_ge(sem("q2_in_psum"), 1)
            dve.tensor_scalar(q2T, bank[1][:, 0:D].rearrange("p (g n) -> p g n", g=DC), 0.0, HD ** -0.5,
                              ALU.max, ALU.mult).then_inc(sem("q2_ready"), 1)
            dve.wait_ge(sem("kv_outer_in_psum"), 1)
            for g in range(DC):
                dve.tensor_tensor(kvm[:, g, :], bank[4 + g][:, 0:P], blockdiag, ALU.mult).then_inc(sem("kvm_ready"), 1)
            dve.wait_ge(sem("o2_in_psum"), 1)
            raw = acc[:, 2, :]
            after(dve.tensor_copy(raw, bank[7][:, 0:D]))
            after(dve.scalar_tensor_tensor(o2sq, raw, 1.0 / HD, raw, ALU.mult, ALU.mult))
            dve.tensor_reduce(small[:, 40:56], o2sq.rearrange("p (h d) -> p h d", d=HD), AX.X, ALU.add)\
                .then_inc(sem("o2_sumsq_ready"), 1)
            dve.wait_ge(sem("o2_norm_ready"), 1)
            after(dve.tensor_scalar(small[:, 64:80], small[:, 64:80], 1e-12, None, ALU.max))
            after(dve.reciprocal(small[:, 80:96], small[:, 64:80]))
            after(dve.tensor_tensor(o2.rearrange("p (h d) -> p h d", d=HD), raw.rearrange("p (h d) -> p h d", d=HD),
                                    small[:, 80:96].rearrange("p (h a) -> p h a", a=1).broadcast_to([P, HEADS, HD]),
                                    ALU.mult))
            dve.wait_ge(sem("u2_ready"), 1)
            dve.tensor_tensor(o2, o2, kvu[:, 2 * D:3 * D], ALU.mult).then_inc(sem("o2_ready"), 1)
            dve.wait_ge(sem("o2T_in_psum"), 1)
            dve.tensor_copy(o2T.rearrange("p c n -> p (c n)"), bank[0][:, 0:D]).then_inc(sem("o2T_ready"), 1)
            add_block(4, 6, xs[:, 4, :], xs[:, 5, :])

            layernorm(6, xs[:, 5, :])
            copy_xhatT(6, 0, 0)
            mixture_weights(1, 7, E1, const("rev1"), True)

            def gated(r):
                dve.wait_ge(sem("silu_done"), r + 1)
                dve.wait_ge(sem("up_in_psum"), r + 1)
                dve.tensor_tensor(h1T[:, 4 * r:4 * r + 4, :], silu_g[:, r % 2, :].rearrange("p (f n) -> p f n", f=4),
                                  bank[2 + 2 * (r % 2)].rearrange("p (f n) -> p f n", f=4), ALU.mult)\
                    .then_inc(sem("h1_ready"), 1)
            gated(0)
            for r in range(4):
                gated(r + 1)
                for e in range(4 * r, 4 * r + 4):
                    mix(E0 + e, e, (0, 5, 6)[e % 3], xs[:, 5, :] if e == 0 else acc[:, (e - 1) % 2, :],
                        acc[:, e % 2, :])
            dve.wait_ge(sem("shared_in_psum"), 1)
            dve.scalar_tensor_tensor(xs[:, 6, :], bank[7][:, 0:D], small[:, 14:15], acc[:, (E1 - 1) % 2, :],
                                     ALU.mult, ALU.add).then_inc(sem("out_ready"), 1)


def kernel(**inputs):
    import concourse.bacc as bacc
    from concourse.bass_utils import run_bass_kernel_spmd

    v = {k: np.asarray(x) for k, x in inputs.items()}
    hid = lambda w: w.transpose(2, 0, 1).reshape(w.shape[2], -1)
    arrays = {
        "x": v["x"][0], "ctxT": np.concatenate([v["ctx_512"][0], v["ctx_512"][0, :CHUNK]]).T,
        "consts": _constants(),
        "ones": np.full((3, KEYS), 0x3F80, np.uint16),
        "wk": np.concatenate([v["L0_xattn_Wk"], v["L1_xattn_Wkv"][:D].T], 1),
        "wv": np.concatenate([v["L0_xattn_Wv"], v["L1_xattn_Wkv"][D:].T], 1),
        "bq": v["L0_xattn_bq"].reshape(DC, P).T, "bk": v["L0_xattn_bk"].reshape(DC, P).T, "bv": v["L0_xattn_bv"], "bo0": v["L0_xattn_bo"],
        "wq0": v["L0_xattn_Wq"], "wq1": v["L1_xattn_Wq"].T, "wo0": v["L0_xattn_Wo"], "wo1": v["L1_xattn_Wo"].T,
        "lin_w": np.concatenate([v["L0_attn_Wq"], v["L0_attn_Wk"], v["L0_attn_Wv"]], 1),
        "lin_wo": v["L0_attn_Wo"], "lin_bo": v["L0_attn_bo"],
        "gamma": v["L0_ffn_ln_gamma"], "beta": v["L0_ffn_ln_beta"], "gate0": v["L0_ffn_gate_w"].T,
        "w1": hid(v["L0_ffn_w1"]), "w2": v["L0_ffn_w2"].transpose(0, 2, 1).reshape(E0 * F0, D),
        "w_q2": v["L1_attn_Wq"].T, "w_o2": v["L1_attn_Wo"].T,
        "w_kvu": np.concatenate([v["L1_attn_Wk"].T, v["L1_attn_Wv"].T, v["L1_attn_Wu"].T], 1),
        "gate1": np.concatenate([v["L1_ffn_Wg"].T, v["L1_ffn_Wsg"].T], 1),
        "we_in": np.stack([np.concatenate([hid(v["L1_ffn_We_gate"]), v["L1_ffn_Ws_gate"].T], 1),
                           np.concatenate([hid(v["L1_ffn_We_up"]), v["L1_ffn_Ws_up"].T], 1)], 1),
        "we_out": np.concatenate([v["L1_ffn_We_down"].transpose(0, 2, 1).reshape(E1 * F1, D),
                                  v["L1_ffn_Ws_down"].T], 0),
    }
    nc = bacc.Bacc("TRN2", target_bir_lowering=False, num_devices=1)
    feed, aps = {}, {}
    for name, x in arrays.items():
        x = np.ascontiguousarray(x)
        feed[f"in_{name}"] = x
        dt = BF16 if name == "ones" else mybir.dt.from_np(x.dtype)
        t = nc.dram_tensor(f"in_{name}", x.shape, mybir.dt.from_np(x.dtype), kind="ExternalInput").ap()
        aps[name] = t.bitcast(BF16) if name == "ones" else t
    out = nc.dram_tensor("out", (P, D), F32, kind="ExternalOutput").ap()
    program(nc, aps, out)
    r = run_bass_kernel_spmd(nc, [feed], core_ids=[0])
    return r.results[0]["out"].reshape(1, P, D)
```

```python
from contextlib import ExitStack

import concourse.bass as bass
import numpy as np
from concourse import mybir

F32 = mybir.dt.float32
BF16 = mybir.dt.bfloat16
ALU = mybir.AluOpType
ACT = mybir.ActivationFunctionType
AX = mybir.AxisListType

P = 128
D = 256
DC = D // P
CD = 128
KEYS = 12544
HEADS = 16
HD = D // HEADS
VW = HD + 1
TILES = KEYS // P
CHUNK = 1792
CHUNKS = KEYS // CHUNK
CT = CHUNK // P
UNIT = 448
UNITS = KEYS // UNIT
UPC = CHUNK // UNIT
GT = 7
GROUPS = TILES // GT
FIRST = CHUNKS + 1
GPC = CT // GT
GH = 8
BATCHES = 4
REST_SLOTS = 2
PREP = (("K", 0, 0), ("K", 1, 2), ("K", 2, 4), ("K", 3, 6), ("V", 0, 8), ("V", 1, 9), ("V", 2, 11), ("V", 3, 13))
FIRST_PREP = (("K", 0), ("K", 1), ("V", 0), ("K", 2), ("V", 1), ("K", 3), ("V", 2), ("V", 3))
GATHERS = ([(h, den) for h in range(8) for den in (0, 1)] + [(h, 1) for h in range(8, HEADS - 1)]
           + [(h, 0) for h in range(8, HEADS - 1)])
PREP1 = (("K", 0), ("K", 1), ("V", 0), ("V", 1), ("K", 2), ("V", 2), ("K", 3), ("V", 3))
V_TILES = ((0, 3), (3, 6), (6, 10), (10, 14))
V_BEFORE_MAX = 3
HALF_READ = 3
K_AT = {j: n for kind, n, j in PREP if kind == "K"}
V_AT = {j: n for kind, n, j in PREP if kind == "V"}
MAX_AHEAD = 8
EARLY = -(-MAX_AHEAD // UPC)
STACK = 6 * HD
QPART = (0, 0, 0, 1, 1, 2)
KROWS = ((0, 3), (48, 2), (80, 1))
SROWS = STACK + 3

LH, LD = 16, 64
LEPS = 1e-3
E0, F0 = 8, 512
E1, F1 = 16, 128
FS = 512
SLOTS1 = E1 + FS // F1
EPP = SLOTS1 // (GH // 2)
LN_EPS = 1e-5

_CONSTS = {"ident": P, "causal": P, "numsel": 2 * P - HD, "densel": 2 * P - HD, "blockdiag": P,
           "rev0": E0, "rev1": E1, "onecol": 31, "spread": LH * LD}


def _const_at(name):
    at = 0
    for n, w in _CONSTS.items():
        if n == name:
            return at, at + w
        at += w


def _constants():
    p = np.arange(P)[:, None]
    out = np.zeros((P, sum(_CONSTS.values())), np.float32)

    def put(name, a):
        lo, hi = _const_at(name)
        out[:, lo:hi] = a
    col = np.arange(P)[None, :]
    put("ident", p == col)
    put("causal", p <= col)
    j = np.arange(2 * P - HD)[None, :] - (P - HD)
    put("numsel", (p % 32 == j) & (j >= 0) & (j < HD))
    put("densel", (p % 32 == HD) & (j >= 0) & (j < HD))
    put("blockdiag", p // HD == col // HD)
    put("rev0", E0 - np.arange(E0)[None, :] + 0 * p)
    put("rev1", E1 - np.arange(E1)[None, :] + 0 * p)
    put("onecol", (np.arange(31)[None, :] == 15) & (p >= 0))
    put("spread", p == np.arange(LH * LD)[None, :] // LD)
    return out


def program(nc, a, out):
    ctx = ExitStack()
    with ctx:
        def sb(name, shape, dt=F32):
            return ctx.enter_context(nc.sbuf_tensor(name, shape, dt))

        sems = {}

        def sem(name):
            if name not in sems:
                sems[name] = ctx.enter_context(nc.semaphore(name))
            return sems[name]

        k_scratch = nc.dram_tensor("k_scratch", [2, HEADS, 3, HD, KEYS], BF16, kind="Internal").ap()
        v_scratch = nc.dram_tensor("v_scratch", [2 * HEADS, P, TILES * VW], F32, kind="Internal").ap()
        q_scratch = nc.dram_tensor("q_scratch", [2, 3, D, P], BF16, kind="Internal").ap()

        consts = sb("consts", [P, sum(_CONSTS.values())])

        def const(name):
            lo, hi = _const_at(name)
            return consts[:, lo:hi]
        ident, causal, blockdiag = const("ident"), const("causal"), const("blockdiag")
        numsel, densel, onecol, spread = const("numsel"), const("densel"), const("onecol"), const("spread")
        wk = sb("wk", [CD, 2 * D])
        wv = sb("wv", [CD, 2 * D])
        bk = sb("bk", [P, 2 * DC])
        bv = sb("bv", [P, 2 * D])
        bq = sb("bq", [P, DC])
        wq = sb("wq", [P, 2, DC, D])
        wo = sb("wo", [P, 2, DC, D])
        bias_rows = sb("bias_rows", [P, 4, D])
        gate0 = sb("gate0", [P, DC, E0])
        gate1 = sb("gate1", [P, DC, E1 + 1])
        xs = sb("xs", [P, 7, D])
        xb = sb("xb", [P, 2, D])
        xhat = sb("xhat", [P, D])
        xhatT = sb("xhatT", [P, 2, DC, P])
        rn = sb("rn", [P, D])
        small = sb("small", [P, 96])
        attnT = sb("attnT", [P, DC, P])
        rden = sb("rden", [P, DC, P])
        qf = sb("qf", [P, DC, P])
        qr = sb("qr", [P, DC, P])
        qp = sb("qp", [P, DC, 3, P], BF16)
        qstack = sb("qstack", [P, HEADS, P], BF16)
        maxima = sb("maxima", [P, 2, UNITS])
        negmax = sb("negmax", [P, 2, 1])
        negrest = sb("negrest", [P, 2, 1])
        gates = sb("gates", [P, 7, E1])
        negparts = sb("negparts", [P, 2, 3], BF16)
        unity = sb("unity", [P, 1])
        eps = sb("eps", [P, 1])
        identb = sb("identb", [P, P], BF16)

        region_k = sb("region_k", [P, 2 * KEYS], BF16)
        kstack = region_k[:, :].rearrange("p (b k) -> p b k", b=2)
        as_f = region_k[:, :].bitcast(F32)
        h0T = as_f[:, KEYS - 32 * P:KEYS].rearrange("p (f n) -> p f n", f=32)
        region_w = sb("region_w", [P, 16384])
        lin_w = region_w[:, 0:DC * 3072].rearrange("p (k n) -> p k n", k=DC)
        lin_wo = region_w[:, 6144:8192].rearrange("p (f c) -> p f c", f=8)
        w2 = region_w[:, 0:32 * D].rearrange("p (f c) -> p f c", f=32)
        w1 = region_w[:, 8192:16384].rearrange("p (k n) -> p k n", k=DC)
        we_in = region_w[:, 0:DC * 2 * 20 * P].rearrange("p (k s f) -> p k s f", k=DC, s=2)
        we_out = region_w[:, 10240:10240 + 20 * D].rearrange("p (e c) -> p e c", e=20)
        o_heads = sb("o_heads", [P, HEADS, P])
        PARTS = CHUNK * 3 // 2
        VRING = GH * CT * VW
        w_at, k_at = 8192, KEYS // 2
        ctx_buf = [region_w[:, w_at:w_at + CHUNK], as_f[:, k_at:k_at + CHUNK]]
        k_parts = [r.bitcast(BF16).rearrange("p (s k) -> p s k", s=3) for r in (
            region_w[:, w_at + CHUNK:w_at + CHUNK + PARTS], as_f[:, k_at + CHUNK:k_at + CHUNK + PARTS])]
        v_ring = [r.rearrange("p (h t c) -> p h t c", h=GH, t=CT) for r in (
            region_w[:, w_at + CHUNK + PARTS:w_at + CHUNK + PARTS + VRING],
            o_heads[:, :, :].rearrange("p a b -> p (a b)")[:, 0:VRING])]
        rest_at = w_at + CHUNK + PARTS + VRING
        k_rest = region_w[:, rest_at:rest_at + REST_SLOTS * UNIT].rearrange("p (b k) -> p b k", b=REST_SLOTS)

        vbuf = sb("vbuf", [P, 2, TILES * VW + 32 - VW])
        probs = sb("probs", [P, 2, GT * P])
        linq = sb("linq", [P, 8, P])
        link = sb("link", [P, 8, P])
        linv = o_heads[:, 0:8, :].rearrange("p a b -> p (a b)")
        lin_oT = o_heads[:, 8:16, :]
        lin_aT = vbuf[:, :, :].rearrange("p a b -> p (a b)")[:, 0:LH * P].rearrange("p (h n) -> p h n", h=LH)
        lin_rd = probs[0:LH, 0, 0:P]
        w_kvu = sb("w_kvu", [P, DC, 3 * D])
        w_q2 = region_w[:, 15360:15872].rearrange("p (k n) -> p k n", k=DC)
        w_o2 = region_w[:, 15872:16384].rearrange("p (k n) -> p k n", k=DC)
        q2T = linq[:, 0:2, :]
        kvu = o_heads[:, 0:6, :].rearrange("p a b -> p (a b)")
        kvm = linq[:, 2:4, :]
        o2 = linq[:, 4:6, :].rearrange("p a b -> p (a b)")
        o2sq = linq[:, 6:8, :].rearrange("p a b -> p (a b)")
        o2T = link[:, 0:2, :]
        h1T = vbuf[:, :, :].rearrange("p a b -> p (a b)")[:, 0:20 * P].rearrange("p (e n) -> p e n", e=20)
        acc = link[:, 0:8, :].rearrange("p a b -> p (a b)").rearrange("p (s c) -> p s c", s=4)
        silu_g = probs[:, :, 0:4 * P]

        psum = ctx.enter_context(nc.psum_tensor("psum", [P, 8, 512], F32))
        bank = [psum[:, b, :] for b in range(8)]
        s_slots = [psum[:, 0:2, :].rearrange("p a b -> p (a b)"), psum[:, 2:4, :].rearrange("p a b -> p (a b)")]
        o_bank = bank[4]
        x_bank = bank[5]
        a_banks = [bank[6], bank[7]]
        num_banks, den_banks = (bank[6], bank[7]), (bank[7], bank[5])

        block = ctx.enter_context(nc.Block())

        KREST_AHEAD, VBATCH_AHEAD = 2, BATCHES
        REDUCED_AHEAD = 2
        SPLIT_AHEAD = REST_SLOTS
        STORED_K, STORED_V = 16 * GH, 16

        def prep_use(p, c):
            return FIRST // 2 + CHUNKS * p + c - FIRST

        def halves(eng, layer, pair):
            for half in range(2):
                p = (2 * layer + half + 1) % 4
                some = lambda c: c if p else None
                first = half * (GH // 2)
                with eng.Fori(first, first + GH // 2 - 1) as i:
                    c = 2 * (i - first) + p % 2
                    pair(i, False, p, (some(c), some(c + 1)))
                pair(first + GH // 2 - 1, half == 1, p, (None if p % 2 else some(CHUNKS - 1), None))

        def batch_tiles(m):
            return range(*V_TILES[m])

        def once(eng, name, *pairs):
            for dst, src in pairs:
                eng.dma_start(dst, src).then_inc(sem(name), 16)
            return 16 * len(pairs)
        on_all = lambda v: v.rearrange("(a n) -> a n", a=1).broadcast_to([P, v.shape[0]])

        def vcols(buf, t):
            return vbuf[:, buf, t * VW:t * VW + 32]

        V_BANKS1 = (bank[4], bank[5], bank[0], bank[4])

        def stack(eng, layer, h, buf, cols, name):
            for row, parts in KROWS:
                rows = parts * HD
                eng.dma_start(kstack[row:row + rows, buf, cols],
                              k_scratch[layer, bass.ds(h, 1)].rearrange("a s d k -> (a s d) k")[0:rows, cols])\
                    .then_inc(sem(name), 16)

        @block.sync
        def _(sp):
            once(sp, "x_loaded", (xs[:, 0, :], a["x"]))
            once(sp, "kv_weights_loaded", (wk[:, :], a["wk"]), (wv[:, :], a["wv"]),
                 (bk[:, 0:DC], a["bk"]), (bv[:, 0:D], on_all(a["bv"])))

            def load_ctx(c, buf, half):
                at = half * (CHUNK // 2)
                sp.dma_start(ctx_buf[buf][:, at:at + CHUNK // 2],
                             a["ctxT"][:, bass.ds(c * CHUNK + at, CHUNK // 2)])\
                    .then_inc(sem(f"ctx_loaded{buf}_{half}"), 16)

            def store_k(p, c, g, buf):
                sp.wait_ge(sem("k_unit_split"), SPLIT_AHEAD + UPC * (g + 1))
                for h in range(GH):
                    sp.dma_start(k_scratch[p // 2, GH * (p % 2) + h, :, :, bass.ds(c * CHUNK, CHUNK)]
                                 .rearrange("s d k -> d s k"), k_parts[buf][h * HD:(h + 1) * HD])\
                        .then_inc(sem(f"k_stored{buf}"), 16)

            def store_v(p, c, g, buf):
                sp.wait_ge(sem("v_batch_done"), VBATCH_AHEAD + BATCHES * (g + 1))
                sp.dma_start(v_scratch[GH * p:GH * (p + 1), :, bass.ds(c * CT * VW, CT * VW)]
                             .rearrange("h p n -> p h n"),
                             v_ring[buf].rearrange("p h t c -> p h (t c)")).then_inc(sem(f"v_stored{buf}"), 16)

            for half in range(2):
                load_ctx(0, 0, half)
            once(sp, "ident_loaded", (ident, a["consts"][:, 0:P]))
            once(sp, "q_weights_loaded", (wq[:, 0], a["wq0"].rearrange("(k p) n -> p k n", p=P)),
                 (bq[:, :], a["bq"]))
            for half in range(2):
                load_ctx(1, 1, half)
            sp.dma_start(kstack[STACK:SROWS, 0, :], a["ones"]).then_inc(sem("ones_loaded0"), 16)

            def stack_q(layer):
                sp.wait_ge(sem("q_split"), layer + 1)
                for g in range(DC):
                    sp.dma_start(q_scratch[layer, :, g * P:(g + 1) * P, :].rearrange("s r n -> r s n"), qp[:, g])\
                        .then_inc(sem("q_stored"), 16)
                sp.wait_ge(sem("q_stored"), 16 * DC * (layer + 1))
                for b, s in enumerate(QPART):
                    sp.dma_start(qstack[b * HD:(b + 1) * HD, :, :],
                                 q_scratch[layer, s].rearrange("(h d) n -> d h n", d=HD))\
                        .then_inc(sem("q_stacked"), 16)

            def after_chunk(p, c, g, buf, ahead=None):
                if ahead is not None:
                    sp.wait_ge(sem("v_in_psum"), BATCHES * (g + 1))
                    for half in range(2):
                        load_ctx(c + ahead, buf, half)
                store_k(p, c, g, buf)
                store_v(p, c, g, buf)

            after_chunk(0, 0, 0, 0, 2)
            stack_q(0)
            after_chunk(0, 1, 1, 1, 2)
            with sp.Fori(1, FIRST // 2 - 1) as i:
                for buf in range(2):
                    c = 2 * i + buf
                    after_chunk(0, c, c, buf, 2)

            def load_k(layer, h, buf, c):
                stack(sp, layer, h, buf, slice(c * CHUNK, (c + 1) * CHUNK), f"k_loaded{buf}_{c}")

            def load_v(layer, h, buf):
                sp.dma_start(vbuf[:, buf, 0:TILES * VW],
                             v_scratch[bass.ds(layer * HEADS + h, 1)].rearrange("a p n -> p (a n)"))\
                    .then_inc(sem(f"v_loaded{buf}"), 16)

            def load_ones(buf):
                sp.dma_start(kstack[STACK:SROWS, buf, :], a["ones"]).then_inc(sem(f"ones_loaded{buf}"), 16)

            def second_stack_start(layer):
                for c in range(EARLY):
                    load_k(layer, 1, 1, c)

            after_chunk(0, CHUNKS - 1, CHUNKS - 1, 0, 2)
            sp.wait_ge(sem("v_in_psum"), BATCHES * FIRST)
            second_stack_start(0)
            for buf, uses in ((0, FIRST // 2), (1, FIRST // 2 - 1)):
                sp.wait_ge(sem(f"v_stored{buf}"), STORED_V * (uses + 1))
            load_v(0, 0, 0)
            after_chunk(1, 0, CHUNKS, 1)
            sp.wait_ge(sem("k_stored1"), STORED_K * (FIRST // 2 + 1))
            load_ones(1)

            def attention_loads(layer):
                base = layer * HEADS
                for c in range(EARLY, CHUNKS):
                    load_k(layer, 1, 1, c)
                if layer == 0:
                    load_v(0, 1, 1)
                    sp.wait_ge(sem("v_stored1"), STORED_V * (FIRST // 2 + 1))
                else:
                    store_v(3, 0, 3 * CHUNKS, 0)
                    store_k(3, 0, 3 * CHUNKS, 0)
                    sp.wait_ge(sem("k_in_psum"), UPC * (3 * CHUNKS + 1))
                    sp.wait_ge(sem("v_in_psum"), BATCHES * (3 * CHUNKS + 1))
                    for half in range(2):
                        load_ctx(1, 0, half)

                if layer == 0:
                    once(sp, "mid_weights_loaded",
                         (wq[:, 1], a["wq1"].rearrange("(k p) n -> p k n", p=P)),
                         (wo[:, 0], a["wo0"].rearrange("(k p) n -> p k n", p=P)),
                         (wo[:, 1], a["wo1"].rearrange("(k p) n -> p k n", p=P)),
                         (bias_rows[:, 0, :], on_all(a["bo0"])), (bias_rows[:, 1, :], on_all(a["lin_bo"])),
                         (bias_rows[:, 2, :], on_all(a["gamma"])), (bias_rows[:, 3, :], on_all(a["beta"])),
                         (gate0[:, :, :], a["gate0"].rearrange("(k p) n -> p k n", p=P)),
                         (gate1[:, :, :], a["gate1"].rearrange("(k p) n -> p k n", p=P)),
                         (w_kvu[:, :, :], a["w_kvu"].rearrange("(k p) n -> p k n", p=P)),
                         (consts[:, P:], a["consts"][:, P:]))

                def head(h, par, more, p, c, new_piece, extra=None):
                    g = CHUNKS * (p or 0) + c if p else None
                    for cc in range(CHUNKS):
                        if more:
                            sp.wait_ge(sem("scores_done"), (base + h) * GROUPS + GPC * (cc + 1))
                            if new_piece:
                                sp.wait_ge(sem("k_stored0"), STORED_K * (prep_use(new_piece, cc) + 2))
                            load_k(layer, h + 2, par, cc)
                        if p and cc == 4:
                            store_k(p, c, g, 0)
                        if p and cc == 5 and not (isinstance(c, int) and c == CHUNKS - 1):
                            sp.wait_ge(sem("v_in_psum"), BATCHES * g + HALF_READ)
                            load_ctx(c + 1, 0, 0)
                        if extra and cc == 5:
                            extra()
                    if p:
                        if not (isinstance(c, int) and c == CHUNKS - 1):
                            sp.wait_ge(sem("v_in_psum"), BATCHES * (g + 1))
                            load_ctx(c + 1, 0, 1)
                        store_v(p, c, g, 0)
                    if more:
                        sp.wait_ge(sem("head_done"), base + h + 1)
                        if new_piece:
                            sp.wait_ge(sem("v_stored0"), STORED_V * (prep_use(new_piece, CHUNKS) + 1))
                        load_v(layer, h + 2, par)

                for half in range(2):
                    p = (2 * layer + half + 1) % 4
                    first = half * (GH // 2)

                    def weights(i):
                        n = i - first

                        def lin_in():
                            cols = bass.ds(n * (3072 // 4), 3072 // 4)
                            once(sp, "lin_weights_loaded",
                                 (lin_w[:, :, cols], a["lin_w"].rearrange("(k p) n -> p k n", p=P)[:, :, cols]))

                        def lin_out():
                            once(sp, "lin_weights_loaded",
                                 (lin_wo[:, bass.ds(2 * n, 2), :],
                                  a["lin_wo"].rearrange("(f p) c -> p f c", p=P)[:, bass.ds(2 * n, 2), :]))

                        def experts_in():
                            cols = bass.ds(n * EPP * P, EPP * P)
                            for s in range(2):
                                once(sp, "experts_loaded",
                                     (we_in[:, :, s, cols], a["we_in"][:, s, cols].rearrange("(k p) f -> p k f", p=P)))

                        def experts_out():
                            once(sp, "experts_loaded",
                                 (we_out[:, bass.ds(n * EPP, EPP), :],
                                  a["we_out"].rearrange("(e p) c -> p e c", p=P)[:, bass.ds(n * EPP, EPP), :]))
                        if layer == 0 and half == 0:
                            return lin_in, lin_out
                        if layer == 1 and half == 1:
                            return experts_in, experts_out
                        return None, None
                    with sp.Fori(first, first + GH // 2 - 1) as i:
                        beside = weights(i)
                        c = 2 * (i - first) + p % 2
                        head(2 * i, 0, True, p, c, None, beside[0])
                        head(2 * i + 1, 1, True, p, c + 1, None, beside[1])
                    i = first + GH // 2 - 1
                    beside = weights(i)
                    new_piece = p if half == 0 else None
                    head(2 * i, 0, half == 0, None if p % 2 else p, CHUNKS - 1, new_piece, beside[0])
                    if layer == 0 and half == 1:
                        sp.wait_ge(sem("k_stored0"), STORED_K * (prep_use(2, CHUNKS) + 1))
                        sp.wait_ge(sem("v_stored0"), STORED_V * (prep_use(2, CHUNKS) + 1))
                        once(sp, "w1_loaded", (w1[:, :, :], a["w1"].rearrange("(k p) n -> p k n", p=P)))
                    head(2 * i + 1, 1, half == 0, None, 0, new_piece, beside[1])
                    if layer == 1 and half == 0:
                        for part in range(2):
                            sp.wait_ge(sem(f"ctx_loaded0_{part}"), 16 * (prep_use(3, CHUNKS) + 1))
                        once(sp, "lin2_weights_loaded",
                             (w_q2, a["w_q2"].rearrange("(k p) n -> p k n", p=P)),
                             (w_o2, a["w_o2"].rearrange("(k p) n -> p k n", p=P)))

            attention_loads(0)
            sp.wait_ge(sem("head_done"), HEADS)
            load_ones(0)
            for c in range(CHUNKS):
                load_k(1, 0, 0, c)
            second_stack_start(1)
            w2_rows = a["w2"].rearrange("(f p) c -> p f c", p=P)
            sp.wait_ge(sem("lin_v_in_psum"), 2)
            once(sp, "w2_start_loaded", (w2[:, 0:24, :], w2_rows[:, 0:24, :]))
            sp.wait_ge(sem("block_out"), 2)
            once(sp, "w2_end_loaded", (w2[:, 24:32, :], w2_rows[:, 24:32, :]))
            for h in range(2):
                load_v(1, h, h)
            sp.wait_ge(sem("h0_in_psum"), E0)
            for half in range(2):
                load_ctx(0, 0, half)
            sp.wait_ge(sem("expert_in_psum"), E0)
            load_ones(1)
            stack_q(1)
            attention_loads(1)
            sp.wait_ge(sem("out_ready"), 1)
            sp.dma_start(out, xs[:, 6, :]).then_inc(sem("out_stored"), 16)
            sp.wait_ge(sem("out_stored"), 16)

        @block.tensor
        def _(pe):
            mm, tr = pe.matmul, pe.transpose

            def transpose_xhat(k, src, slot, b):
                for c in range(DC):
                    ins = tr(bank[b][:, c * P:(c + 1) * P], src[:, c * P:(c + 1) * P], ident)
                ins.then_inc(sem("xhatT_in_psum"), 1)

            def project_q(layer, par, b):
                for g in range(DC):
                    for c in range(DC):
                        ins = mm(bank[b][:, g * P:(g + 1) * P], wq[:, layer, c, g * P:(g + 1) * P],
                                 xhatT[:, par, c, :], start=(c == 0), stop=(c == DC - 1))
                ins.then_inc(sem("q_in_psum"), 1)

            pe.wait_ge(sem("kv_weights_loaded"), 64)

            def k_unit(p, buf, n, b):
                mm(b[:, 0:UNIT], wk[:, p * P:(p + 1) * P], ctx_buf[buf][:, n * UNIT:(n + 1) * UNIT],
                   start=True, stop=True).then_inc(sem("k_in_psum"), 1)

            def v_batch(p, buf, m, b):
                for k, t in enumerate(batch_tiles(m)):
                    ins = mm(b[:, k * P:(k + 1) * P], ctx_buf[buf][:, t * P:(t + 1) * P], wv[:, p * P:(p + 1) * P],
                             start=True, stop=True)
                ins.then_inc(sem("v_in_psum"), 1)

            def max_matmul(n, a_, qh, keys):
                pe.wait_ge(sem("unit_reduced"), REDUCED_AHEAD + n - 1)
                mm(a_banks[a_ % 2][:, 0:UNIT], qstack[0:STACK, bass.ds(qh, 1), :], keys, start=True, stop=True)\
                    .then_inc(sem("unit_in_psum"), 1)

            def first_stack_units(c, par, uses):
                pe.wait_ge(sem("q_stacked"), 96)
                pe.wait_ge(sem(f"first_stack_loaded{par}"), 48 * (uses + 1))
                for n in range(UPC):
                    max_matmul(UPC * c + n, n, 0, kstack[0:STACK, 0, bass.ds(c * CHUNK + n * UNIT, UNIT)])

            def first_prep(c, use, buf, stack=True, p=0):
                for kind, n in FIRST_PREP:
                    if kind == "K":
                        if n % 2 == 0:
                            pe.wait_ge(sem(f"ctx_loaded{buf}_{n // 2}"), 16 * (use + 1))
                        pe.wait_ge(sem("k_rest_done"), UPC * c + n + 1)
                        k_unit(p, buf, n, bank[n % 2])
                    else:
                        if stack and n == BATCHES - 1:
                            first_stack_units(c - 2, buf, use - 1)
                        pe.wait_ge(sem("v_batch_done"), BATCHES * c + n + 1)
                        v_batch(p, buf, n, bank[2 + n])

            first_prep(0, 0, 0, stack=False)
            pe.wait_ge(sem("ident_loaded"), 16)
            pe.wait_ge(sem("xhat_ready"), 1)
            transpose_xhat(0, xhat, 0, 6)
            pe.wait_ge(sem("q_weights_loaded"), 32)
            pe.wait_ge(sem("xhatT_ready"), 1)
            project_q(0, 0, 7)
            first_prep(1, 0, 1, stack=False)
            with pe.Fori(1, FIRST // 2 - 1) as i:
                first_prep(2 * i, i, 0)
                first_prep(2 * i + 1, i, 1)
            first_prep(CHUNKS - 1, FIRST // 2 - 1, 0)
            first_prep(CHUNKS, FIRST // 2 - 1, 1, p=1)
            first_stack_units(CHUNKS - 1, 0, FIRST // 2 - 1)

            def before_layer1(kind, n):
                g = 3 * CHUNKS
                if kind == "K":
                    pe.wait_ge(sem("k_rest_done"), UPC * g + n + 1)
                    k_unit(3, 0, n, bank[2 + n % 2])
                else:
                    if n == BATCHES - 1:
                        pe.wait_ge(sem("v_batch_done"), VBATCH_AHEAD + BATCHES * g + 1)
                    v_batch(3, 0, n, V_BANKS1[n])

            def attention(layer):
                base = layer * HEADS

                def max_unit(h, par, a_, loads=None):
                    n = (base + h) * UNITS + a_
                    if a_ % UPC == 0:
                        pe.wait_ge(sem(f"k_loaded{par}_{a_ // UPC}"),
                                   48 * (layer * (HEADS // 2) + loads + (1 if par else 0)))
                    max_matmul(n, a_, h, kstack[0:STACK, par, a_ * UNIT:(a_ + 1) * UNIT])

                def max_row(h, par):
                    pe.wait_ge(sem("negmax_split"), base + h + 1)
                    tr(x_bank[96:99, 0:P // 2].bitcast(BF16), negparts[:, par, :], identb[:, :])\
                        .then_inc(sem("negmax_in_psum"), 1)

                def prep_beside(p, c, j):
                    g = CHUNKS * p + c
                    for at, (kind, n, beside) in enumerate(PREP):
                        if beside != j:
                            continue
                        if kind == "K" and n % 2 == 0:
                            pe.wait_ge(sem(f"ctx_loaded0_{n // 2}"), 16 * (prep_use(p, c) + 1))
                        if at == 0:
                            pe.wait_ge(sem("v_batch_done"), VBATCH_AHEAD + BATCHES * g)
                        elif PREP[at - 1][0] == "K":
                            pe.wait_ge(sem("k_rest_done"), KREST_AHEAD + UPC * g + PREP[at - 1][1] + 1)
                        else:
                            pe.wait_ge(sem("v_batch_done"), VBATCH_AHEAD + BATCHES * g + PREP[at - 1][1] + 1)
                        if kind == "K":
                            k_unit(p, 0, n, x_bank)
                        else:
                            v_batch(p, 0, n, x_bank)

                def scores(h, par, j):
                    if j == 0:
                        pe.wait_ge(sem("qstack_max_ready"), base + h + 1)
                        pe.wait_ge(sem(f"ones_loaded{par}"), 16 * (layer + 1))
                    for t in range(GT):
                        key = (j * GT + t) * P
                        ins = mm(s_slots[j % 2][:, t * P:(t + 1) * P], kstack[0:SROWS, par, key:key + P],
                                 qstack[0:SROWS, bass.ds(h, 1), :], start=True, stop=True)
                    ins.then_inc(sem("scores_done"), 1)

                def values(h, par, j, loads):
                    pe.wait_ge(sem("exp_done"), (base + h) * GROUPS + j + 1)
                    if j == 0:
                        pe.wait_ge(sem("o_copied"), base + h + 1)
                        pe.wait_ge(sem(f"v_loaded{par}"), 16 * (layer * (HEADS // 2) + loads + 1))
                        pe.wait_ge(sem("vbuf_padded"), layer + 1)
                    for t in range(GT):
                        tile, g = j * GT + t, (j * GT + t) % 4
                        ins = mm(o_bank[32 * g:32 * g + 32, 0:P], vcols(par, tile),
                                 probs[:, j % 2, t * P:(t + 1) * P], start=(tile < 4), stop=(tile >= TILES - 4))
                    if j == GROUPS - 1:
                        ins.then_inc(sem("head_done"), 1)

                if layer == 1:
                    for step in PREP1:
                        before_layer1(*step)
                    pe.wait_ge(sem("q_stacked"), 96 * (layer + 1))
                    for a_ in range(UNITS):
                        max_unit(0, 0, a_, 0)
                for a_ in range(MAX_AHEAD):
                    max_unit(1, 1, a_, 0)
                pe.wait_ge(sem("k_rest_done"), KREST_AHEAD + UPC * (CHUNKS * (2 * layer + 1) + 1))
                pe.wait_ge(sem("v_batch_done"), VBATCH_AHEAD + BATCHES * (CHUNKS * (2 * layer + 1) + 1))
                max_row(0, 0)
                scores(0, 0, 0)

                def pair(i, last, p, chunks):
                    for par in range(2):
                        h = 2 * i + par
                        end = last and par == 1
                        for j in range(GROUPS):
                            if j == GROUPS - 2 and not end:
                                if chunks[par] is not None:
                                    pe.wait_ge(sem("v_batch_done"),
                                               VBATCH_AHEAD + BATCHES * (CHUNKS * p + chunks[par]) + V_BEFORE_MAX)
                                max_row(h + 1, 1 - par)
                            if j < GROUPS - 1:
                                scores(h, par, j + 1)
                            elif not end:
                                scores(h + 1, 1 - par, 0)

                            def unit(a_):
                                if a_ < UNITS and not end:
                                    max_unit(h + 1, 1 - par, a_, i + par)
                                elif a_ >= UNITS and not last:
                                    max_unit(h + 2, par, a_ - UNITS, i + 1)
                            unit(2 * j + MAX_AHEAD)
                            if chunks[par] is not None:
                                prep_beside(p, chunks[par], j)
                            unit(2 * j + 1 + MAX_AHEAD)
                            values(h, par, j, i)
                            if end:
                                n = len(GATHERS)
                                for at in range(j * n // GROUPS, (j + 1) * n // GROUPS):
                                    gather(*GATHERS[at])

                def gather(h, den):
                    g, hh = h // 8, h % 8
                    if h == 0 and not den:
                        pe.wait_ge(sem("mid_weights_loaded"), 16 * 11)
                        pe.wait_ge(sem("unit_reduced"), REDUCED_AHEAD + (base + HEADS) * UNITS)
                    if h == 8 and not den:
                        pe.wait_ge(sem("attnT_ready"), DC * layer + 1)
                    if h == 8 and den:
                        pe.wait_ge(sem("v_batch_done"), VBATCH_AHEAD + BATCHES * CHUNKS * (3 + layer))
                    pe.wait_ge(sem("o_copied"), 1 + base + h + 1)
                    lo = P - HD - HD * hh
                    ins = mm((den_banks if den else num_banks)[g][:, 0:P], (densel if den else numsel)[:, lo:lo + P],
                             o_heads[:, h, :], start=(hh == 0), stop=(hh == 7))
                    if den and hh == 7:
                        ins.then_inc(sem("o_gathered"), 1)

                halves(pe, layer, pair)

                for den in range(2):
                    gather(HEADS - 1, den)
                for g in range(DC):
                    pe.wait_ge(sem("attnT_ready"), DC * layer + g + 1)
                    ins = mm(bank[6][:, 0:D], attnT[:, g, :], wo[:, layer, g, :], start=(g == 0), stop=(g == DC - 1))
                ins.then_inc(sem("block_out"), 1)

            def normed(k, b):
                pe.wait_ge(sem("xhat_ready"), k + 1 if k < 3 else k)
                transpose_xhat(k, xhat, 0, b)

            pe.wait_ge(sem("identb_ready"), 1)
            attention(0)

            normed(1, 0)
            pe.wait_ge(sem("lin_weights_loaded"), 32 * (GH // 2))
            pe.wait_ge(sem("xhatT_ready"), 2)
            for m in range(2):
                for f in range(8):
                    for c in range(DC):
                        ins = mm(bank[1 + 2 * m + f // 4][:, (f % 4) * P:(f % 4 + 1) * P],
                                 lin_w[:, c, 1024 * m + f * P:1024 * m + (f + 1) * P], xhatT[:, 1, c, :],
                                 start=(c == 0), stop=(c == DC - 1))
                    if f % 4 == 3:
                        ins.then_inc(sem("lin_qk_in_psum"), 1)
            for f in range(2):
                for c in range(DC):
                    ins = mm(bank[5 + f], xhatT[:, 1, c, :], lin_w[:, c, 2048 + 512 * f:2048 + 512 * (f + 1)],
                             start=(c == 0), stop=(c == DC - 1))
                ins.then_inc(sem("lin_v_in_psum"), 1)
            pe.wait_ge(sem("lin_qk_ready"), 4)
            for h in range(LH):
                r, f = 64 * (h % 2), h // 2
                b = 1 + 2 * (h % 2) + f // 4
                ins = mm(bank[b][:, (f % 4) * P:(f % 4 + 1) * P], link[r:r + 64, f, :], linq[r:r + 64, f, :],
                         start=True, stop=True)
                if h in (LH // 2 - 1, LH - 1):
                    ins.then_inc(sem("lin_scores_in_psum"), 1)
            pe.wait_ge(sem("lin_aT_ready"), 4)
            for h in range(LH):
                ins = mm(bank[0][0:LH, 0:P], onecol[:, 15 - h:31 - h], lin_aT[:, h, :],
                         start=(h == 0), stop=(h == LH - 1))
            ins.then_inc(sem("lin_sums_in_psum"), 1)
            pe.wait_ge(sem("lin_v_ready"), 2)
            for h in range(LH):
                r, f = 64 * (h % 2), h // 2
                ins = mm(bank[5 + f // 4][r:r + 64, (f % 4) * P:(f % 4 + 1) * P],
                         linv[:, h * LD:(h + 1) * LD], lin_aT[:, h, :], start=True, stop=True)
            ins.then_inc(sem("lin_av_in_psum"), 1)
            pe.wait_ge(sem("lin_rsum_ready"), 1)
            for f in range(8):
                ins = mm(bank[1 + f // 4][:, (f % 4) * P:(f % 4 + 1) * P], spread[0:LH, f * P:(f + 1) * P],
                         lin_rd, start=True, stop=True)
            ins.then_inc(sem("lin_rsum_spread"), 1)
            pe.wait_ge(sem("lin_oT_ready"), 2)
            for f in range(8):
                ins = mm(bank[7][:, 0:D], lin_oT[:, f, :], lin_wo[:, f, :], start=(f == 0), stop=(f == 7))
            ins.then_inc(sem("block_out"), 1)

            normed(2, 0)
            pe.wait_ge(sem("xhatT_ready"), 3)
            pe.wait_ge(sem("w1_loaded"), 16)

            def expert_in0(e):
                b = 1 + e % 2
                if e >= 2:
                    pe.wait_ge(sem("h0_ready"), e - 1)
                for f in range(4):
                    for c in range(DC):
                        at = e * F0 + f * P
                        ins = mm(bank[b][:, f * P:(f + 1) * P], w1[:, c, at:at + P], xhatT[:, 0, c, :],
                                 start=(c == 0), stop=(c == DC - 1))
                ins.then_inc(sem("h0_in_psum"), 1)

            def gate_logits(w, n, b, par):
                for c in range(DC):
                    ins = mm(bank[b][:, 0:n], xhatT[:, par, c, :], w[:, c, :], start=(c == 0), stop=(c == DC - 1))
                ins.then_inc(sem("logits_in_psum"), 1)

            expert_in0(0)
            expert_in0(1)
            pe.wait_ge(sem("rn_ready"), 1)
            transpose_xhat(3, rn, 0, 3)
            pe.wait_ge(sem("xhatT_ready"), 4)
            gate_logits(gate0, E0, 0, 1)
            for e in range(E0):
                if e in (0, 6):
                    pe.wait_ge(sem("w2_start_loaded" if e == 0 else "w2_end_loaded"), 16)
                if e >= 1 and e + 1 < E0:
                    expert_in0(e + 1)
                b = 4 + e % 4
                if e >= 4:
                    pe.wait_ge(sem("expert_mixed"), e - 3)
                pe.wait_ge(sem("h0_ready"), e + 1)
                for f in range(4):
                    ins = mm(bank[b][:, 0:D], h0T[:, 4 * e + f, :], w2[:, 4 * e + f, :], start=(f == 0), stop=(f == 3))
                ins.then_inc(sem("expert_in_psum"), 1)

            normed(4, 0)
            pe.wait_ge(sem("xhatT_ready"), 5)
            project_q(1, 0, 1)
            pe.wait_ge(sem("expert_mixed"), E0)
            for half in range(2):
                pe.wait_ge(sem(f"ctx_loaded0_{half}"), 16 * (prep_use(3, 0) + 1))
            attention(1)

            normed(5, 0)
            pe.wait_ge(sem("lin2_weights_loaded"), 32)
            pe.wait_ge(sem("xhatT_ready"), 6)
            for g in range(DC):
                for c in range(DC):
                    ins = mm(bank[1][:, g * P:(g + 1) * P], w_q2[:, c, g * P:(g + 1) * P], xhatT[:, 1, c, :],
                             start=(c == 0), stop=(c == DC - 1))
            ins.then_inc(sem("q2_in_psum"), 1)
            for s, (b, lo, n) in enumerate(((2, 0, 512), (3, 512, 256))):
                for c in range(DC):
                    ins = mm(bank[b][:, 0:n], xhatT[:, 1, c, :], w_kvu[:, c, lo:lo + n],
                             start=(c == 0), stop=(c == DC - 1))
                ins.then_inc(sem("kvu_in_psum"), 1)
            pe.wait_ge(sem("kv2_ready"), 2)
            for g in range(DC):
                ins = mm(bank[4 + g][:, 0:P], kvu[:, g * P:(g + 1) * P], kvu[:, D + g * P:D + (g + 1) * P],
                         start=True, stop=True)
            ins.then_inc(sem("kv_outer_in_psum"), 1)
            pe.wait_ge(sem("q2_ready"), 1)
            pe.wait_ge(sem("kvm_ready"), 2)
            for g in range(DC):
                ins = mm(bank[7][:, g * P:(g + 1) * P], q2T[:, g, :], kvm[:, g, :], start=True, stop=True)
            ins.then_inc(sem("o2_in_psum"), 1)
            pe.wait_ge(sem("o2_ready"), 1)
            for c in range(DC):
                ins = tr(bank[0][:, c * P:(c + 1) * P], o2[:, c * P:(c + 1) * P], ident)
            ins.then_inc(sem("o2T_in_psum"), 1)
            pe.wait_ge(sem("o2T_ready"), 1)
            for c in range(DC):
                ins = mm(bank[6][:, 0:D], o2T[:, c, :], w_o2[:, c, :], start=(c == 0), stop=(c == DC - 1))
            ins.then_inc(sem("block_out"), 1)

            normed(6, 0)
            pe.wait_ge(sem("xhatT_ready"), 7)
            gate_logits(gate1, E1 + 1, 7, 0)
            pe.wait_ge(sem("experts_loaded"), 48 * (GH // 2))

            def experts_in(r):
                if r >= 2:
                    pe.wait_ge(sem("h1_ready"), r - 1)
                for s in range(2):
                    for f in range(4):
                        for c in range(DC):
                            at = (4 * r + f) * P
                            ins = mm(bank[1 + 2 * (r % 2) + s][:, f * P:(f + 1) * P], we_in[:, c, s, at:at + P],
                                     xhatT[:, 0, c, :], start=(c == 0), stop=(c == DC - 1))
                    ins.then_inc(sem("gate_in_psum" if s == 0 else "up_in_psum"), 1)

            def experts_out(r):
                pe.wait_ge(sem("h1_ready"), r + 1)
                for e in range(4 * r, 4 * r + 4):
                    b = (0, 5, 6)[e % 3]
                    if e < 16:
                        if e >= 3:
                            pe.wait_ge(sem("expert_mixed"), E0 + e - 2)
                        mm(bank[b][:, 0:D], h1T[:, e, :], we_out[:, e, :], start=True, stop=True)\
                            .then_inc(sem("expert_in_psum"), 1)
                    else:
                        if e == 16:
                            pe.wait_ge(sem("sigmoid_ready"), 1)
                        ins = mm(bank[7][:, 0:D], h1T[:, e, :], we_out[:, e, :], start=(e == 16), stop=(e == 19))
                if r == 4:
                    ins.then_inc(sem("shared_in_psum"), 1)
            experts_in(0)
            experts_in(1)
            for r in range(5):
                experts_out(r)
                if r + 2 < 5:
                    experts_in(r + 2)

        @block.scalar
        def _(act):
            def std(k):
                act.wait_ge(sem("var_ready"), k + 1)
                act.activation(small[:, 10:11], small[:, 7:8], ACT.Sqrt, bias=eps[:, :]).then_inc(sem("std_ready"), 1)

            std(0)
            act.wait_ge(sem("bk_zeroed"), 1)
            act.wait_ge(sem("kv_weights_loaded"), 64)

            for buf in range(2):
                act.sem_inc(sem(f"k_stored{buf}"), STORED_K)

            def first_part(p, g, use, buf, n, b):
                if n == 0:
                    act.wait_ge(sem(f"k_stored{buf}"), STORED_K * (use + 1))
                act.wait_ge(sem("k_in_psum"), UPC * g + n + 1)
                act.activation(k_parts[buf][:, 0, n * UNIT:(n + 1) * UNIT], b[:, 0:UNIT],
                               ACT.Identity, bias=bk[:, p:p + 1]).then_inc(sem("k1_done"), 1)

            def second_part(g, buf, n):
                act.wait_ge(sem("k_rest_done"), KREST_AHEAD + UPC * g + n + 1)
                act.activation(k_parts[buf][:, 1, n * UNIT:(n + 1) * UNIT], k_rest[:, n % REST_SLOTS, :], ACT.Copy)\
                    .then_inc(sem("k2_done"), 1)

            def two_parts(p, g, use, buf, banks):
                for n in range(UPC):
                    first_part(p, g, use, buf, n, banks[n % 2])
                    if n:
                        second_part(g, buf, n - 1)
                second_part(g, buf, UPC - 1)

            def first_stack(c, par, uses):
                act.wait_ge(sem(f"k_stored{par}"), STORED_K * (uses + 1))
                stack(act, 0, 0, 0, bass.ds(c * CHUNK, CHUNK), f"first_stack_loaded{par}")

            def first_prep(c, use, buf, p=0):
                two_parts(p, c, use, buf, bank[0:2])
                first_stack(c - 1, 1 - buf, use + buf)

            two_parts(0, 0, 0, 0, bank[0:2])
            first_prep(1, 0, 1)
            with act.Fori(1, FIRST // 2 - 1) as i:
                first_prep(2 * i, i, 0)
                first_prep(2 * i + 1, i, 1)
            first_prep(CHUNKS - 1, FIRST // 2 - 1, 0)
            first_prep(CHUNKS, FIRST // 2 - 1, 1, p=1)

            def attention(layer):
                base = layer * HEADS

                def exp_group(h, j):
                    act.wait_ge(sem("scores_done"), (base + h) * GROUPS + j + 1)
                    act.activation(probs[:, j % 2, :], s_slots[j % 2][:, 0:GT * P], ACT.Exp)\
                        .then_inc(sem("exp_done"), 1)

                def put_max(h, par):
                    act.wait_ge(sem("negmax_in_psum"), base + h + 1)
                    act.activation(qstack[96:99, bass.ds(h, 1), :],
                                   x_bank[96:99, 0:P // 2].bitcast(BF16), ACT.Copy)\
                        .then_inc(sem("qstack_max_ready"), 1)

                def copy_out(h, par):
                    act.wait_ge(sem("head_done"), base + h + 1)
                    if layer == 0:
                        act.wait_ge(sem("v_stored1"), STORED_V * (FIRST // 2 + 1))
                    ins = act.activation(o_heads[:, bass.ds(h, 1), :], o_bank[:, 0:P], ACT.Copy)
                    ins.then_inc(sem("o_copied"), 1)

                if layer == 0:
                    act.sem_inc(sem("o_copied"), 1)
                if layer == 1:
                    two_parts(3, 3 * CHUNKS, prep_use(3, 0), 0, bank[2:4])
                act.wait_ge(sem("q_stacked"), 96 * (layer + 1))
                put_max(0, 0)

                def pair(i, last, p, chunks):
                    for par in range(2):
                        h = 2 * i + par
                        for j in range(1, GROUPS):
                            exp_group(h, j)
                            if j - 1 in K_AT and chunks[par] is not None:
                                c = chunks[par]
                                first_part(p, CHUNKS * p + c, prep_use(p, c), 0, K_AT[j - 1], x_bank)
                            if j == GROUPS - 2 and not (last and par == 1):
                                put_max(h + 1, 1 - par)
                        if not (last and par == 1):
                            exp_group(h + 1, 0)
                        copy_out(h, par)

                exp_group(0, 0)
                halves(act, layer, pair)

            attention(0)

            std(1)
            for f in range(2):
                act.wait_ge(sem("lin_v_in_psum"), f + 1)
                act.activation(linv[:, 512 * f:512 * (f + 1)], bank[5 + f], ACT.Copy).then_inc(sem("lin_v_ready"), 1)
            for f in range(2):
                act.wait_ge(sem("lin_rsum_spread"), 1)
                act.activation(linq[:, 4 * f:4 * f + 4, :].rearrange("p f n -> p (f n)"), bank[1 + f], ACT.Copy)\
                    .then_inc(sem("lin_spread_ready"), 1)
            std(2)
            std(3)

            def gelu(e):
                act.wait_ge(sem("h0_in_psum"), e + 1)
                act.activation(h0T[:, 4 * e:4 * e + 4, :], bank[1 + e % 2].rearrange("p (f n) -> p f n", f=4),
                               ACT.Gelu).then_inc(sem("h0_ready"), 1)
            gelu(0)
            gelu(1)
            act.wait_ge(sem("gate_neg_ready"), 1)
            act.activation(small[:, 40:40 + E0], bank[0][:, 0:E0], ACT.Exp, bias=small[:, 12:13],
                           accum_out=small[:, 13:14]).then_inc(sem("gate_exp_ready"), 1)
            for e in range(2, E0):
                gelu(e)
            std(4)
            attention(1)
            std(5)
            act.wait_ge(sem("kvu_in_psum"), 2)
            act.activation(kvu[:, 2 * D:3 * D], bank[3][:, 0:D], ACT.Silu).then_inc(sem("u2_ready"), 1)
            act.wait_ge(sem("o2_sumsq_ready"), 1)
            act.activation(small[:, 64:80], small[:, 40:56], ACT.Sqrt).then_inc(sem("o2_norm_ready"), 1)
            std(6)
            act.wait_ge(sem("gate_neg_ready"), 2)
            act.activation(small[:, 40:40 + E1], bank[7][:, 0:E1], ACT.Exp, bias=small[:, 12:13],
                           accum_out=small[:, 13:14]).then_inc(sem("gate_exp_ready"), 1)
            act.activation(small[:, 14:15], bank[7][:, E1:E1 + 1], ACT.Sigmoid).then_inc(sem("sigmoid_ready"), 1)
            for r in range(5):
                act.wait_ge(sem("gate_in_psum"), r + 1)
                if r >= 2:
                    act.wait_ge(sem("h1_ready"), r - 1)
                act.activation(silu_g[:, r % 2, :], bank[1 + 2 * (r % 2)], ACT.Silu).then_inc(sem("silu_done"), 1)

        @block.gpsimd
        def _(pool):
            def cast(dst, src):
                return pool.tensor_tensor(dst, src, unity[:, :].broadcast_to(list(src.shape)), ALU.mult)

            pool.memset(unity[:, :], 1.0).then_inc(sem("unity_ready"), 1)
            pool.wait_ge(sem("unity_ready"), 1)

            def split_unit(g, buf, n, both=True):
                cols = slice(n * UNIT, (n + 1) * UNIT)
                rest = k_rest[:, n % REST_SLOTS, :]
                if both:
                    pool.wait_ge(sem("k_rest_done"), KREST_AHEAD + UPC * g + n + 1)
                    cast(k_parts[buf][:, 1, cols], rest).then_inc(sem("k2_done"), 1)
                pool.wait_ge(sem("k2_done"), UPC * g + n + 1)
                pool.tensor_tensor(k_parts[buf][:, 2, cols], rest, k_parts[buf][:, 1, cols], ALU.subtract)\
                    .then_inc(sem("k_unit_split"), 1)

            pool.sem_inc(sem("k_unit_split"), SPLIT_AHEAD)
            with pool.Fori(0, FIRST // 2) as i:
                for buf in range(2):
                    for n in range(UPC):
                        split_unit(2 * i + buf, buf, n, both=False)

            def split_max(h, par, layer):
                n = layer * HEADS + h
                pool.wait_ge(sem("negmax_ready"), n + 1)
                cast(negparts[:, par, 0:1], negmax[:, par]).then_inc(sem("split_step"), 1)
                pool.wait_ge(sem("split_step"), 3 * n + 1)
                pool.tensor_tensor(negrest[:, par], negmax[:, par], negparts[:, par, 0:1], ALU.subtract)\
                    .then_inc(sem("split_step"), 1)
                pool.wait_ge(sem("split_step"), 3 * n + 2)
                cast(negparts[:, par, 1:2], negrest[:, par]).then_inc(sem("split_step"), 1)
                pool.wait_ge(sem("split_step"), 3 * n + 3)
                pool.tensor_tensor(negparts[:, par, 2:3], negrest[:, par], negparts[:, par, 1:2], ALU.subtract)\
                    .then_inc(sem("negmax_split"), 1)

            for layer in range(2):
                for n in range(UPC if layer == 1 else 0):
                    split_unit(CHUNKS * 3, 0, n, both=False)
                split_max(0, 0, layer)

                def pair(i, last, p, chunks):
                    for par in range(2):
                        if chunks[par] is not None:
                            for n in range(UPC):
                                split_unit(CHUNKS * p + chunks[par], 0, n)
                        if not (last and par == 1):
                            split_max(2 * i + par + 1, 1 - par, layer)

                halves(pool, layer, pair)

        @block.vector
        def _(dve):
            steps = [0]

            def after(ins):
                ins.then_inc(sem("dve_step"), 1)
                steps[0] += 1
                dve.wait_ge(sem("dve_step"), steps[0])

            def stats(k, src):
                after(dve.bn_stats(small[:, 0:6], src))
                dve.bn_aggr(small[:, 6:8], small[:, 0:6]).then_inc(sem("var_ready"), 1)
                dve.wait_ge(sem("std_ready"), k + 1)
                after(dve.reciprocal(small[:, 11:12], small[:, 10:11]))

            def layernorm(k, src):
                stats(k, src)
                dve.tensor_scalar(xhat[:, :], src, small[:, 6:7], small[:, 11:12], ALU.subtract, ALU.mult)\
                    .then_inc(sem("xhat_ready"), 1)

            def copy_xhatT(k, par, b):
                dve.wait_ge(sem("xhatT_in_psum"), k + 1)
                dve.tensor_copy(xhatT[:, par].rearrange("p c n -> p (c n)"), bank[b][:, 0:D])\
                    .then_inc(sem("xhatT_ready"), 1)

            def split_q(layer, b):
                dve.wait_ge(sem("q_in_psum"), layer + 1)
                for g in range(DC):
                    src = bank[b][:, g * P:(g + 1) * P]
                    if layer == 0:
                        ins = dve.tensor_scalar(qf[:, g, :], src, bq[:, g:g + 1], HD ** -0.5, ALU.add, ALU.mult)
                    else:
                        ins = dve.tensor_scalar(qf[:, g, :], src, HD ** -0.5, None, ALU.mult)
                after(ins)
                if layer == 1:
                    dve.wait_ge(sem("q_stored"), 16 * DC)
                after(dve.tensor_copy(qp[:, :, 0, :], qf[:, :, :]))
                after(dve.tensor_tensor(qr[:, :, :], qf[:, :, :], qp[:, :, 0, :], ALU.subtract))
                after(dve.tensor_copy(qp[:, :, 1, :], qr[:, :, :]))
                dve.tensor_tensor(qp[:, :, 2, :], qr[:, :, :], qp[:, :, 1, :], ALU.subtract)\
                    .then_inc(sem("q_split"), 1)

            dve.memset(bk[:, DC:2 * DC], 0.0).then_inc(sem("bk_zeroed"), 1)
            after(dve.memset(eps[:, :], LN_EPS))
            after(dve.memset(bv[:, D:2 * D], 0.0))
            for buf in range(2):
                after(dve.memset(v_ring[buf][:, :, :, HD:VW].rearrange("p h t c -> p (h t c)"), 1.0))
            dve.memset(vbuf[:, :, TILES * VW:], 0.0).then_inc(sem("vbuf_padded"), 1)
            dve.wait_ge(sem("x_loaded"), 16)
            layernorm(0, xs[:, 0, :])

            dve.sem_inc(sem("unit_reduced"), REDUCED_AHEAD)
            dve.sem_inc(sem("k_rest_done"), KREST_AHEAD)
            dve.sem_inc(sem("v_batch_done"), VBATCH_AHEAD)
            for buf in range(2):
                dve.sem_inc(sem(f"v_stored{buf}"), STORED_V)
            dve.wait_ge(sem("kv_weights_loaded"), 64)

            def k_remainder(p, g, buf, n, b):
                dve.wait_ge(sem("k_unit_split"), UPC * g + n + 1)
                dve.wait_ge(sem("k1_done"), UPC * g + n + 1)
                dve.scalar_tensor_tensor(k_rest[:, n % REST_SLOTS, :], b[:, 0:UNIT], bk[:, p:p + 1],
                                         k_parts[buf][:, 0, n * UNIT:(n + 1) * UNIT],
                                         ALU.add, ALU.subtract).then_inc(sem("k_rest_done"), 1)

            def v_to_ring(p, g, use, buf, m, b):
                if m == 0:
                    dve.wait_ge(sem(f"v_stored{buf}"), STORED_V * (use + 1))
                tiles = batch_tiles(m)
                nt = len(tiles)
                dve.wait_ge(sem("v_in_psum"), BATCHES * g + m + 1)
                dve.tensor_tensor(
                    v_ring[buf][:, :, tiles[0]:tiles[0] + nt, 0:HD].rearrange("p h t d -> p t h d"),
                    b[:, 0:nt * P].rearrange("p (t h d) -> p t h d", h=GH, d=HD),
                    bv[:, p * P:(p + 1) * P].rearrange("p (a h d) -> p a h d", a=1, d=HD)
                    .broadcast_to([P, nt, GH, HD]), ALU.add).then_inc(sem("v_batch_done"), 1)

            def reduce_scores(n, par, u, b):
                dve.wait_ge(sem("unit_in_psum"), n + 1)
                dve.tensor_reduce(maxima[:, par, bass.ds(u, 1)], b[:, 0:UNIT], AX.X, ALU.max)\
                    .then_inc(sem("unit_reduced"), 1)

            def reduce_first_stack(c):
                for n in range(UPC):
                    reduce_scores(UPC * c + n, 0, UPC * c + n, a_banks[n % 2])

            def first_prep(c, use, buf, stack=True, p=0):
                for kind, n in FIRST_PREP:
                    if kind == "K":
                        k_remainder(p, c, buf, n, bank[n % 2])
                    else:
                        if stack and n == BATCHES - 1:
                            reduce_first_stack(c - 2)
                        v_to_ring(p, c, use, buf, n, bank[2 + n])

            first_prep(0, 0, 0, stack=False)
            dve.wait_ge(sem("ident_loaded"), 16)
            dve.tensor_copy(identb[:, :], ident).then_inc(sem("identb_ready"), 1)
            copy_xhatT(0, 0, 6)
            dve.wait_ge(sem("q_weights_loaded"), 32)
            split_q(0, 7)
            first_prep(1, 0, 1, stack=False)
            with dve.Fori(1, FIRST // 2 - 1) as i:
                first_prep(2 * i, i, 0)
                first_prep(2 * i + 1, i, 1)
            first_prep(CHUNKS - 1, FIRST // 2 - 1, 0)
            first_prep(CHUNKS, FIRST // 2 - 1, 1, p=1)

            def before_layer1(kind, n):
                if kind == "K":
                    k_remainder(3, 3 * CHUNKS, 0, n, bank[2 + n % 2])
                else:
                    v_to_ring(3, 3 * CHUNKS, prep_use(3, 0), 0, n, V_BANKS1[n])

            def attention(layer):
                base = layer * HEADS

                def reduce_unit(h, par, u):
                    n = (base + h) * UNITS + u
                    reduce_scores(n, par, u, a_banks[u % 2])
                    if u == UNITS - 1:
                        dve.wait_ge(sem("unit_reduced"), REDUCED_AHEAD + n + 1)
                        dve.tensor_reduce(negmax[:, par], maxima[:, par], AX.X, ALU.max, negate=True)\
                            .then_inc(sem("negmax_ready"), 1)

                if layer == 1:
                    for step in PREP1:
                        before_layer1(*step)
                for u in range(UNITS - UPC if layer == 0 else 0, UNITS):
                    reduce_unit(0, 0, u)
                for u in range(MAX_AHEAD):
                    reduce_unit(1, 1, u)

                def pair(i, last, p, chunks):
                    for par in range(2):
                        h = 2 * i + par
                        for j in range(GROUPS):
                            for q in (2 * j, 2 * j + 1):
                                u = q + MAX_AHEAD
                                if u < UNITS and not (last and par == 1):
                                    reduce_unit(h + 1, 1 - par, u)
                                elif u >= UNITS and not last:
                                    reduce_unit(h + 2, par, u - UNITS)
                                if chunks[par] is None:
                                    continue
                                c = chunks[par]
                                if q % 2 and j in K_AT:
                                    k_remainder(p, CHUNKS * p + c, 0, K_AT[j], x_bank)
                                if q % 2 == 0 and j in V_AT:
                                    v_to_ring(p, CHUNKS * p + c, prep_use(p, c), 0, V_AT[j], x_bank)

                halves(dve, layer, pair)

                for g in range(DC):
                    dve.wait_ge(sem("o_gathered"), DC * layer + g + 1)
                    after(dve.reciprocal(rden[:, g, :], den_banks[g][:, 0:P]))
                    dve.tensor_tensor(attnT[:, g, :], num_banks[g][:, 0:P], rden[:, g, :], ALU.mult)\
                        .then_inc(sem("attnT_ready"), 1)

            def add_block(k, b, res, dst):
                dve.wait_ge(sem("block_out"), k)
                after(dve.tensor_tensor(dst, bank[b][:, 0:D], res, ALU.add))

            attention(0)
            dve.wait_ge(sem("mid_weights_loaded"), 16 * 11)
            after(dve.tensor_tensor(xb[:, 0, :], xs[:, 0, :], bias_rows[:, 0, :], ALU.add))
            add_block(1, 6, xb[:, 0, :], xs[:, 1, :])

            layernorm(1, xs[:, 1, :])
            dve.tensor_tensor(xb[:, 1, :], xs[:, 1, :], bias_rows[:, 1, :], ALU.add).then_inc(sem("xb_ready"), 1)
            copy_xhatT(1, 1, 0)
            for n in range(4):
                dve.wait_ge(sem("lin_qk_in_psum"), n + 1)
                dst = (linq, link)[n // 2][:, 4 * (n % 2):4 * (n % 2) + 4, :]
                dve.tensor_scalar(dst, bank[1 + n].rearrange("p (f n) -> p f n", f=4), 0.0, LEPS, ALU.max, ALU.add)\
                    .then_inc(sem("lin_qk_ready"), 1)
            by_parity = lin_aT.rearrange("p (f r) n -> p r f n", r=2)
            for f in range(2):
                dve.wait_ge(sem("lin_scores_in_psum"), f + 1)
                for r in range(2):
                    dve.tensor_tensor(by_parity[:, r, 4 * f:4 * f + 4, :],
                                      bank[1 + 2 * r + f].rearrange("p (f n) -> p f n", f=4),
                                      causal.rearrange("p (a n) -> p a n", a=1).broadcast_to([P, 4, P]), ALU.mult)\
                        .then_inc(sem("lin_aT_ready"), 1)
            dve.wait_ge(sem("lin_sums_in_psum"), 1)
            dve.reciprocal(lin_rd, bank[0][0:LH, 0:P]).then_inc(sem("lin_rsum_ready"), 1)
            dve.wait_ge(sem("lin_av_in_psum"), 1)
            for f in range(2):
                dve.wait_ge(sem("lin_spread_ready"), f + 1)
                dve.tensor_tensor(lin_oT[:, 4 * f:4 * f + 4, :], bank[5 + f].rearrange("p (f n) -> p f n", f=4),
                                  linq[:, 4 * f:4 * f + 4, :], ALU.mult).then_inc(sem("lin_oT_ready"), 1)
            dve.wait_ge(sem("xb_ready"), 1)
            add_block(2, 7, xb[:, 1, :], xs[:, 2, :])

            def mixture_weights(k, b, n, rev, normalise):
                g = lambda j: gates[:, j, 0:n]
                one = lambda j: small[:, j:j + 1]
                dve.wait_ge(sem("logits_in_psum"), k + 1)
                dve.tensor_reduce(one(12), bank[b][:, 0:n], AX.X, ALU.max, negate=True)\
                    .then_inc(sem("gate_neg_ready"), 1)
                dve.wait_ge(sem("gate_exp_ready"), k + 1)
                after(dve.reciprocal(one(15), one(13)))
                after(dve.tensor_scalar(g(0), small[:, 40:40 + n], one(15), None, ALU.mult))
                for r in range(2):
                    p_, pick, left = (0, 1, 2) if r == 0 else (2, 3, None)
                    after(dve.tensor_reduce(one(16 + 2 * r), g(p_), AX.X, ALU.max))
                    after(dve.scalar_tensor_tensor(g(4), g(p_), one(16 + 2 * r), rev, ALU.is_equal, ALU.mult))
                    after(dve.tensor_reduce(one(17 + 2 * r), g(4), AX.X, ALU.max))
                    after(dve.tensor_scalar(g(pick), g(4), one(17 + 2 * r), None, ALU.is_equal))
                    if r == 0:
                        after(dve.scalar_tensor_tensor(g(left), g(pick), -2.0, g(p_), ALU.mult, ALU.add))
                after(dve.tensor_tensor(g(5), g(1), g(3), ALU.add))
                after(dve.tensor_tensor(g(6), g(5), g(0), ALU.mult))
                if normalise:
                    after(dve.tensor_tensor(one(20), one(16), one(18), ALU.add))
                    after(dve.reciprocal(one(21), one(20)))
                    after(dve.tensor_scalar(g(6), g(6), one(21), None, ALU.mult))

            def mix(n, e, b, res, dst):
                dve.wait_ge(sem("expert_in_psum"), n + 1)
                dve.scalar_tensor_tensor(dst, bank[b][:, 0:D], gates[:, 6, e:e + 1], res, ALU.mult, ALU.add)\
                    .then_inc(sem("expert_mixed"), 1)
                dve.wait_ge(sem("expert_mixed"), n + 1)

            layernorm(2, xs[:, 2, :])
            copy_xhatT(2, 0, 0)
            dve.wait_ge(sem("xhat_ready"), 3)
            stats(3, xhat[:, :])
            after(dve.tensor_scalar(rn[:, :], xhat[:, :], small[:, 6:7], small[:, 11:12], ALU.subtract, ALU.mult))
            after(dve.tensor_tensor(rn[:, :], rn[:, :], bias_rows[:, 2, :], ALU.mult))
            dve.tensor_tensor(rn[:, :], rn[:, :], bias_rows[:, 3, :], ALU.add).then_inc(sem("rn_ready"), 1)
            copy_xhatT(3, 1, 3)
            mixture_weights(0, 0, E0, const("rev0"), False)
            for e in range(E0):
                mix(e, e, 4 + e % 4, xs[:, 2, :] if e == 0 else acc[:, (e - 1) % 2, :],
                    xs[:, 3, :] if e == E0 - 1 else acc[:, e % 2, :])

            dve.memset(vbuf[:, :, TILES * VW:], 0.0).then_inc(sem("vbuf_padded"), 1)
            after(dve.memset(v_ring[0][:, :, :, HD:VW].rearrange("p h t c -> p (h t c)"), 1.0))
            layernorm(4, xs[:, 3, :])
            copy_xhatT(4, 0, 0)
            split_q(1, 1)
            attention(1)
            add_block(3, 6, xs[:, 3, :], xs[:, 4, :])

            layernorm(5, xs[:, 4, :])
            copy_xhatT(5, 1, 0)
            dve.wait_ge(sem("kvu_in_psum"), 1)
            dve.tensor_scalar(kvu[:, 0:D], bank[2][:, 0:D], 0.0, HD ** -0.5, ALU.max, ALU.mult)\
                .then_inc(sem("kv2_ready"), 1)
            dve.tensor_copy(kvu[:, D:2 * D], bank[2][:, D:2 * D]).then_inc(sem("kv2_ready"), 1)
            dve.wait_ge(sem("q2_in_psum"), 1)
            dve.tensor_scalar(q2T, bank[1][:, 0:D].rearrange("p (g n) -> p g n", g=DC), 0.0, HD ** -0.5,
                              ALU.max, ALU.mult).then_inc(sem("q2_ready"), 1)
            dve.wait_ge(sem("kv_outer_in_psum"), 1)
            for g in range(DC):
                dve.tensor_tensor(kvm[:, g, :], bank[4 + g][:, 0:P], blockdiag, ALU.mult).then_inc(sem("kvm_ready"), 1)
            dve.wait_ge(sem("o2_in_psum"), 1)
            raw = acc[:, 2, :]
            after(dve.tensor_copy(raw, bank[7][:, 0:D]))
            after(dve.scalar_tensor_tensor(o2sq, raw, 1.0 / HD, raw, ALU.mult, ALU.mult))
            dve.tensor_reduce(small[:, 40:56], o2sq.rearrange("p (h d) -> p h d", d=HD), AX.X, ALU.add)\
                .then_inc(sem("o2_sumsq_ready"), 1)
            dve.wait_ge(sem("o2_norm_ready"), 1)
            after(dve.tensor_scalar(small[:, 64:80], small[:, 64:80], 1e-12, None, ALU.max))
            after(dve.reciprocal(small[:, 80:96], small[:, 64:80]))
            after(dve.tensor_tensor(o2.rearrange("p (h d) -> p h d", d=HD), raw.rearrange("p (h d) -> p h d", d=HD),
                                    small[:, 80:96].rearrange("p (h a) -> p h a", a=1).broadcast_to([P, HEADS, HD]),
                                    ALU.mult))
            dve.wait_ge(sem("u2_ready"), 1)
            dve.tensor_tensor(o2, o2, kvu[:, 2 * D:3 * D], ALU.mult).then_inc(sem("o2_ready"), 1)
            dve.wait_ge(sem("o2T_in_psum"), 1)
            dve.tensor_copy(o2T.rearrange("p c n -> p (c n)"), bank[0][:, 0:D]).then_inc(sem("o2T_ready"), 1)
            add_block(4, 6, xs[:, 4, :], xs[:, 5, :])

            layernorm(6, xs[:, 5, :])
            copy_xhatT(6, 0, 0)
            mixture_weights(1, 7, E1, const("rev1"), True)

            def gated(r):
                dve.wait_ge(sem("silu_done"), r + 1)
                dve.wait_ge(sem("up_in_psum"), r + 1)
                dve.tensor_tensor(h1T[:, 4 * r:4 * r + 4, :], silu_g[:, r % 2, :].rearrange("p (f n) -> p f n", f=4),
                                  bank[2 + 2 * (r % 2)].rearrange("p (f n) -> p f n", f=4), ALU.mult)\
                    .then_inc(sem("h1_ready"), 1)
            gated(0)
            for r in range(4):
                gated(r + 1)
                for e in range(4 * r, 4 * r + 4):
                    mix(E0 + e, e, (0, 5, 6)[e % 3], xs[:, 5, :] if e == 0 else acc[:, (e - 1) % 2, :],
                        acc[:, e % 2, :])
            dve.wait_ge(sem("shared_in_psum"), 1)
            dve.scalar_tensor_tensor(xs[:, 6, :], bank[7][:, 0:D], small[:, 14:15], acc[:, (E1 - 1) % 2, :],
                                     ALU.mult, ALU.add).then_inc(sem("out_ready"), 1)


def kernel(**inputs):
    import concourse.bacc as bacc
    from concourse.bass_utils import run_bass_kernel_spmd

    v = {k: np.asarray(x) for k, x in inputs.items()}
    hid = lambda w: w.transpose(2, 0, 1).reshape(w.shape[2], -1)
    arrays = {
        "x": v["x"][0], "ctxT": np.concatenate([v["ctx_512"][0], v["ctx_512"][0, :2 * CHUNK]]).T,
        "consts": _constants(),
        "ones": np.full((3, KEYS), 0x3F80, np.uint16),
        "wk": np.concatenate([v["L0_xattn_Wk"], v["L1_xattn_Wkv"][:D].T], 1),
        "wv": np.concatenate([v["L0_xattn_Wv"], v["L1_xattn_Wkv"][D:].T], 1),
        "bq": v["L0_xattn_bq"].reshape(DC, P).T, "bk": v["L0_xattn_bk"].reshape(DC, P).T, "bv": v["L0_xattn_bv"], "bo0": v["L0_xattn_bo"],
        "wq0": v["L0_xattn_Wq"], "wq1": v["L1_xattn_Wq"].T, "wo0": v["L0_xattn_Wo"], "wo1": v["L1_xattn_Wo"].T,
        "lin_w": np.concatenate([v["L0_attn_Wq"], v["L0_attn_Wk"], v["L0_attn_Wv"]], 1),
        "lin_wo": v["L0_attn_Wo"], "lin_bo": v["L0_attn_bo"],
        "gamma": v["L0_ffn_ln_gamma"], "beta": v["L0_ffn_ln_beta"], "gate0": v["L0_ffn_gate_w"].T,
        "w1": hid(v["L0_ffn_w1"]), "w2": v["L0_ffn_w2"].transpose(0, 2, 1).reshape(E0 * F0, D),
        "w_q2": v["L1_attn_Wq"].T, "w_o2": v["L1_attn_Wo"].T,
        "w_kvu": np.concatenate([v["L1_attn_Wk"].T, v["L1_attn_Wv"].T, v["L1_attn_Wu"].T], 1),
        "gate1": np.concatenate([v["L1_ffn_Wg"].T, v["L1_ffn_Wsg"].T], 1),
        "we_in": np.stack([np.concatenate([hid(v["L1_ffn_We_gate"]), v["L1_ffn_Ws_gate"].T], 1),
                           np.concatenate([hid(v["L1_ffn_We_up"]), v["L1_ffn_Ws_up"].T], 1)], 1),
        "we_out": np.concatenate([v["L1_ffn_We_down"].transpose(0, 2, 1).reshape(E1 * F1, D),
                                  v["L1_ffn_Ws_down"].T], 0),
    }
    nc = bacc.Bacc("TRN2", target_bir_lowering=False, num_devices=1)
    feed, aps = {}, {}
    for name, x in arrays.items():
        x = np.ascontiguousarray(x)
        feed[f"in_{name}"] = x
        dt = BF16 if name == "ones" else mybir.dt.from_np(x.dtype)
        t = nc.dram_tensor(f"in_{name}", x.shape, mybir.dt.from_np(x.dtype), kind="ExternalInput").ap()
        aps[name] = t.bitcast(BF16) if name == "ones" else t
    out = nc.dram_tensor("out", (P, D), F32, kind="ExternalOutput").ap()
    program(nc, aps, out)
    r = run_bass_kernel_spmd(nc, [feed], core_ids=[0])
    return r.results[0]["out"].reshape(1, P, D)
```
